# Optimizing a Trainium2 kernel written in Bass

```python
import numpy as np
import jax
import jax.numpy as jnp

def _softmax(x, axis=-1):
    return jax.nn.softmax(x, axis=axis)

def _gelu(x):
    return jax.nn.gelu(x, approximate=True)

def _silu(x):
    return jax.nn.silu(x)

def _sigmoid(x):
    return jax.nn.sigmoid(x)

def _layernorm(x, axis=-1, eps=1e-05):
    m = jnp.mean(x, axis=axis, keepdims=True)
    v = jnp.var(x, axis=axis, keepdims=True)
    return (x - m) / jnp.sqrt(v + eps)

def _scatter_add(tgt, idx, src, axis=0):
    return tgt.at[idx].add(src)

def _segment_sum(src, seg, n):
    return jax.ops.segment_sum(src, seg, n)
kernel_name = 'mk_xattn_seq_d4_seqx_r8_da5dc4'

def setup_inputs(seed: int=0):
    np.random.seed(seed)
    _w = jnp.asarray

    def _rec_inputs():
        import jax
        import jax.numpy as jnp
        _rk = jax.random.key(seed)
        x = 7.22e-05 + 1 * jax.random.normal(jax.random.fold_in(_rk, 1), (4, 256, 256), jnp.float32)
        _lenS = 256 - jax.random.randint(jax.random.fold_in(_rk, 7), (4,), 0, max(1, 256 // 4) + 1, jnp.int32)
        _lenS2 = 256 - jax.random.randint(jax.random.fold_in(_rk, 8), (4,), 0, max(1, 256 // 4) + 1, jnp.int32)
        _ctx_2048P = jax.random.normal(jax.random.fold_in(_rk, 11), (4, 16, 256), jnp.float32)
        _ctx_2048c = jax.random.dirichlet(jax.random.fold_in(_rk, 511), 0.3 * jnp.ones((16,), jnp.float32), (4, 256))
        _ctx_2048t = jnp.einsum('bsk,bkd->bsd', _ctx_2048c, _ctx_2048P)
        _ctx_2048t = _ctx_2048t * jax.lax.rsqrt(jnp.mean(jnp.square(_ctx_2048t)) + 1e-12) * 0.953939
        ctx_2048 = 4.13588e-05 + 0.999923 * (_ctx_2048t + 0.3 * jax.random.normal(jax.random.fold_in(_rk, 611), (4, 256, 256), jnp.float32))
        _validS = jnp.arange(256)[None, :] < _lenS[:, None]
        _validS2 = jnp.arange(256)[None, :] < _lenS2[:, None]
        _causal = jnp.tril(jnp.ones((256, 256), dtype=bool))
        mask_Bx1xSxS2_ff0 = jnp.where(jnp.ones((4, 1, 256, 256), dtype=bool), 0.0, -1000000000.0).astype(jnp.float32)
        mask_BxS2_ik0 = jnp.where(jnp.broadcast_to(_validS2[:, :], (4, 256)), 0, 1).astype(jnp.int32)
        return (x, ctx_2048, mask_Bx1xSxS2_ff0, mask_BxS2_ik0)
    x, ctx_2048, mask_Bx1xSxS2_ff0, mask_BxS2_ik0 = _rec_inputs()

    def _L0_xattn_setup():
        import jax, jax.numpy as jnp
        import numpy as np
        H = 256
        NH = 32
        KVH = 8
        HD = H // NH
        GROUPS = NH // KVH
        EPS = 1e-06
        B, L, S = (4, 128, 128)

        def _gqa_forward(hidden_state, encoder_hidden_state, encoder_attention_mask, Wq, bq, Wk, bk, Wv, bv, Wo, bo, gamma, beta):
            b, l, _ = hidden_state.shape
            s = encoder_hidden_state.shape[1]
            q = hidden_state @ Wq + bq
            k = encoder_hidden_state @ Wk + bk
            v = encoder_hidden_state @ Wv + bv
            q = q.reshape(b, l, KVH, GROUPS, HD).transpose(0, 2, 3, 1, 4)
            k = k.reshape(b, s, KVH, HD).transpose(0, 2, 1, 3)
            v = v.reshape(b, s, KVH, HD).transpose(0, 2, 1, 3)
            scale = 1.0 / jnp.sqrt(jnp.asarray(HD, q.dtype))
            scores = jnp.einsum('bkgld,bksd->bkgls', q, k) * scale
            scores = scores + encoder_attention_mask[:, :, None, :, :]
            attn = jax.nn.softmax(scores, axis=-1)
            out = jnp.einsum('bkgls,bksd->bkgld', attn, v)
            out = out.transpose(0, 3, 1, 2, 4).reshape(b, l, H)
            out = out @ Wo + bo
            x = out + hidden_state
            mu = jnp.mean(x, axis=-1, keepdims=True)
            var = jnp.var(x, axis=-1, keepdims=True)
            return (x - mu) * jax.lax.rsqrt(var + EPS) * gamma + beta
        key = jax.random.key(seed)
        ks = jax.random.split(key, 12)
        sd = 0.02
        return {'hidden_state': jax.random.normal(ks[0], (B, L, H), jnp.float32), 'encoder_hidden_state': jax.random.normal(ks[1], (B, S, H), jnp.float32), 'encoder_attention_mask': jnp.zeros((B, 1, L, S), jnp.float32), 'Wq': jax.random.normal(ks[2], (H, H), jnp.float32) * sd, 'bq': jnp.zeros((H,), jnp.float32), 'Wk': jax.random.normal(ks[3], (H, KVH * HD), jnp.float32) * sd, 'bk': jnp.zeros((KVH * HD,), jnp.float32), 'Wv': jax.random.normal(ks[4], (H, KVH * HD), jnp.float32) * sd, 'bv': jnp.zeros((KVH * HD,), jnp.float32), 'Wo': jax.random.normal(ks[5], (H, H), jnp.float32) * sd, 'bo': jnp.zeros((H,), jnp.float32), 'gamma': jnp.ones((H,), jnp.float32), 'beta': jnp.zeros((H,), jnp.float32)}
    _L0_xattn_all = _L0_xattn_setup()
    _L0_xattn_in = {k: v for k, v in _L0_xattn_all.items() if k in ('Wq', 'bq', 'Wk', 'bk', 'Wv', 'bv', 'Wo', 'bo', 'gamma', 'beta')}
    del _L0_xattn_all

    def _L1_xattn_setup():
        import jax, jax.numpy as jnp
        import numpy as np
        B, Q, S1, S2 = (4, 32, 256, 256)
        D, H, K, F = (256, 16, 128, 1024)
        LN_EPS = 1e-05

        def _layer_norm(x, scale, offset):
            mu = jnp.mean(x, axis=-1, keepdims=True)
            var = jnp.var(x, axis=-1, keepdims=True)
            return (x - mu) * jax.lax.rsqrt(var + LN_EPS) * scale + offset

        def _cross_attention(q_in, kv_in, wq, bq, wk, bk, wv, bv, wo, bo, bias_k, bias_v):
            b, q_len, _ = q_in.shape
            t = kv_in.shape[1]
            qh = (q_in @ wq + bq).reshape(b, q_len, H, K)
            kh = (kv_in @ wk + bk).reshape(b, t, H, K)
            vh = (kv_in @ wv + bv).reshape(b, t, H, K)
            kh = jnp.concatenate([kh, jnp.broadcast_to(bias_k, (b, 1, H, K))], axis=1)
            vh = jnp.concatenate([vh, jnp.broadcast_to(bias_v, (b, 1, H, K))], axis=1)
            scale = jnp.sqrt(jnp.asarray(K, q_in.dtype))
            logits = jnp.einsum('bqhk,bthk->bhqt', qh, kh) / scale
            weights = jax.nn.softmax(logits, axis=-1)
            ctx = jnp.einsum('bhqt,bthk->bqhk', weights, vh).reshape(b, q_len, H * K)
            return ctx @ wo + bo

        def _forward(x, xf_1, xf_2, ln1_scale, ln1_offset, wq1, bq1, wk1, bk1, wv1, bv1, wo1, bo1, bias_k1, bias_v1, ln2_scale, ln2_offset, wq2, bq2, wk2, bk2, wv2, bv2, wo2, bo2, bias_k2, bias_v2, ln_mlp_scale, ln_mlp_offset, w_fc1, b_fc1, w_fc2, b_fc2):
            res = x
            h = _layer_norm(x, ln1_scale, ln1_offset)
            x = res + _cross_attention(h, xf_1, wq1, bq1, wk1, bk1, wv1, bv1, wo1, bo1, bias_k1, bias_v1)
            res = x
            h = _layer_norm(x, ln2_scale, ln2_offset)
            x = res + _cross_attention(h, xf_2, wq2, bq2, wk2, bk2, wv2, bv2, wo2, bo2, bias_k2, bias_v2)
            h = _layer_norm(x, ln_mlp_scale, ln_mlp_offset)
            h = jax.nn.gelu(h @ w_fc1 + b_fc1, approximate=False) @ w_fc2 + b_fc2
            return x + h
        key = jax.random.key(seed)
        ks = iter(jax.random.split(key, 64))

        def rn(shape, s=0.02):
            return jax.random.normal(next(ks), shape, jnp.float32) * s
        inp = {'x': rn((B, Q, D), 1.0), 'xf_1': rn((B, S1, D), 1.0), 'xf_2': rn((B, S2, D), 1.0)}
        for i in (1, 2):
            inp[f'ln{i}_scale'] = jnp.ones((D,), jnp.float32)
            inp[f'ln{i}_offset'] = jnp.zeros((D,), jnp.float32)
            inp[f'wq{i}'] = rn((D, H * K))
            inp[f'bq{i}'] = jnp.zeros((H * K,), jnp.float32)
            inp[f'wk{i}'] = rn((D, H * K))
            inp[f'bk{i}'] = jnp.zeros((H * K,), jnp.float32)
            inp[f'wv{i}'] = rn((D, H * K))
            inp[f'bv{i}'] = jnp.zeros((H * K,), jnp.float32)
            inp[f'wo{i}'] = rn((H * K, D))
            inp[f'bo{i}'] = jnp.zeros((D,), jnp.float32)
            inp[f'bias_k{i}'] = rn((1, 1, H, K))
            inp[f'bias_v{i}'] = rn((1, 1, H, K))
        inp['ln_mlp_scale'] = jnp.ones((D,), jnp.float32)
        inp['ln_mlp_offset'] = jnp.zeros((D,), jnp.float32)
        inp['w_fc1'] = rn((D, F))
        inp['b_fc1'] = jnp.zeros((F,), jnp.float32)
        inp['w_fc2'] = rn((F, D))
        inp['b_fc2'] = jnp.zeros((D,), jnp.float32)
        return inp
    _L1_xattn_all = _L1_xattn_setup()
    _L1_xattn_in = {k: v for k, v in _L1_xattn_all.items() if k in ('ln1_scale', 'ln1_offset', 'wq1', 'bq1', 'wk1', 'bk1', 'wv1', 'bv1', 'wo1', 'bo1', 'bias_k1', 'bias_v1', 'ln2_scale', 'ln2_offset', 'wq2', 'bq2', 'wk2', 'bk2', 'wv2', 'bv2', 'wo2', 'bo2', 'bias_k2', 'bias_v2', 'ln_mlp_scale', 'ln_mlp_offset', 'w_fc1', 'b_fc1', 'w_fc2', 'b_fc2')}
    del _L1_xattn_all

    def _L2_xattn_setup():
        import jax, jax.numpy as jnp
        import numpy as np
        H = 256
        B, L, S = (4, 512, 10)
        key = jax.random.key(seed)
        k1, k2, k3, k4, k5, k6 = jax.random.split(key, 6)
        scale = 1.0 / np.sqrt(H)
        return {'h_english': jax.random.normal(k1, (B, L, H), dtype=jnp.float32), 'h_lojban': jax.random.normal(k2, (B, S, H), dtype=jnp.float32), 'w_q': jax.random.normal(k3, (H, H), dtype=jnp.float32) * scale, 'w_k': jax.random.normal(k4, (H, H), dtype=jnp.float32) * scale, 'w_v': jax.random.normal(k5, (H, H), dtype=jnp.float32) * scale, 'w_o': jax.random.normal(k6, (H, H), dtype=jnp.float32) * scale, 'alpha': jnp.float32(0.1)}
    _L2_xattn_all = _L2_xattn_setup()
    _L2_xattn_in = {k: v for k, v in _L2_xattn_all.items() if k in ('w_q', 'w_k', 'w_v', 'w_o', 'alpha')}
    del _L2_xattn_all

    def _L3_xattn_setup():
        import jax, jax.numpy as jnp
        import numpy as np
        B, P, K, H, NH = (4, 256, 32, 256, 16)
        DH = H // NH
        EPS = 1e-06

        def rmsnorm(x, w):
            var = jnp.mean(jnp.square(x), axis=-1, keepdims=True)
            return x * jax.lax.rsqrt(var + EPS) * w
        key = jax.random.key(seed)
        ks = jax.random.split(key, 12)
        s = 0.02
        return {'x': jax.random.normal(ks[0], (B, P, H), jnp.float32), 'latents': jax.random.normal(ks[1], (B, K, H), jnp.float32), 'attention_mask': jax.random.randint(ks[2], (B, P), 0, 2, jnp.int32), 'q_w': s * jax.random.normal(ks[3], (H, H), jnp.float32), 'q_b': jnp.zeros((H,), jnp.float32), 'kv_w': s * jax.random.normal(ks[4], (H, 2 * H), jnp.float32), 'kv_b': jnp.zeros((2 * H,), jnp.float32), 'out_w': s * jax.random.normal(ks[5], (H, H), jnp.float32), 'out_b': jnp.zeros((H,), jnp.float32), 'postnorm_w': jnp.ones((H,), jnp.float32), 'mlp_w1': s * jax.random.normal(ks[6], (H, 4 * H), jnp.float32), 'mlp_b1': jnp.zeros((4 * H,), jnp.float32), 'mlp_w2': s * jax.random.normal(ks[7], (4 * H, H), jnp.float32), 'mlp_b2': jnp.zeros((H,), jnp.float32)}
    _L3_xattn_all = _L3_xattn_setup()
    _L3_xattn_in = {k: v for k, v in _L3_xattn_all.items() if k in ('q_w', 'q_b', 'kv_w', 'kv_b', 'out_w', 'out_b', 'postnorm_w', 'mlp_w1', 'mlp_b1', 'mlp_w2', 'mlp_b2')}
    del _L3_xattn_all
    return {'x': x, 'ctx_2048': ctx_2048, 'mask_Bx1xSxS2_ff0': mask_Bx1xSxS2_ff0, 'mask_BxS2_ik0': mask_BxS2_ik0, 'L0_xattn_Wq': _L0_xattn_in['Wq'], 'L0_xattn_bq': _L0_xattn_in['bq'], 'L0_xattn_Wk': _L0_xattn_in['Wk'], 'L0_xattn_bk': _L0_xattn_in['bk'], 'L0_xattn_Wv': _L0_xattn_in['Wv'], 'L0_xattn_bv': _L0_xattn_in['bv'], 'L0_xattn_Wo': _L0_xattn_in['Wo'], 'L0_xattn_bo': _L0_xattn_in['bo'], 'L0_xattn_gamma': _L0_xattn_in['gamma'], 'L0_xattn_beta': _L0_xattn_in['beta'], 'L1_xattn_ln1_scale': _L1_xattn_in['ln1_scale'], 'L1_xattn_ln1_offset': _L1_xattn_in['ln1_offset'], 'L1_xattn_wq1': _L1_xattn_in['wq1'], 'L1_xattn_bq1': _L1_xattn_in['bq1'], 'L1_xattn_wk1': _L1_xattn_in['wk1'], 'L1_xattn_bk1': _L1_xattn_in['bk1'], 'L1_xattn_wv1': _L1_xattn_in['wv1'], 'L1_xattn_bv1': _L1_xattn_in['bv1'], 'L1_xattn_wo1': _L1_xattn_in['wo1'], 'L1_xattn_bo1': _L1_xattn_in['bo1'], 'L1_xattn_bias_k1': _L1_xattn_in['bias_k1'], 'L1_xattn_bias_v1': _L1_xattn_in['bias_v1'], 'L1_xattn_ln2_scale': _L1_xattn_in['ln2_scale'], 'L1_xattn_ln2_offset': _L1_xattn_in['ln2_offset'], 'L1_xattn_wq2': _L1_xattn_in['wq2'], 'L1_xattn_bq2': _L1_xattn_in['bq2'], 'L1_xattn_wk2': _L1_xattn_in['wk2'], 'L1_xattn_bk2': _L1_xattn_in['bk2'], 'L1_xattn_wv2': _L1_xattn_in['wv2'], 'L1_xattn_bv2': _L1_xattn_in['bv2'], 'L1_xattn_wo2': _L1_xattn_in['wo2'], 'L1_xattn_bo2': _L1_xattn_in['bo2'], 'L1_xattn_bias_k2': _L1_xattn_in['bias_k2'], 'L1_xattn_bias_v2': _L1_xattn_in['bias_v2'], 'L1_xattn_ln_mlp_scale': _L1_xattn_in['ln_mlp_scale'], 'L1_xattn_ln_mlp_offset': _L1_xattn_in['ln_mlp_offset'], 'L1_xattn_w_fc1': _L1_xattn_in['w_fc1'], 'L1_xattn_b_fc1': _L1_xattn_in['b_fc1'], 'L1_xattn_w_fc2': _L1_xattn_in['w_fc2'], 'L1_xattn_b_fc2': _L1_xattn_in['b_fc2'], 'L2_xattn_w_q': _L2_xattn_in['w_q'], 'L2_xattn_w_k': _L2_xattn_in['w_k'], 'L2_xattn_w_v': _L2_xattn_in['w_v'], 'L2_xattn_w_o': _L2_xattn_in['w_o'], 'L2_xattn_alpha': _L2_xattn_in['alpha'], 'L3_xattn_q_w': _L3_xattn_in['q_w'], 'L3_xattn_q_b': _L3_xattn_in['q_b'], 'L3_xattn_kv_w': _L3_xattn_in['kv_w'], 'L3_xattn_kv_b': _L3_xattn_in['kv_b'], 'L3_xattn_out_w': _L3_xattn_in['out_w'], 'L3_xattn_out_b': _L3_xattn_in['out_b'], 'L3_xattn_postnorm_w': _L3_xattn_in['postnorm_w'], 'L3_xattn_mlp_w1': _L3_xattn_in['mlp_w1'], 'L3_xattn_mlp_b1': _L3_xattn_in['mlp_b1'], 'L3_xattn_mlp_w2': _L3_xattn_in['mlp_w2'], 'L3_xattn_mlp_b2': _L3_xattn_in['mlp_b2']}

def reference(x, ctx_2048, mask_Bx1xSxS2_ff0, mask_BxS2_ik0, L0_xattn_Wq, L0_xattn_bq, L0_xattn_Wk, L0_xattn_bk, L0_xattn_Wv, L0_xattn_bv, L0_xattn_Wo, L0_xattn_bo, L0_xattn_gamma, L0_xattn_beta, L1_xattn_ln1_scale, L1_xattn_ln1_offset, L1_xattn_wq1, L1_xattn_bq1, L1_xattn_wk1, L1_xattn_bk1, L1_xattn_wv1, L1_xattn_bv1, L1_xattn_wo1, L1_xattn_bo1, L1_xattn_bias_k1, L1_xattn_bias_v1, L1_xattn_ln2_scale, L1_xattn_ln2_offset, L1_xattn_wq2, L1_xattn_bq2, L1_xattn_wk2, L1_xattn_bk2, L1_xattn_wv2, L1_xattn_bv2, L1_xattn_wo2, L1_xattn_bo2, L1_xattn_bias_k2, L1_xattn_bias_v2, L1_xattn_ln_mlp_scale, L1_xattn_ln_mlp_offset, L1_xattn_w_fc1, L1_xattn_b_fc1, L1_xattn_w_fc2, L1_xattn_b_fc2, L2_xattn_w_q, L2_xattn_w_k, L2_xattn_w_v, L2_xattn_w_o, L2_xattn_alpha, L3_xattn_q_w, L3_xattn_q_b, L3_xattn_kv_w, L3_xattn_kv_b, L3_xattn_out_w, L3_xattn_out_b, L3_xattn_postnorm_w, L3_xattn_mlp_w1, L3_xattn_mlp_b1, L3_xattn_mlp_w2, L3_xattn_mlp_b2):
    import jax
    import jax.numpy as jnp

    def _L0_xattn_ref(hidden_state, encoder_hidden_state, encoder_attention_mask, Wq, bq, Wk, bk, Wv, bv, Wo, bo, gamma, beta):
        import jax, jax.numpy as jnp
        import numpy as np
        H = 256
        NH = 32
        KVH = 8
        HD = H // NH
        GROUPS = NH // KVH
        EPS = 1e-06
        B, L, S = (4, 128, 128)

        def _gqa_forward(hidden_state, encoder_hidden_state, encoder_attention_mask, Wq, bq, Wk, bk, Wv, bv, Wo, bo, gamma, beta):
            b, l, _ = hidden_state.shape
            s = encoder_hidden_state.shape[1]
            q = hidden_state @ Wq + bq
            k = encoder_hidden_state @ Wk + bk
            v = encoder_hidden_state @ Wv + bv
            q = q.reshape(b, l, KVH, GROUPS, HD).transpose(0, 2, 3, 1, 4)
            k = k.reshape(b, s, KVH, HD).transpose(0, 2, 1, 3)
            v = v.reshape(b, s, KVH, HD).transpose(0, 2, 1, 3)
            scale = 1.0 / jnp.sqrt(jnp.asarray(HD, q.dtype))
            scores = jnp.einsum('bkgld,bksd->bkgls', q, k) * scale
            scores = scores + encoder_attention_mask[:, :, None, :, :]
            attn = jax.nn.softmax(scores, axis=-1)
            out = jnp.einsum('bkgls,bksd->bkgld', attn, v)
            out = out.transpose(0, 3, 1, 2, 4).reshape(b, l, H)
            out = out @ Wo + bo
            x = out + hidden_state
            mu = jnp.mean(x, axis=-1, keepdims=True)
            var = jnp.var(x, axis=-1, keepdims=True)
            return (x - mu) * jax.lax.rsqrt(var + EPS) * gamma + beta
        return _gqa_forward(hidden_state, encoder_hidden_state, encoder_attention_mask, Wq, bq, Wk, bk, Wv, bv, Wo, bo, gamma, beta)

    def _L1_xattn_ref(x, xf_1, xf_2, ln1_scale, ln1_offset, wq1, bq1, wk1, bk1, wv1, bv1, wo1, bo1, bias_k1, bias_v1, ln2_scale, ln2_offset, wq2, bq2, wk2, bk2, wv2, bv2, wo2, bo2, bias_k2, bias_v2, ln_mlp_scale, ln_mlp_offset, w_fc1, b_fc1, w_fc2, b_fc2):
        import jax, jax.numpy as jnp
        import numpy as np
        B, Q, S1, S2 = (4, 32, 256, 256)
        D, H, K, F = (256, 16, 128, 1024)
        LN_EPS = 1e-05

        def _layer_norm(x, scale, offset):
            mu = jnp.mean(x, axis=-1, keepdims=True)
            var = jnp.var(x, axis=-1, keepdims=True)
            return (x - mu) * jax.lax.rsqrt(var + LN_EPS) * scale + offset

        def _cross_attention(q_in, kv_in, wq, bq, wk, bk, wv, bv, wo, bo, bias_k, bias_v):
            b, q_len, _ = q_in.shape
            t = kv_in.shape[1]
            qh = (q_in @ wq + bq).reshape(b, q_len, H, K)
            kh = (kv_in @ wk + bk).reshape(b, t, H, K)
            vh = (kv_in @ wv + bv).reshape(b, t, H, K)
            kh = jnp.concatenate([kh, jnp.broadcast_to(bias_k, (b, 1, H, K))], axis=1)
            vh = jnp.concatenate([vh, jnp.broadcast_to(bias_v, (b, 1, H, K))], axis=1)
            scale = jnp.sqrt(jnp.asarray(K, q_in.dtype))
            logits = jnp.einsum('bqhk,bthk->bhqt', qh, kh) / scale
            weights = jax.nn.softmax(logits, axis=-1)
            ctx = jnp.einsum('bhqt,bthk->bqhk', weights, vh).reshape(b, q_len, H * K)
            return ctx @ wo + bo

        def _forward(x, xf_1, xf_2, ln1_scale, ln1_offset, wq1, bq1, wk1, bk1, wv1, bv1, wo1, bo1, bias_k1, bias_v1, ln2_scale, ln2_offset, wq2, bq2, wk2, bk2, wv2, bv2, wo2, bo2, bias_k2, bias_v2, ln_mlp_scale, ln_mlp_offset, w_fc1, b_fc1, w_fc2, b_fc2):
            res = x
            h = _layer_norm(x, ln1_scale, ln1_offset)
            x = res + _cross_attention(h, xf_1, wq1, bq1, wk1, bk1, wv1, bv1, wo1, bo1, bias_k1, bias_v1)
            res = x
            h = _layer_norm(x, ln2_scale, ln2_offset)
            x = res + _cross_attention(h, xf_2, wq2, bq2, wk2, bk2, wv2, bv2, wo2, bo2, bias_k2, bias_v2)
            h = _layer_norm(x, ln_mlp_scale, ln_mlp_offset)
            h = jax.nn.gelu(h @ w_fc1 + b_fc1, approximate=False) @ w_fc2 + b_fc2
            return x + h
        return _forward(x, xf_1, xf_2, ln1_scale, ln1_offset, wq1, bq1, wk1, bk1, wv1, bv1, wo1, bo1, bias_k1, bias_v1, ln2_scale, ln2_offset, wq2, bq2, wk2, bk2, wv2, bv2, wo2, bo2, bias_k2, bias_v2, ln_mlp_scale, ln_mlp_offset, w_fc1, b_fc1, w_fc2, b_fc2)

    def _L2_xattn_ref(h_english, h_lojban, w_q, w_k, w_v, w_o, alpha):
        import jax, jax.numpy as jnp
        import numpy as np
        H = 256
        B, L, S = (4, 512, 10)
        h = h_english.shape[-1]
        q = jnp.einsum('blh,oh->blo', h_english, w_q)
        k = jnp.einsum('bsh,oh->bso', h_lojban, w_k)
        v = jnp.einsum('bsh,oh->bso', h_lojban, w_v)
        scores = jnp.einsum('blh,bsh->bls', q, k) / jnp.sqrt(jnp.float32(h))
        probs = jax.nn.softmax(scores, axis=-1)
        context = jnp.einsum('bls,bsh->blh', probs, v)
        delta = jnp.einsum('blh,oh->blo', context, w_o)
        return h_english + alpha * delta

    def _L3_xattn_ref(x, latents, attention_mask, q_w, q_b, kv_w, kv_b, out_w, out_b, postnorm_w, mlp_w1, mlp_b1, mlp_w2, mlp_b2):
        import jax, jax.numpy as jnp
        import numpy as np
        B, P, K, H, NH = (4, 256, 32, 256, 16)
        DH = H // NH
        EPS = 1e-06

        def rmsnorm(x, w):
            var = jnp.mean(jnp.square(x), axis=-1, keepdims=True)
            return x * jax.lax.rsqrt(var + EPS) * w
        b, p, _ = x.shape
        k_len = latents.shape[1]
        residual = latents
        h = jnp.concatenate([x, latents], axis=1)
        q = (latents @ q_w + q_b).reshape(b, k_len, NH, DH)
        kv = (h @ kv_w + kv_b).reshape(b, p + k_len, NH, DH, 2)
        kmat, v = (kv[..., 0], kv[..., 1])
        attn = jnp.einsum('bkhd,bnhd->bhkn', q, kmat) / DH
        full_mask = jnp.concatenate([attention_mask.astype(bool), jnp.ones((b, k_len), bool)], axis=-1)
        attn = jnp.where(full_mask[:, None, None, :], attn, -jnp.inf)
        attn = jax.nn.softmax(attn.astype(jnp.float32), axis=-1).astype(q.dtype)
        attn_out = jnp.einsum('bhkn,bnhd->bkhd', attn, v).reshape(b, k_len, H)
        attn_out = attn_out @ out_w + out_b + residual
        out = rmsnorm(attn_out, postnorm_w)
        out = jax.nn.gelu(out @ mlp_w1 + mlp_b1) @ mlp_w2 + mlp_b2
        return out + residual
    x = _L0_xattn_ref(x, ctx_2048, mask_Bx1xSxS2_ff0, L0_xattn_Wq, L0_xattn_bq, L0_xattn_Wk, L0_xattn_bk, L0_xattn_Wv, L0_xattn_bv, L0_xattn_Wo, L0_xattn_bo, L0_xattn_gamma, L0_xattn_beta)
    x = _L1_xattn_ref(x, ctx_2048, ctx_2048, L1_xattn_ln1_scale, L1_xattn_ln1_offset, L1_xattn_wq1, L1_xattn_bq1, L1_xattn_wk1, L1_xattn_bk1, L1_xattn_wv1, L1_xattn_bv1, L1_xattn_wo1, L1_xattn_bo1, L1_xattn_bias_k1, L1_xattn_bias_v1, L1_xattn_ln2_scale, L1_xattn_ln2_offset, L1_xattn_wq2, L1_xattn_bq2, L1_xattn_wk2, L1_xattn_bk2, L1_xattn_wv2, L1_xattn_bv2, L1_xattn_wo2, L1_xattn_bo2, L1_xattn_bias_k2, L1_xattn_bias_v2, L1_xattn_ln_mlp_scale, L1_xattn_ln_mlp_offset, L1_xattn_w_fc1, L1_xattn_b_fc1, L1_xattn_w_fc2, L1_xattn_b_fc2)
    x = _L2_xattn_ref(x, ctx_2048, L2_xattn_w_q, L2_xattn_w_k, L2_xattn_w_v, L2_xattn_w_o, L2_xattn_alpha)
    x = _L3_xattn_ref(ctx_2048, x, mask_BxS2_ik0, L3_xattn_q_w, L3_xattn_q_b, L3_xattn_kv_w, L3_xattn_kv_b, L3_xattn_out_w, L3_xattn_out_b, L3_xattn_postnorm_w, L3_xattn_mlp_w1, L3_xattn_mlp_b1, L3_xattn_mlp_w2, L3_xattn_mlp_b2)
    return x

_drawn_inputs = setup_inputs


def setup_inputs(seed=0):
    import zlib

    import numpy as np

    out = dict(_drawn_inputs(seed))
    spreads = {'L0_xattn_bq': (0.0, 0.8),
     'L0_xattn_bk': (0.0, 2.0),
     'L0_xattn_bv': (0.0, 0.1),
     'L0_xattn_bo': (0.0, 0.1),
     'L0_xattn_gamma': (1.0, 0.2),
     'L0_xattn_beta': (0.0, 0.1),
     'L1_xattn_ln1_scale': (1.0, 0.6),
     'L1_xattn_ln1_offset': (0.0, 0.8),
     'L1_xattn_bq1': (0.0, 0.8),
     'L1_xattn_bk1': (0.0, 2.0),
     'L1_xattn_bv1': (0.0, 0.1),
     'L1_xattn_bo1': (0.0, 0.1),
     'L1_xattn_ln2_scale': (1.0, 0.6),
     'L1_xattn_ln2_offset': (0.0, 0.8),
     'L1_xattn_bq2': (0.0, 0.8),
     'L1_xattn_bk2': (0.0, 2.0),
     'L1_xattn_bv2': (0.0, 0.1),
     'L1_xattn_bo2': (0.0, 0.1),
     'L1_xattn_ln_mlp_scale': (1.0, 0.6),
     'L1_xattn_ln_mlp_offset': (0.0, 0.707),
     'L1_xattn_b_fc1': (0.0, 0.1),
     'L1_xattn_b_fc2': (0.0, 0.1),
     'L3_xattn_q_b': (0.0, 2.0),
     'L3_xattn_kv_b': (0.0, 0.8),
     'L3_xattn_out_b': (0.0, 2.0),
     'L3_xattn_postnorm_w': (1.0, 0.6),
     'L3_xattn_mlp_b1': (0.0, 0.1),
     'L3_xattn_mlp_b2': (0.0, 0.1)}
    factors = {'L0_xattn_Wq': 8.0,
     'L0_xattn_Wk': 8.0,
     'L1_xattn_wq1': 8.0,
     'L1_xattn_wk1': 8.0,
     'L1_xattn_bias_k1': 64.0,
     'L1_xattn_bias_v1': 64.0,
     'L1_xattn_wq2': 8.0,
     'L1_xattn_wk2': 8.0,
     'L1_xattn_bias_k2': 64.0,
     'L1_xattn_bias_v2': 64.0,
     'L2_xattn_w_q': 2.705,
     'L2_xattn_w_k': 2.852,
     'L3_xattn_q_w': 8.0,
     'L3_xattn_kv_w': 8.0,
     'L3_xattn_out_w': 8.0}
    for name, (base, spread) in spreads.items():
        noise = np.random.default_rng([zlib.crc32(name.encode()), seed]).standard_normal(out[name].shape)
        drawn = base * np.exp(spread * noise) if base else spread * noise
        out[name] = jnp.asarray(drawn.astype(out[name].dtype))
    for name, factor in factors.items():
        out[name] = (out[name] * factor).astype(out[name].dtype)
    return out
```

```python
from contextlib import ExitStack

import concourse.bass as bass
from concourse import mybir

F32 = mybir.dt.float32
F32R = mybir.dt.float32r
I32 = mybir.dt.int32
ACT = mybir.ActivationFunctionType
ALU = mybir.AluOpType
AXX = mybir.AxisListType.X

P = 128
B = 4
S = 256
TOK = B * S
NT = TOK // P
D = 256
KC = D // P
BANK = 512
FAR = -1e30


class Core:

    def __init__(self, nc, outer):
        self.nc, self.outer, self.stack, self.n = nc, outer, [outer], 0

    def sb(self, name, shape, dt=F32):
        return self.stack[-1].enter_context(self.nc.sbuf_tensor(name, shape, dt))

    def ps(self, name, shape, dt=F32):
        return self.stack[-1].enter_context(self.nc.psum_tensor(name, shape, dt))

    def sem(self, name):
        return self.outer.enter_context(self.nc.semaphore(name))

    def push(self):
        self.stack.append(ExitStack())

    def pop(self):
        self.stack.pop().close()


def norm_transpose(k, name, X, hT, xn, ident, eps, scale=None, offset=None, rms=False, after_ready=None):
    nc = k.nc
    k.push()
    ps = k.ps(f"{name}_ps", [P, 4, BANK])
    stats = k.sb(f"{name}_stats", [P, NT, 6])
    mv = k.sb(f"{name}_mv", [P, NT, 2])
    ms = k.sb(f"{name}_ms", [P, NT])
    ve = k.sb(f"{name}_ve", [P, NT])
    sd = k.sb(f"{name}_sd", [P, NT])
    rstd = k.sb(f"{name}_rstd", [P, NT])
    small = k.sem(f"{name}_small")
    var_ready = k.sem(f"{name}_var_ready")
    sd_ready = k.sem(f"{name}_sd_ready")
    tile_normed = k.sem(f"{name}_tile_normed")
    transposed = k.sem(f"{name}_transposed")
    hT_act = k.sem(f"{name}_hT_act")
    with nc.Block() as block:
        @block.vector
        def _(dve):
            done = [0]

            def link(ins):
                done[0] += 1
                ins.then_inc(small, 1)
                dve.wait_ge(small, done[0])

            for t in range(NT):
                ins = nc.vector.bn_stats(stats[:, t, :], X[:, t, :])
            link(ins)
            for t in range(NT):
                ins = nc.vector.bn_aggr(mv[:, t, :], stats[:, t, :])
            link(ins)
            if rms:
                link(nc.vector.tensor_tensor(ms[:, :], mv[:, :, 0], mv[:, :, 0], ALU.mult))
                link(nc.vector.tensor_tensor(ve[:, :], ms[:, :], mv[:, :, 1], ALU.add))
                nc.vector.tensor_scalar(ms[:, :], ve[:, :], eps, None, ALU.add).then_inc(var_ready, 1)
            else:
                nc.vector.tensor_scalar(ms[:, :], mv[:, :, 1], eps, None, ALU.add).then_inc(var_ready, 1)
            dve.wait_ge(sd_ready, 1)
            link(nc.vector.reciprocal(rstd[:, :], sd[:, :]))
            for t in range(NT):
                if rms:
                    ins = nc.vector.tensor_scalar(xn[:, t, :], X[:, t, :], rstd[:, t:t + 1], None, ALU.mult)
                else:
                    ins = nc.vector.tensor_scalar(xn[:, t, :], X[:, t, :], mv[:, t, 0:1], rstd[:, t:t + 1],
                                                  ALU.subtract, ALU.mult)
                ins.then_inc(tile_normed, 1)

        @block.tensor
        def _(pe):
            for half in range(2):
                for c in range(KC):
                    for t in range(4):
                        if c == 0:
                            pe.wait_ge(tile_normed, 4 * half + t + 1)
                        ins = nc.tensor.transpose(ps[:, 2 * half + c, t * P:(t + 1) * P],
                                                  xn[:, 4 * half + t, c * P:(c + 1) * P], ident)
                    ins.then_inc(transposed, 1)

        @block.scalar
        def _(act):
            act.wait_ge(var_ready, 1)
            nc.scalar.activation(sd[:, :], ms[:, :], ACT.Sqrt).then_inc(sd_ready, 1)
            for half in range(2):
                for c in range(KC):
                    act.wait_ge(transposed, 2 * half + c + 1)
                    ins = nc.scalar.activation(hT[:, c, half * BANK:(half + 1) * BANK], ps[:, 2 * half + c, :],
                                               ACT.Identity, bias=offset[:, c:c + 1] if offset is not None else 0.0,
                                               scale=scale[:, c:c + 1])
            ins.then_inc(hT_act, 1)
            act.wait_ge(hT_act, 1)
    k.pop()


def transpose_tokens(k, name, X, xT, ident):
    nc = k.nc
    k.push()
    ps = k.ps(f"{name}_ps", [P, 4, BANK])
    transposed = k.sem(f"{name}_transposed")
    copied = k.sem(f"{name}_copied")
    with nc.Block() as block:
        @block.tensor
        def _(pe):
            for n in range(4):
                half, c = n // KC, n % KC
                for t in range(4):
                    ins = nc.tensor.transpose(ps[:, n, t * P:(t + 1) * P],
                                              X[:, 4 * half + t, c * P:(c + 1) * P], ident)
                ins.then_inc(transposed, 1)

        @block.scalar
        def _(act):
            for n in range(0, 4, 2):
                act.wait_ge(transposed, n + 1)
                nc.scalar.copy(xT[:, n % KC, (n // KC) * BANK:(n // KC + 1) * BANK], ps[:, n, :]).then_inc(copied, 1)

        @block.vector
        def _(dve):
            for n in range(1, 4, 2):
                dve.wait_ge(transposed, n + 1)
                nc.vector.tensor_copy(xT[:, n % KC, (n // KC) * BANK:(n // KC + 1) * BANK],
                                      ps[:, n, :]).then_inc(copied, 1)
    k.pop()


def small_head_attention(k, name, J, ST, VN, queryT, keyTs, attnT, wq, wk, wv, bq, bk, bv_row, scale,
                         mask_of, sel_q, sel_k, expand, ident, loads):
    nc = k.nc
    CH = 8
    W = J * ST * P
    KEYS = ST * P
    RH = P // J
    FD = 32 // J
    KPJ = BANK // KEYS
    NK = CH // KPJ
    NQ = CH // 2
    VT = 2
    NV = ST // VT
    NQK = NK + NQ
    NJ = NQK + NV
    STEPS = B * 2 * CH
    PT_SLOTS = 6
    k.push()
    psS = k.ps(f"{name}_psS", [P, 2, W])
    psT = k.ps(f"{name}_psT", [P, W])
    psM = k.ps(f"{name}_psM", [P, BANK])
    psC = k.ps(f"{name}_psC", [P, BANK])
    Qst = k.sb(f"{name}_Qst", [P, 2, CH, S], F32R)
    Kst = k.sb(f"{name}_Kst", [P, 2, BANK], F32R)
    Kbd = k.sb(f"{name}_Kbd", [P, 2, CH, J, KEYS], F32R)
    Vpad = k.sb(f"{name}_Vpad", [P, 2, ST, CH, J, 32])
    full = k.sb(f"{name}_full", [P, 2, BANK])
    hi = k.sb(f"{name}_hi", [P, BANK], F32R)
    Sm = k.sb(f"{name}_Sm", [P, 2, W])
    PT = k.sb(f"{name}_PT", [P, PT_SLOTS, W])
    nmax = k.sb(f"{name}_nmax", [P, 2, J])
    sums = k.sb(f"{name}_sums", [P, 2, 4 * J])
    rec = k.sb(f"{name}_rec", [P, 4 * J])
    recT = k.sb(f"{name}_recT", [4 * J, P])
    R = k.sb(f"{name}_R", [P, P])

    zeroed = k.sem(f"{name}_zeroed")
    proj_done = k.sem(f"{name}_proj_done")
    full_ready = k.sem(f"{name}_full_ready")
    hi_ready = k.sem(f"{name}_hi_ready")
    stacked = k.sem(f"{name}_stacked")
    k_placed = k.sem(f"{name}_k_placed")
    v_ready = k.sem(f"{name}_v_ready")
    scored = k.sem(f"{name}_scored")
    maxed = k.sem(f"{name}_maxed")
    exped = k.sem(f"{name}_exped")
    turned = k.sem(f"{name}_turned")
    pt_act = k.sem(f"{name}_pt_act")
    pt_dve = k.sem(f"{name}_pt_dve")
    rec_ready = k.sem(f"{name}_rec_ready")
    rec_turned = k.sem(f"{name}_rec_turned")
    recT_ready = k.sem(f"{name}_recT_ready")
    rec_spread = k.sem(f"{name}_rec_spread")
    R_ready = k.sem(f"{name}_R_ready")
    pv_done = k.sem(f"{name}_pv_done")
    out_ready = k.sem(f"{name}_out_ready")

    def where(n):
        b, r = divmod(n, 16)
        c4, r = divmod(r, 8)
        qt, gg = divmod(r, 4)
        return b, c4, qt, gg

    def jobs_at(n):
        b, m = n // 16 + 1, n % 16
        return (b, m) if b < B and m < NJ else None

    with nc.Block() as block:
        @block.tensor
        def _(pe):
            def project(b, m):
                if m == 0 and b > 0:
                    pe.wait_ge(v_ready, b * NV)
                elif 0 < m <= NQK:
                    pe.wait_ge(full_ready, b * NQK + m)
                elif m > NQK:
                    pe.wait_ge(v_ready, b * NV + m - NQK)
                if m < NK:
                    for i in range(KPJ):
                        chunk = m * KPJ + i
                        for s, keyT in enumerate(keyTs):
                            o = i * KEYS + s * S
                            for c in range(KC):
                                ins = nc.tensor.matmul(psM[:, o:o + S], wk[:, c, chunk * P:(chunk + 1) * P],
                                                       keyT[:, c, b * S:(b + 1) * S],
                                                       start=(c == 0), stop=(c == KC - 1))
                elif m < NQK:
                    for i in range(2):
                        chunk = 2 * (m - NK) + i
                        for c in range(KC):
                            ins = nc.tensor.matmul(psM[:, i * S:(i + 1) * S], wq[:, c, chunk * P:(chunk + 1) * P],
                                                   queryT[:, c, b * S:(b + 1) * S],
                                                   start=(c == 0), stop=(c == KC - 1))
                else:
                    N = VN
                    for i in range(VT):
                        t = (m - NQK) * VT + i
                        src, tt = keyTs[t // 2], 2 * b + t % 2
                        for c in range(KC):
                            ins = nc.tensor.matmul(psM[:, i * N:(i + 1) * N], src[:, c, tt * P:(tt + 1) * P],
                                                   wv[:, c, :], start=(c == 0), stop=(c == KC - 1))
                ins.then_inc(proj_done, 1)

            def score(n):
                b, c4, qt, gg = where(n)
                if n % 16 == 0:
                    pe.wait_ge(stacked, (b + 1) * NQK)
                    pe.wait_ge(k_placed, (b + 1) * NK * J)
                if n >= 2:
                    pe.wait_ge(maxed, n - 1)
                chunk = 4 * c4 + gg
                kk = Kbd[:, b % 2, chunk, :, :].rearrange("p j s -> p (j s)")
                for o in range(0, W, BANK):
                    ins = nc.tensor.matmul(psS[:, n % 2, o:o + BANK], Qst[:, b % 2, chunk, qt * P:(qt + 1) * P],
                                           kk[:, o:o + BANK], start=True, stop=True)
                ins.then_inc(scored, 1)

            for load in loads:
                pe.wait_ge(*load)
            pe.wait_ge(zeroed, 2)
            for m in range(NJ):
                project(0, m)
            score(0)
            for n in range(STEPS + 4):
                u, s = n // 4 - 1, n % 4
                if n + 1 < STEPS:
                    score(n + 1)
                if jobs_at(n):
                    project(*jobs_at(n))
                if n < STEPS:
                    pe.wait_ge(exped, n + 1)
                    if n >= 1:
                        pe.wait_ge(pt_act, n)
                        pe.wait_ge(pt_dve, n)
                    for t in range(8):
                        ins = nc.tensor.transpose(psT[:, t * P:(t + 1) * P], Sm[:, n % 2, t * P:(t + 1) * P], ident)
                    ins.then_inc(turned, 1)
                if u < 0:
                    continue
                if s == 0:
                    pe.wait_ge(rec_ready, u + 1)
                    if u >= 1:
                        pe.wait_ge(out_ready, u)
                    nc.tensor.transpose(psC[0:4 * J, 256:256 + P], rec[:, :], ident).then_inc(rec_turned, 1)
                elif s == 1:
                    pe.wait_ge(recT_ready, u + 1)
                    nc.tensor.matmul(psC[:, P:2 * P], expand, recT[:, :], start=True, stop=True).then_inc(rec_spread, 1)
                elif s == 2:
                    b = u // 4
                    pe.wait_ge(R_ready, u + 1)
                    pe.wait_ge(pt_act, 4 * u + 4)
                    pe.wait_ge(pt_dve, 4 * u + 4)
                    pe.wait_ge(v_ready, (b + 1) * NV)
                    for t in range(8):
                        for gg in range(4):
                            chunk = 4 * ((u // 2) % 2) + gg
                            ins = nc.tensor.matmul(psC[32 * gg:32 * gg + 32, 0:P],
                                                   Vpad[:, b % 2, t % ST, chunk, t // ST, :],
                                                   PT[:, (4 * u + gg) % PT_SLOTS, t * P:(t + 1) * P],
                                                   start=(t == 0), stop=(t == 7), tile_position=(0, 32 * gg))
                    ins.then_inc(pv_done, 1)

        @block.scalar
        def _(act):
            def evacuate(b, m):
                if m >= NQK:
                    return
                i = b * NQK + m
                act.wait_ge(proj_done, b * NJ + m + 1)
                if i >= 2:
                    act.wait_ge(stacked, i - 1)
                if m < NK:
                    for c in range(KPJ):
                        ins = nc.scalar.activation(full[:, i % 2, c * KEYS:(c + 1) * KEYS],
                                                   psM[:, c * KEYS:(c + 1) * KEYS], ACT.Identity,
                                                   bias=bk[:, m * KPJ + c:m * KPJ + c + 1])
                else:
                    for c in range(2):
                        ch = 2 * (m - NK) + c
                        ins = nc.scalar.activation(full[:, i % 2, c * S:(c + 1) * S], psM[:, c * S:(c + 1) * S],
                                                   ACT.Identity, bias=bq[:, ch:ch + 1], scale=scale)
                ins.then_inc(full_ready, 1)

            for m in range(NJ):
                evacuate(0, m)
            for n in range(STEPS + 4):
                u, s = n // 4 - 1, n % 4
                if n >= 1 and jobs_at(n - 1):
                    evacuate(*jobs_at(n - 1))
                if u >= 0 and s == 1:
                    act.wait_ge(rec_turned, u + 1)
                    nc.scalar.copy(recT[:, :], psC[0:4 * J, 256:256 + P]).then_inc(recT_ready, 1)
                if u >= 0 and s == 2:
                    act.wait_ge(rec_spread, u + 1)
                    if u >= 1:
                        act.wait_ge(out_ready, u)
                    nc.scalar.copy(R[:, :], psC[:, P:2 * P]).then_inc(R_ready, 1)
                if n < STEPS:
                    q = n // 4
                    act.wait_ge(maxed, n + 1)
                    if q >= 2 and s == 0:
                        act.wait_ge(rec_ready, q - 1)
                    for j in range(J):
                        ins = nc.scalar.activation(Sm[:, n % 2, j * KEYS:(j + 1) * KEYS],
                                                   Sm[:, n % 2, j * KEYS:(j + 1) * KEYS], ACT.Exp,
                                                   bias=nmax[:, n % 2, j:j + 1], scale=-1.0,
                                                   accum_out=sums[:, q % 2, s * J + j:s * J + j + 1])
                    ins.then_inc(exped, 1)
                if 1 <= n <= STEPS:
                    t = n - 1
                    act.wait_ge(turned, t + 1)
                    if t >= PT_SLOTS:
                        act.wait_ge(pv_done, (t - PT_SLOTS) // 4 + 1)
                    nc.scalar.copy(PT[:, t % PT_SLOTS, 0:BANK], psT[:, 0:BANK]).then_inc(pt_act, 1)

        def place(eng, b, m):
            kj = b * NK + m
            for j in range(J):
                r = slice(j * RH, (j + 1) * RH)
                src = Kst[r, kj % 2, :].bitcast(F32).rearrange("p (c s) -> p c s", c=KPJ)
                eng.tensor_copy(Kbd[r, b % 2, m * KPJ:(m + 1) * KPJ, j, :], src).then_inc(k_placed, 1)

        @block.vector
        def _(dve):
            def stack(b, m):
                if m >= NQK:
                    v = m - NQK
                    dve.wait_ge(proj_done, b * NJ + m + 1)
                    if b >= 2 and v == 0:
                        dve.wait_ge(pv_done, 4 * (b - 1))
                    src = psM[:, 0:VT * VN].rearrange("p (t g d) -> p t g d", t=VT, d=FD)
                    row = bv_row.rearrange("p (g d) -> p g d", d=FD)
                    for j in range(J):
                        for t in range(VT):
                            s_, r_ = (src[:, t], row) if J == 4 else (src[:, t, j::J], row[:, j::J])
                            ins = nc.vector.tensor_tensor(Vpad[:, b % 2, v * VT + t, :, j, FD * j:FD * (j + 1)],
                                                          s_, r_, ALU.add)
                    ins.then_inc(v_ready, 1)
                    return
                i = b * NQK + m
                dve.wait_ge(full_ready, i + 1)
                if i >= 1:
                    dve.wait_ge(stacked, i)
                nc.vector.tensor_copy(hi[:, :], full[:, i % 2, :]).then_inc(hi_ready, 1)
                dve.wait_ge(hi_ready, i + 1)
                if m < NK:
                    kj = b * NK + m
                    if kj >= 2:
                        dve.wait_ge(k_placed, (kj - 1) * J)
                    out, sel = Kst[:, kj % 2, :], sel_k
                else:
                    if b >= 2 and m == NK:
                        dve.wait_ge(scored, 16 * (b - 1))
                    q = 2 * (m - NK)
                    out, sel = Qst[:, b % 2, q:q + 2, :].rearrange("p c s -> p (c s)"), sel_q
                nc.vector.scalar_tensor_tensor(out=out, in0=hi[:, :].bitcast(F32), scalar=sel, in1=full[:, i % 2, :],
                                               op0=ALU.mult, op1=ALU.add).then_inc(stacked, 1)
                if m < NK and b == 0:
                    dve.wait_ge(stacked, i + 1)
                    place(nc.vector, 0, m)

            nc.vector.memset(Kbd[:, 0].rearrange("p c j s -> p (c j s)").bitcast(F32), 0.0).then_inc(zeroed, 1)
            dve.wait_ge(zeroed, 2)
            for m in range(NJ):
                stack(0, m)
            for n in range(STEPS + 4):
                u, s = n // 4 - 1, n % 4
                if n < STEPS:
                    b, c4, qt, gg = where(n)
                    dve.wait_ge(scored, n + 1)
                    if n >= 2:
                        dve.wait_ge(turned, n - 1)
                    for j in range(J):
                        ins = nc.vector.tensor_tensor_reduce(Sm[:, n % 2, j * KEYS:(j + 1) * KEYS],
                                                             psS[:, n % 2, j * KEYS:(j + 1) * KEYS], mask_of(b, qt),
                                                             -1.0, 3.4e38, ALU.add, ALU.min,
                                                             nmax[:, n % 2, j:j + 1])
                    ins.then_inc(maxed, 1)
                if 1 <= n <= STEPS:
                    t = n - 1
                    dve.wait_ge(turned, t + 1)
                    if t >= PT_SLOTS:
                        dve.wait_ge(pv_done, (t - PT_SLOTS) // 4 + 1)
                    nc.vector.tensor_copy(PT[:, t % PT_SLOTS, BANK:W], psT[:, BANK:W]).then_inc(pt_dve, 1)
                if u >= 0 and s == 0:
                    dve.wait_ge(exped, 4 * u + 4)
                    if u >= 1:
                        dve.wait_ge(rec_turned, u)
                    nc.vector.reciprocal(rec[:, :], sums[:, u % 2, :]).then_inc(rec_ready, 1)
                if n >= 1 and jobs_at(n - 1):
                    stack(*jobs_at(n - 1))
                if u >= 0 and s == 3:
                    b, c4, qt = u // 4, (u // 2) % 2, u % 2
                    o = b * S + qt * P
                    dve.wait_ge(pv_done, u + 1)
                    nc.vector.tensor_tensor(attnT[:, c4, o:o + P], psC[:, 0:P], R[:, :], ALU.mult).then_inc(out_ready, 1)

        @block.gpsimd
        def _(pool):
            nc.gpsimd.memset(Vpad[:, :].rearrange("p a b c d e -> p (a b c d e)"), 0.0)
            nc.gpsimd.memset(Kbd[:, 1].rearrange("p c j s -> p (c j s)").bitcast(F32), 0.0).then_inc(zeroed, 1)
            for b in range(1, B):
                for m in range(NK):
                    pool.wait_ge(stacked, b * NQK + m + 1)
                    if b == 1 and m == 0:
                        pool.wait_ge(zeroed, 2)
                    if b >= 2 and m == 0:
                        pool.wait_ge(scored, 16 * (b - 1))
                    place(nc.gpsimd, b, m)
    k.pop()


def out_projection(k, name, inT, nch, w, X, residual, row):
    nc = k.nc
    k.push()
    ps = k.ps(f"{name}_ps", [P, NT, BANK])
    addend = k.sb(f"{name}_addend", [P, NT, D])
    done = k.sem(f"{name}_done")
    added = k.sem(f"{name}_added")
    with nc.Block() as block:
        @block.tensor
        def _(pe):
            for t in range(NT):
                for c in range(nch):
                    ins = nc.tensor.matmul(ps[:, t, 0:D], inT[:, c, t * P:(t + 1) * P], w[:, c, :],
                                           start=(c == 0), stop=(c == nch - 1))
                ins.then_inc(done, 1)

        @block.vector
        def _(dve):
            nc.vector.tensor_tensor(addend[:, :, :], residual[:, :, :], row.unsqueeze(1).broadcast_to([P, NT, D]),
                                    ALU.add).then_inc(added, 1)
            dve.wait_ge(added, 1)
            for t in range(NT):
                dve.wait_ge(done, t + 1)
                ins = nc.vector.tensor_tensor(X[:, t, :], ps[:, t, 0:D], addend[:, t, :], ALU.add)
            ins.then_inc(added, 1)
    k.pop()


def hidden_layer(k, name, hT, w1, b1, gT, func, nf):
    nc = k.nc
    k.push()
    ps = k.ps(f"{name}_ps", [P, 8, BANK])
    done = k.sem(f"{name}_done")
    read = k.sem(f"{name}_read")
    with nc.Block() as block:
        @block.tensor
        def _(pe):
            for n in range(2 * nf):
                f, half = n // 2, n % 2
                if n >= 8:
                    pe.wait_ge(read, n - 7)
                for c in range(KC):
                    ins = nc.tensor.matmul(ps[:, n % 8, :], w1[:, c, f * P:(f + 1) * P],
                                           hT[:, c, half * BANK:(half + 1) * BANK],
                                           start=(c == 0), stop=(c == KC - 1))
                ins.then_inc(done, 1)

        @block.scalar
        def _(act):
            for n in range(2 * nf):
                f, half = n // 2, n % 2
                act.wait_ge(done, n + 1)
                nc.scalar.activation(gT[:, f, half * BANK:(half + 1) * BANK], ps[:, n % 8, :], func,
                                     bias=b1[:, f:f + 1]).then_inc(read, 1)
    k.pop()


def wide_head_attention(k, name, hT, cT, w_dram, wo_dram, X, ident, bq, bk, bias_k, bias_v, vrow, bo_row):
    nc = k.nc
    H = 16
    SCALE = 128 ** -0.5
    KS = S + 1
    NU = 4 * H
    k.push()
    psS = k.ps(f"{name}_psS", [P, 2, 2, BANK])
    psT = k.ps(f"{name}_psT", [P, 2, S])
    psC = k.ps(f"{name}_psC", [P, BANK])
    psP = k.ps(f"{name}_psP", [P, 2, BANK])
    wqkv = k.sb(f"{name}_w", [P, 2, KC, 3 * P])
    wo = k.sb(f"{name}_wo", [P, H, D])
    qT = k.sb(f"{name}_qT", [P, 2, TOK])
    kT = k.sb(f"{name}_kT", [P, 2, B, KS + 1])
    v = k.sb(f"{name}_v", [P, 2, NT, P])
    Pr = k.sb(f"{name}_Pr", [P, 2, 2, KS + 1])
    PT = k.sb(f"{name}_PT", [P, 2, 2, S])
    ctxT = k.sb(f"{name}_ctxT", [P, H, TOK])
    nmax = k.sb(f"{name}_nmax", [P, 2, 2])
    sums = k.sb(f"{name}_sums", [P, 2, 2])
    rec = k.sb(f"{name}_rec", [P, 2, 2])
    XB = k.sb(f"{name}_XB", [P, NT, D])

    w_in = [k.sem(f"{name}_w_in{i}") for i in range(2)]
    wo_in = k.sem(f"{name}_wo_in")
    proj_done = k.sem(f"{name}_proj_done")
    qk_ready = k.sem(f"{name}_qk_ready")
    v_ready = k.sem(f"{name}_v_ready")
    extra_key = k.sem(f"{name}_extra_key")
    xb_ready = k.sem(f"{name}_xb_ready")
    scored = k.sem(f"{name}_scored")
    maxed = k.sem(f"{name}_maxed")
    exped = k.sem(f"{name}_exped")
    rec_ready = k.sem(f"{name}_rec_ready")
    normed = k.sem(f"{name}_normed")
    turned = k.sem(f"{name}_turned")
    pt_ready = k.sem(f"{name}_pt_ready")
    pv_done = k.sem(f"{name}_pv_done")
    ctx_ready = k.sem(f"{name}_ctx_ready")
    o_done = k.sem(f"{name}_o_done")
    added = k.sem(f"{name}_added")

    JOBS = [("k", 0), ("q", 0), ("v", 0), ("k", 1), ("q", 1), ("v", 1)]
    AT = {0: (0, 1), 1: (2, 3), 2: (4, None), 3: (None, 5)}
    QK_COUNT = [1, 2, 2, 3, 4, 4]
    V_COUNT = [0, 0, 1, 1, 1, 2]

    with nc.Block() as block:
        @block.sync
        def _(sp):
            for h in range(H):
                if h >= 2:
                    sp.wait_ge(proj_done, 6 * (h - 1))
                sp.dma_start(wqkv[:, h % 2].rearrange("p c n -> p (c n)"), w_dram[h]).then_inc(w_in[h % 2], 16)
                if h == 1:
                    sp.dma_start(wo[:, :].rearrange("p h n -> p (h n)"), wo_dram).then_inc(wo_in, 16)

        @block.gpsimd
        def _(pool):
            for h in range(2):
                nc.gpsimd.tensor_copy(kT[:, h % 2, :, S:KS], bias_k[:, h:h + 1].unsqueeze(2).broadcast_to([P, B, 1])
                                      ).then_inc(extra_key, 1)
            nc.gpsimd.tensor_tensor(XB[:, :].rearrange("p t d -> p (t d)"), X[:, :].rearrange("p t d -> p (t d)"),
                                    bo_row.unsqueeze(1).broadcast_to([P, NT, D]), ALU.add).then_inc(xb_ready, 1)
            for h in range(2, H):
                pool.wait_ge(scored, 4 * (h - 1))
                nc.gpsimd.tensor_copy(kT[:, h % 2, :, S:KS], bias_k[:, h:h + 1].unsqueeze(2).broadcast_to([P, B, 1])
                                      ).then_inc(extra_key, 1)

        @block.tensor
        def _(pe):
            def project(h, m):
                n = 6 * h + m
                kind, half = JOBS[m]
                if m == 0:
                    pe.wait_ge(w_in[h % 2], 16 * (h // 2 + 1))
                if n >= 2:
                    hh, mm = divmod(n - 2, 6)
                    if JOBS[mm][0] == "v":
                        pe.wait_ge(v_ready, 2 * hh + V_COUNT[mm])
                    else:
                        pe.wait_ge(qk_ready, 4 * hh + QK_COUNT[mm])
                o = {"q": 0, "k": P, "v": 2 * P}[kind]
                if kind == "v":
                    for t in range(4):
                        for c in range(KC):
                            ins = nc.tensor.matmul(psP[:, n % 2, t * P:(t + 1) * P],
                                                   cT[:, c, (4 * half + t) * P:(4 * half + t + 1) * P],
                                                   wqkv[:, h % 2, c, o:o + P], start=(c == 0), stop=(c == KC - 1))
                else:
                    src = hT if kind == "q" else cT
                    for c in range(KC):
                        ins = nc.tensor.matmul(psP[:, n % 2, :], wqkv[:, h % 2, c, o:o + P],
                                               src[:, c, half * BANK:(half + 1) * BANK],
                                               start=(c == 0), stop=(c == KC - 1))
                ins.then_inc(proj_done, 1)

            def score(u):
                h, b = divmod(u, 4)
                pe.wait_ge(qk_ready, 4 * h + (2 if b < 2 else 4))
                if b == 0:
                    pe.wait_ge(extra_key, h + 1)
                if u >= 2:
                    pe.wait_ge(exped, u - 1)
                for qt in range(2):
                    o = b * S + qt * P
                    ins = nc.tensor.matmul(psS[:, u % 2, qt, 0:KS], qT[:, h % 2, o:o + P], kT[:, h % 2, b, 0:KS],
                                           start=True, stop=True)
                ins.then_inc(scored, 1)

            for m in range(6):
                project(0, m)
            score(0)
            for u in range(NU):
                h, b = divmod(u, 4)
                before, after = AT[b]
                if h + 1 < H and before is not None:
                    project(h + 1, before)
                if u + 1 < NU:
                    score(u + 1)
                pe.wait_ge(normed, u + 1)
                if u >= 1:
                    pe.wait_ge(pt_ready, u)
                for qt in range(2):
                    for st in range(2):
                        ins = nc.tensor.transpose(psT[:, st, qt * P:(qt + 1) * P],
                                                  Pr[:, u % 2, qt, st * P:(st + 1) * P], ident)
                ins.then_inc(turned, 1)
                if h + 1 < H and after is not None:
                    project(h + 1, after)
                pe.wait_ge(pt_ready, u + 1)
                pe.wait_ge(v_ready, 2 * h + (1 if b < 2 else 2))
                if b % 2 == 0 and u >= 2:
                    pe.wait_ge(ctx_ready, u // 2)
                for st in range(2):
                    ins = nc.tensor.matmul(psC[:, (b % 2) * S:(b % 2 + 1) * S], v[:, h % 2, 2 * b + st, :],
                                           PT[:, u % 2, st, :], start=(st == 0), stop=(st == 1))
                ins.then_inc(pv_done, 1)
            pe.wait_ge(wo_in, 16)
            pe.wait_ge(ctx_ready, NU // 2)
            for t in range(NT):
                if t >= 2:
                    pe.wait_ge(added, t - 1)
                for h in range(H):
                    ins = nc.tensor.matmul(psP[:, t % 2, 0:D], ctxT[:, h, t * P:(t + 1) * P], wo[:, h, :],
                                           start=(h == 0), stop=(h == H - 1))
                ins.then_inc(o_done, 1)

        def copy_ctx(act, pair):
            h, half = divmod(pair, 2)
            act.wait_ge(pv_done, 2 * pair + 2)
            nc.scalar.activation(ctxT[:, h, half * BANK:(half + 1) * BANK], psC[:, :], ACT.Identity,
                                 bias=bias_v[:, h:h + 1]).then_inc(ctx_ready, 1)

        @block.scalar
        def _(act):
            def evacuate(h, m):
                kind, half = JOBS[m]
                if kind == "v":
                    return
                act.wait_ge(proj_done, 6 * h + m + 1)
                if h >= 2:
                    act.wait_ge(scored, 4 * (h - 1))
                if kind == "q":
                    ins = nc.scalar.activation(qT[:, h % 2, half * BANK:(half + 1) * BANK],
                                               psP[:, (6 * h + m) % 2, :], ACT.Identity, bias=bq[:, h:h + 1],
                                               scale=SCALE)
                else:
                    ins = nc.scalar.activation(kT[:, h % 2, 2 * half:2 * half + 2, 0:S],
                                               psP[:, (6 * h + m) % 2, :].rearrange("p (b s) -> p b s", b=2),
                                               ACT.Identity, bias=bk[:, h:h + 1])
                ins.then_inc(qk_ready, 1)

            for m in range(6):
                evacuate(0, m)
            for u in range(NU):
                h, b = divmod(u, 4)
                before, after = AT[b]
                act.wait_ge(maxed, u + 1)
                if u >= 2:
                    act.wait_ge(turned, u - 1)
                for qt in range(2):
                    ins = nc.scalar.activation(Pr[:, u % 2, qt, 0:KS], psS[:, u % 2, qt, 0:KS], ACT.Exp,
                                               bias=nmax[:, u % 2, qt:qt + 1], accum_out=sums[:, u % 2, qt:qt + 1])
                ins.then_inc(exped, 1)
                if u >= 1 and (u - 1) % 2 == 1:
                    pair = (u - 1) // 2
                    copy_ctx(act, pair)
                if h + 1 < H and before is not None:
                    evacuate(h + 1, before)
                act.wait_ge(turned, u + 1)
                if u >= 2:
                    act.wait_ge(pv_done, u - 1)
                nc.scalar.copy(PT[:, u % 2], psT[:, :]).then_inc(pt_ready, 1)
                if h + 1 < H and after is not None:
                    evacuate(h + 1, after)
            copy_ctx(act, NU // 2 - 1)

        @block.vector
        def _(dve):
            def evacuate(h, m):
                kind, half = JOBS[m]
                if kind != "v":
                    return
                dve.wait_ge(proj_done, 6 * h + m + 1)
                if h >= 2:
                    dve.wait_ge(pv_done, 4 * (h - 1))
                row = vrow[:, h * P:(h + 1) * P].unsqueeze(1).broadcast_to([P, 4, P])
                nc.vector.tensor_tensor(v[:, h % 2, 4 * half:4 * half + 4, :],
                                        psP[:, (6 * h + m) % 2, :].rearrange("p (t n) -> p t n", t=4), row,
                                        ALU.add).then_inc(v_ready, 1)

            def top(u):
                dve.wait_ge(scored, u + 1)
                if u >= 2:
                    dve.wait_ge(exped, u - 1)
                nc.vector.tensor_reduce(nmax[:, u % 2], psS[:, u % 2, :, 0:KS], AXX, ALU.max,
                                        negate=True).then_inc(maxed, 1)

            for m in range(6):
                evacuate(0, m)
            top(0)
            for u in range(NU):
                h, b = divmod(u, 4)
                before, after = AT[b]
                dve.wait_ge(exped, u + 1)
                if u >= 1:
                    dve.wait_ge(normed, u)
                nc.vector.reciprocal(rec[:, u % 2], sums[:, u % 2]).then_inc(rec_ready, 1)
                dve.wait_ge(rec_ready, u + 1)
                for qt in range(2):
                    ins = nc.vector.tensor_scalar(Pr[:, u % 2, qt, 0:S], Pr[:, u % 2, qt, 0:S],
                                                  rec[:, u % 2, qt:qt + 1], None, ALU.mult)
                ins.then_inc(normed, 1)
                if h + 1 < H and before is not None:
                    evacuate(h + 1, before)
                if u + 1 < NU:
                    top(u + 1)
                if h + 1 < H and after is not None:
                    evacuate(h + 1, after)
            dve.wait_ge(xb_ready, 1)
            for t in range(NT):
                dve.wait_ge(o_done, t + 1)
                nc.vector.tensor_tensor(X[:, t, :], psP[:, t % 2, 0:D], XB[:, t, :], ALU.add).then_inc(added, 1)
    k.pop()


def norm_rows(k, name, X, eps, gamma, beta):
    nc = k.nc
    k.push()
    stats = k.sb(f"{name}_stats", [P, NT, 6])
    mv = k.sb(f"{name}_mv", [P, NT, 2])
    ve = k.sb(f"{name}_ve", [P, NT])
    sd = k.sb(f"{name}_sd", [P, NT])
    rstd = k.sb(f"{name}_rstd", [P, NT])
    small = k.sem(f"{name}_small")
    var_ready = k.sem(f"{name}_var_ready")
    sd_ready = k.sem(f"{name}_sd_ready")
    with nc.Block() as block:
        @block.vector
        def _(dve):
            done = [0]

            def link(ins):
                done[0] += 1
                ins.then_inc(small, 1)
                dve.wait_ge(small, done[0])

            for t in range(NT):
                ins = nc.vector.bn_stats(stats[:, t, :], X[:, t, :])
            link(ins)
            for t in range(NT):
                ins = nc.vector.bn_aggr(mv[:, t, :], stats[:, t, :])
            link(ins)
            nc.vector.tensor_scalar(ve[:, :], mv[:, :, 1], eps, None, ALU.add).then_inc(var_ready, 1)
            dve.wait_ge(sd_ready, 1)
            link(nc.vector.reciprocal(rstd[:, :], sd[:, :]))
            for t in range(NT):
                ins = nc.vector.tensor_scalar(X[:, t, :], X[:, t, :], mv[:, t, 0:1], rstd[:, t:t + 1],
                                              ALU.subtract, ALU.mult)
            link(ins)
            link(nc.vector.tensor_tensor(X[:, :, :], X[:, :, :], gamma.unsqueeze(1).broadcast_to([P, NT, D]), ALU.mult))
            link(nc.vector.tensor_tensor(X[:, :, :], X[:, :, :], beta.unsqueeze(1).broadcast_to([P, NT, D]), ALU.add))

        @block.scalar
        def _(act):
            act.wait_ge(var_ready, 1)
            nc.scalar.activation(sd[:, :], ve[:, :], ACT.Sqrt).then_inc(sd_ready, 1)
    k.pop()


def single_head_attention(k, name, xT, cT, X, w, w_in, alpha, ident):
    nc = k.nc
    SCALE = D ** -0.5
    k.push()
    qT = k.sb(f"{name}_qT", [P, KC, TOK])
    kT = k.sb(f"{name}_kT", [P, KC, TOK])
    v = k.sb(f"{name}_v", [P, NT, D])
    k.push()
    ps = k.ps(f"{name}_ps", [P, 8, BANK])
    proj_done = k.sem(f"{name}_proj_done")
    by_act = k.sem(f"{name}_by_act")
    by_dve = k.sem(f"{name}_by_dve")
    NJ = 12
    with nc.Block() as block:
        @block.tensor
        def _(pe):
            pe.wait_ge(w_in, 16)
            for n in range(NJ):
                if n >= 8:
                    pe.wait_ge(by_dve if n % 2 else by_act, (n - 8) // 2 + 1)
                if n < 8:
                    a, oc, half = n // 4, n // 2 % 2, n % 2
                    for c in range(KC):
                        ins = nc.tensor.matmul(ps[:, n % 8, :], w[:, c, a, oc * P:(oc + 1) * P],
                                               (xT, cT)[a][:, c, half * BANK:(half + 1) * BANK],
                                               start=(c == 0), stop=(c == KC - 1))
                else:
                    for i in range(2):
                        t = 2 * (n - 8) + i
                        for c in range(KC):
                            ins = nc.tensor.matmul(ps[:, n % 8, i * D:(i + 1) * D], cT[:, c, t * P:(t + 1) * P],
                                                   w[:, c, 2, :], start=(c == 0), stop=(c == KC - 1))
                ins.then_inc(proj_done, 1)

        def target(n):
            if n < 8:
                a, oc, half = n // 4, n // 2 % 2, n % 2
                return (qT, kT)[a][:, oc, half * BANK:(half + 1) * BANK]
            return v[:, 2 * (n - 8):2 * (n - 8) + 2, :].rearrange("p t d -> p (t d)")

        @block.scalar
        def _(act):
            for n in range(0, NJ, 2):
                act.wait_ge(proj_done, n + 1)
                nc.scalar.activation(target(n), ps[:, n % 8, :], ACT.Copy, scale=SCALE if n < 4 else 1.0
                                     ).then_inc(by_act, 1)

        @block.vector
        def _(dve):
            for n in range(1, NJ, 2):
                dve.wait_ge(proj_done, n + 1)
                nc.vector.tensor_scalar(target(n), ps[:, n % 8, :], SCALE if n < 4 else 1.0, None, ALU.mult
                                        ).then_inc(by_dve, 1)
    k.pop()

    psS = k.ps(f"{name}_psS", [P, 2, BANK])
    psT = k.ps(f"{name}_psT", [P, 2, S])
    psX = k.ps(f"{name}_psX", [P, KC, S])
    psD = k.ps(f"{name}_psD", [P, 2, BANK])
    Pr = k.sb(f"{name}_Pr", [P, 2, S])
    PT = k.sb(f"{name}_PT", [P, 2, 2, S])
    cxT = k.sb(f"{name}_cxT", [P, KC, S])
    nmax = k.sb(f"{name}_nmax", [P, 2])
    sums = k.sb(f"{name}_sums", [P, 2])
    rec = k.sb(f"{name}_rec", [P, 2])
    scored = k.sem(f"{name}_scored")
    maxed = k.sem(f"{name}_maxed")
    exped = k.sem(f"{name}_exped")
    rec_ready = k.sem(f"{name}_rec_ready")
    normed = k.sem(f"{name}_normed")
    turned = k.sem(f"{name}_turned")
    pt_ready = k.sem(f"{name}_pt_ready")
    x_done = k.sem(f"{name}_x_done")
    cx_ready = k.sem(f"{name}_cx_ready")
    d_done = k.sem(f"{name}_d_done")
    added = k.sem(f"{name}_added")
    with nc.Block() as block:
        @block.tensor
        def _(pe):
            def score(n):
                if n >= 2:
                    pe.wait_ge(exped, n - 1)
                for c in range(KC):
                    ins = nc.tensor.matmul(psS[:, n % 2, 0:S], qT[:, c, n * P:(n + 1) * P],
                                           kT[:, c, (n // 2) * S:(n // 2 + 1) * S],
                                           start=(c == 0), stop=(c == KC - 1))
                ins.then_inc(scored, 1)

            score(0)
            for n in range(NT):
                if n + 1 < NT:
                    score(n + 1)
                pe.wait_ge(normed, n + 1)
                if n >= 1:
                    pe.wait_ge(pt_ready, n)
                qt, b = n % 2, n // 2
                for st in range(2):
                    ins = nc.tensor.transpose(psT[:, st, qt * P:(qt + 1) * P], Pr[:, n % 2, st * P:(st + 1) * P],
                                              ident)
                ins.then_inc(turned, 1)
                if qt == 0:
                    continue
                pe.wait_ge(pt_ready, n + 1)
                if b >= 1:
                    pe.wait_ge(cx_ready, b)
                for fc in range(KC):
                    for st in range(2):
                        ins = nc.tensor.matmul(psX[:, fc, :], v[:, 2 * b + st, fc * P:(fc + 1) * P],
                                               PT[:, b % 2, st, :], start=(st == 0), stop=(st == 1))
                ins.then_inc(x_done, 1)
                pe.wait_ge(cx_ready, b + 1)
                for i in range(2):
                    t = 2 * b + i
                    if t >= 2:
                        pe.wait_ge(added, t - 1)
                    for c in range(KC):
                        ins = nc.tensor.matmul(psD[:, t % 2, 0:D], cxT[:, c, i * P:(i + 1) * P], w[:, c, 3, :],
                                               start=(c == 0), stop=(c == KC - 1))
                    ins.then_inc(d_done, 1)

        @block.scalar
        def _(act):
            for n in range(NT):
                act.wait_ge(maxed, n + 1)
                if n >= 2:
                    act.wait_ge(turned, n - 1)
                nc.scalar.activation(Pr[:, n % 2, :], psS[:, n % 2, 0:S], ACT.Exp, bias=nmax[:, n % 2:n % 2 + 1],
                                     accum_out=sums[:, n % 2:n % 2 + 1]).then_inc(exped, 1)
                qt, b = n % 2, n // 2
                act.wait_ge(turned, n + 1)
                if b >= 2 and qt == 0:
                    act.wait_ge(x_done, b - 1)
                nc.scalar.copy(PT[:, b % 2, :, qt * P:(qt + 1) * P], psT[:, :, qt * P:(qt + 1) * P]
                               ).then_inc(pt_ready, 1)
                if qt == 1:
                    act.wait_ge(x_done, b + 1)
                    if b >= 1:
                        act.wait_ge(d_done, 2 * b)
                    nc.scalar.copy(cxT[:, :, :], psX[:, :, :]).then_inc(cx_ready, 1)

        def add(dve, t):
            dve.wait_ge(d_done, t + 1)
            nc.vector.scalar_tensor_tensor(out=X[:, t, :], in0=psD[:, t % 2, 0:D], scalar=alpha, in1=X[:, t, :],
                                           op0=ALU.mult, op1=ALU.add).then_inc(added, 1)

        @block.vector
        def _(dve):
            for n in range(NT):
                dve.wait_ge(scored, n + 1)
                if n >= 2:
                    dve.wait_ge(exped, n - 1)
                nc.vector.tensor_reduce(nmax[:, n % 2:n % 2 + 1], psS[:, n % 2, 0:S], AXX, ALU.max,
                                        negate=True).then_inc(maxed, 1)
                dve.wait_ge(exped, n + 1)
                if n >= 1:
                    dve.wait_ge(normed, n)
                nc.vector.reciprocal(rec[:, n % 2:n % 2 + 1], sums[:, n % 2:n % 2 + 1]).then_inc(rec_ready, 1)
                dve.wait_ge(rec_ready, n + 1)
                nc.vector.tensor_scalar(Pr[:, n % 2, :], Pr[:, n % 2, :], rec[:, n % 2:n % 2 + 1], None,
                                        ALU.mult).then_inc(normed, 1)
                if n >= 2 and n % 2 == 0:
                    add(dve, n - 2)
                    add(dve, n - 1)
            add(dve, NT - 2)
            add(dve, NT - 1)

    k.pop()


COLS = ["g_bq", "g_bk", "sel_gq", "sel_gk", "l_bq", "l_bk", "sel_lq", "sel_lk",
        "ln1_scale", "ln1_offset", "bq1", "bk1", "bias_k1", "bias_v1",
        "ln2_scale", "ln2_offset", "bq2", "bk2", "bias_k2", "bias_v2",
        "ln_mlp_scale", "ln_mlp_offset", "b_fc1", "alpha", "postnorm_w", "mlp_b1"]
ROWS = ["g_bv", "g_bo", "gamma", "beta", "bo1", "bo2", "b_fc2", "l_bv", "l_bo", "mlp_b2"]


def cross_attention_stack(nc, a, at_col, at_row, out):
    with ExitStack() as outer:
        k = Core(nc, outer)
        X = k.sb("X", [P, NT, D])
        xT = k.sb("xT", [P, KC, TOK])
        cT = k.sb("cT", [P, KC, TOK])
        NCOL, NROW = a["cols"].shape[1], a["rows"].shape[1]
        cols = k.sb("cols", [P, NCOL])
        rows = k.sb("rows", [P, NROW])
        consts = k.sb("consts", [P, 3 * P])
        ident = consts[:, 0:P]
        expand_g = consts[0:16, P:2 * P]
        expand_l = consts[0:8, 2 * P:3 * P]

        def col(name, dt=None):
            o, w = at_col[name]
            return cols[:, o:o + w]

        def row(name):
            o, w = at_row[name]
            return rows[:, o:o + w]

        act_in = k.sem("activations_in")
        vec_in = k.sem("vectors_in")
        x_in = k.sem("x_in")
        g_in = k.sem("g_weights_in")
        mask_in = k.sem("mask_in")
        prep = k.sem("vectors_prepared")

        k.push()
        g_wo = k.sb("g_wo", [P, KC, D])
        k.push()
        g_w = k.sb("g_w", [P, KC, 2 * 8 * P + 64])
        mask = k.sb("mask", [P, NT, S])
        with nc.Block() as block:
            @block.sync
            def _(sp):
                sp.dma_start(xT[:, :].rearrange("p c t -> p (c t)"), a["xT"]).then_inc(act_in, 16)
                sp.dma_start(cT[:, :].rearrange("p c t -> p (c t)"), a["cT"]).then_inc(act_in, 16)
                sp.dma_start(X[:, :], a["x"].rearrange("(n p) d -> p n d", p=P)).then_inc(x_in, 16)
                sp.dma_start(mask[:, :], a["mask"].rearrange("(n p) d -> p n d", p=P)).then_inc(mask_in, 16)
                sp.wait_ge(mask_in, 16)
                sp.wait_ge(x_in, 16)

            @block.scalar
            def _(act):
                act.dma_start(cols[:, :], a["cols"]).then_inc(vec_in, 16)
                act.dma_start(rows[:, :], a["rows"].broadcast_to([P, NROW])).then_inc(vec_in, 16)
                act.dma_start(consts[:, :], a["consts"]).then_inc(vec_in, 16)
                act.dma_start(g_w[:, :].rearrange("p c n -> p (c n)"), a["g_w"]).then_inc(g_in, 16)
                act.dma_start(g_wo[:, :].rearrange("p c n -> p (c n)"), a["g_wo"]).then_inc(g_in, 16)

            @block.vector
            def _(dve):
                dve.wait_ge(vec_in, 48)
                for name, scale in (("g_bq", 8 ** -0.5), ("bq1", 128 ** -0.5), ("bq2", 128 ** -0.5),
                                    ("l_bq", 1 / 16)):
                    ins = nc.vector.tensor_scalar(col(name), col(name), scale, None, ALU.mult)
                ins.then_inc(prep, 1)
                dve.wait_ge(prep, 1)
        small_head_attention(
            k, "gqa", 4, 2, 64, xT, [cT], xT, g_w[:, :, 0:8 * P], g_w[:, :, 8 * P:16 * P], g_w[:, :, 16 * P:], col("g_bq"), col("g_bk"), row("g_bv"), 8 ** -0.5,
            lambda b, qt: mask[:, 2 * b + qt, :], col("sel_gq"), col("sel_gk"), expand_g, ident,
            [(act_in, 32), (vec_in, 48), (g_in, 32)])
        k.pop()
        out_projection(k, "gqa_out", xT, KC, g_wo, X, X, row("g_bo"))
        k.pop()
        norm_rows(k, "gqa_norm", X, 1e-6, row("gamma"), row("beta"))

        hT = xT
        for i in (1, 2):
            k.push()
            xn = k.sb(f"ln{i}_xn", [P, NT, D])
            norm_transpose(k, f"ln{i}", X, hT, xn, ident, 1e-5, col(f"ln{i}_scale"), col(f"ln{i}_offset"))
            k.pop()
            k.push()
            vrow = k.sb(f"vrow{i}", [P, 16 * P])
            k.push()
            bvr = k.sb(f"bias_v_row{i}", [P, 16 * P])
            rows_in = k.sem(f"v_rows_in{i}")
            with nc.Block() as block:
                @block.sync
                def _(sp):
                    sp.dma_start(vrow[:, :], a[f"bv{i}"].broadcast_to([P, 16 * P])).then_inc(rows_in, 16)
                    sp.dma_start(bvr[:, :], a[f"bias_v{i}"].broadcast_to([P, 16 * P])).then_inc(rows_in, 16)

                @block.vector
                def _(dve):
                    dve.wait_ge(rows_in, 32)
                    nc.vector.tensor_tensor(vrow[:, :], vrow[:, :], bvr[:, :], ALU.subtract).then_inc(rows_in, 1)
                    dve.wait_ge(rows_in, 33)
            k.pop()
            wide_head_attention(k, f"wide{i}", hT, cT, a[f"w{i}"], a[f"wo{i}"], X, ident, col(f"bq{i}"), col(f"bk{i}"),
                                col(f"bias_k{i}"), col(f"bias_v{i}"), vrow, row(f"bo{i}"))
            k.pop()

        def mlp(name, w1_dram, w2_dram, b1, func, residual, b2, norm):
            k.push()
            w1 = k.sb(f"{name}_w1", [P, KC, 1024])
            w2 = k.sb(f"{name}_w2", [P, 8, D])
            gT = k.sb(f"{name}_gT", [P, 8, TOK])
            xn = k.sb(f"{name}_xn", [P, NT, D])
            w_in = k.sem(f"{name}_w_in")
            with nc.Block() as block:
                @block.sync
                def _(sp):
                    sp.dma_start(w1[:, :].rearrange("p c n -> p (c n)"), w1_dram).then_inc(w_in, 16)
                    sp.dma_start(w2[:, :].rearrange("p c n -> p (c n)"), w2_dram).then_inc(w_in, 16)
                    sp.wait_ge(w_in, 32)
            norm(xn)
            hidden_layer(k, f"{name}_1", hT, w1, b1, gT, func, 8)
            out_projection(k, f"{name}_2", gT, 8, w2, X, residual, b2)
            k.pop()

        mlp("mlp1", a["w_fc1"], a["w_fc2"], col("b_fc1"), ACT.Gelu, X, row("b_fc2"),
            lambda xn: norm_transpose(k, "ln_mlp", X, hT, xn, ident, 1e-5, col("ln_mlp_scale"), col("ln_mlp_offset")))

        k.push()
        s_w = k.sb("s_w", [P, KC, 4, D])
        s_in = k.sem("s_weights_in")
        with nc.Block() as block:
            @block.sync
            def _(sp):
                sp.dma_start(s_w[:, :].rearrange("p c a n -> p (c a n)"), a["s_w"]).then_inc(s_in, 16)
        transpose_tokens(k, "x2", X, xT, ident)
        single_head_attention(k, "one", xT, cT, X, s_w, s_in, col("alpha"), ident)
        k.pop()

        transpose_tokens(k, "x3", X, xT, ident)
        l_wo = k.sb("l_wo", [P, KC, D])
        k.push()
        l_w = k.sb("l_w", [P, KC, 2 * 8 * P + D])
        far = k.sb("far", [P, B, 2 * S])
        k.push()
        mask_int = k.sb("mask_int", [P, B * S], I32)
        l_in = k.sem("l_weights_in")
        lm_in = k.sem("l_mask_in")
        far_ready = k.sem("far_ready")
        with nc.Block() as block:
            @block.sync
            def _(sp):
                sp.dma_start(mask_int[:, :], a["key_mask"].broadcast_to([P, B * S])).then_inc(lm_in, 16)
                sp.dma_start(l_w[:, :].rearrange("p c n -> p (c n)"), a["l_w"]).then_inc(l_in, 16)
                sp.dma_start(l_wo[:, :].rearrange("p c n -> p (c n)"), a["l_wo"]).then_inc(l_in, 16)

            @block.vector
            def _(dve):
                nc.vector.memset(far[:, :, S:2 * S], 0.0)
                dve.wait_ge(lm_in, 16)
                nc.vector.tensor_scalar(far[:, :, 0:S], mask_int[:, :].rearrange("p (b s) -> p b s", b=B), 0.0, FAR,
                                        ALU.is_equal, ALU.mult).then_inc(far_ready, 1)
                dve.wait_ge(far_ready, 1)
        k.pop()
        small_head_attention(
            k, "latent", 2, 4, 256, xT, [cT, xT], xT, l_w[:, :, 0:8 * P], l_w[:, :, 8 * P:16 * P],
            l_w[:, :, 16 * P:], col("l_bq"), col("l_bk"), row("l_bv"), 1 / 16,
            lambda b, qt: far[:, b, :], col("sel_lq"), col("sel_lk"), expand_l, ident, [(l_in, 32)])
        k.pop()
        LX = k.sb("LX", [P, NT, D])
        out_projection(k, "latent_out", xT, KC, l_wo, LX, X, row("l_bo"))
        saved = X
        X = LX
        mlp("mlp3", a["mlp_w1"], a["mlp_w2"], col("mlp_b1"), ACT.Gelu_apprx_tanh, saved, row("mlp_b2"),
            lambda xn: norm_transpose(k, "rms", X, hT, xn, ident, 1e-6, col("postnorm_w"), None, rms=True))
        stored = k.sem("stored")
        with nc.Block() as block:
            @block.sync
            def _(sp):
                sp.dma_start(out.rearrange("(n p) d -> p n d", p=P), X[:, :]).then_inc(stored, 16)
                sp.wait_ge(stored, 16)


def kernel(**inputs):
    import numpy as np
    import concourse.bacc as bacc
    from concourse.bass_utils import run_bass_kernel_spmd

    v = {n: np.asarray(x) for n, x in inputs.items()}

    def w(m):
        m = np.asarray(m)
        return np.ascontiguousarray(m.reshape(-1, 128, m.shape[1]).transpose(1, 0, 2).reshape(128, -1))

    def spread(bias, J):
        b4 = np.asarray(bias).reshape(8, -1, 1, 32 // J)
        return np.broadcast_to(b4, (8, J, 4, 32 // J)).transpose(1, 2, 3, 0).reshape(128, 8)

    def copies(m, J):
        m4 = np.asarray(m).reshape(256, 8, -1, 1, 32 // J)
        return np.broadcast_to(m4, (256, 8, J, 4, 32 // J)).reshape(256, 1024)

    def by_feature(vec):
        return np.asarray(vec).reshape(-1, 128).T

    L0, L1, L2, L3 = "L0_xattn_", "L1_xattn_", "L2_xattn_", "L3_xattn_"
    p = np.arange(128)
    kv_b = v[L3 + "kv_b"].reshape(256, 2)
    kv_w = v[L3 + "kv_w"].reshape(256, 256, 2)
    col = {
        "g_bq": spread(v[L0 + "bq"], 4), "g_bk": spread(v[L0 + "bk"], 4),
        "sel_gq": -(p // 8 % 4 >= 2).astype(np.float32)[:, None],
        "sel_gk": -(p // 8 % 2).astype(np.float32)[:, None],
        "l_bq": spread(v[L3 + "q_b"], 2), "l_bk": spread(kv_b[:, 0], 2),
        "sel_lq": -(p // 16 % 4 >= 2).astype(np.float32)[:, None],
        "sel_lk": -(p // 16 % 2).astype(np.float32)[:, None],
        "alpha": np.broadcast_to(v[L2 + "alpha"].reshape(1, 1), (128, 1)),
        "postnorm_w": by_feature(v[L3 + "postnorm_w"]), "mlp_b1": by_feature(v[L3 + "mlp_b1"]),
    }
    for n in COLS:
        if n not in col:
            col[n] = by_feature(v[L1 + n])
    row = {"g_bv": v[L0 + "bv"], "g_bo": v[L0 + "bo"], "gamma": v[L0 + "gamma"], "beta": v[L0 + "beta"],
           "bo1": v[L1 + "bo1"], "bo2": v[L1 + "bo2"], "b_fc2": v[L1 + "b_fc2"],
           "l_bv": kv_b[:, 1], "l_bo": v[L3 + "out_b"], "mlp_b2": v[L3 + "mlp_b2"]}

    def offsets(names, widths):
        at, o = {}, 0
        for n in names:
            at[n] = (o, widths[n])
            o += widths[n]
        return at

    at_col = offsets(COLS, {n: col[n].shape[1] for n in COLS})
    at_row = offsets(ROWS, {n: row[n].size for n in ROWS})
    consts = np.zeros((128, 384), np.float32)
    consts[:, 0:128] = np.eye(128)
    consts[p // 8, 128 + p] = 1.0
    consts[p // 16, 256 + p] = 1.0

    arrays = {
        "x": v["x"].reshape(1024, 256), "xT": w(v["x"].reshape(1024, 256).T), "cT": w(v["ctx_2048"].reshape(1024, 256).T),
        "mask": v["mask_Bx1xSxS2_ff0"].reshape(1024, 256), "key_mask": v["mask_BxS2_ik0"].reshape(1, 1024),
        "cols": np.concatenate([col[n] for n in COLS], axis=1),
        "rows": np.concatenate([row[n].reshape(1, -1) for n in ROWS], axis=1),
        "consts": consts,
        "g_w": w(np.concatenate([copies(v[L0 + "Wq"], 4), copies(v[L0 + "Wk"], 4), v[L0 + "Wv"]], axis=1)),
        "g_wo": w(v[L0 + "Wo"]), "l_wo": w(v[L3 + "out_w"]),
        "s_w": w(np.concatenate([v[L2 + n].T for n in ("w_q", "w_k", "w_v", "w_o")], axis=1)),
        "l_w": w(np.concatenate([copies(v[L3 + "q_w"], 2), copies(kv_w[:, :, 0], 2), kv_w[:, :, 1]], axis=1)),
        "w_fc1": w(v[L1 + "w_fc1"]), "w_fc2": w(v[L1 + "w_fc2"]),
        "mlp_w1": w(v[L3 + "mlp_w1"]), "mlp_w2": w(v[L3 + "mlp_w2"]),
    }
    for i in ("1", "2"):
        qkv = np.stack([v[L1 + n + i].reshape(2, 128, 16, 128) for n in ("wq", "wk", "wv")])
        arrays["w" + i] = qkv.transpose(3, 2, 1, 0, 4).reshape(16, 128, 768)
        arrays["wo" + i] = w(v[L1 + "wo" + i])
        arrays["bv" + i] = v[L1 + "bv" + i].reshape(1, 2048)
        arrays["bias_v" + i] = v[L1 + "bias_v" + i].reshape(1, 2048)

    nc = bacc.Bacc("TRN2", target_bir_lowering=False, num_devices=1)
    feed, aps = {}, {}
    for n, x in arrays.items():
        x = np.ascontiguousarray(x)
        feed[f"in_{n}"] = x
        aps[n] = nc.dram_tensor(f"in_{n}", x.shape, mybir.dt.from_np(x.dtype), kind="ExternalInput").ap()
    out = nc.dram_tensor("out", (1024, 256), F32, kind="ExternalOutput").ap()
    cross_attention_stack(nc, aps, at_col, at_row, out)
    r = run_bass_kernel_spmd(nc, [feed], core_ids=[0])
    return r.results[0]["out"].reshape(4, 256, 256)
```

```python
from contextlib import ExitStack

import concourse.bass as bass
from concourse import mybir

F32 = mybir.dt.float32
F32R = mybir.dt.float32r
BF16 = mybir.dt.bfloat16
I32 = mybir.dt.int32
ACT = mybir.ActivationFunctionType
ALU = mybir.AluOpType
AXX = mybir.AxisListType.X

P = 128
B = 4
S = 256
TOK = B * S
NT = TOK // P
D = 256
KC = D // P
BANK = 512
FAR = -1e30


class Core:

    def __init__(self, nc, outer):
        self.nc, self.outer, self.stack = nc, outer, [outer]
        self.norm_sems = [self.sem(f"norm_{n}") for n in ("small", "var_ready", "sd_ready", "tile_normed",
                                                          "transposed", "hT_ready")]
        self.norm_uses, self.norm_links = 0, [0]

    def sb(self, name, shape, dt=F32):
        return self.stack[-1].enter_context(self.nc.sbuf_tensor(name, shape, dt))

    def ps(self, name, shape, dt=F32):
        return self.stack[-1].enter_context(self.nc.psum_tensor(name, shape, dt))

    def sem(self, name):
        return self.outer.enter_context(self.nc.semaphore(name))

    def push(self):
        self.stack.append(ExitStack())

    def pop(self):
        self.stack.pop().close()


def norm_transpose(k, name, X, hT, xn, ident, eps, scale=None, offset=None, rms=False):
    nc = k.nc
    k.push()
    ps = k.ps(f"{name}_ps", [P, 4, BANK])
    stats = k.sb(f"{name}_stats", [P, NT, 6])
    mv = k.sb(f"{name}_mv", [P, NT, 2])
    ms = k.sb(f"{name}_ms", [P, NT])
    ve = k.sb(f"{name}_ve", [P, NT])
    sd = k.sb(f"{name}_sd", [P, NT])
    rstd = k.sb(f"{name}_rstd", [P, NT])
    small, var_ready, sd_ready, tile_normed, transposed, hT_act = k.norm_sems
    use, done = k.norm_uses, k.norm_links
    k.norm_uses += 1
    with nc.Block() as block:
        @block.vector
        def _(dve):
            def link(ins):
                done[0] += 1
                ins.then_inc(small, 1)
                dve.wait_ge(small, done[0])

            for t in range(NT):
                ins = nc.vector.bn_stats(stats[:, t, :], X[:, t, :])
            link(ins)
            for t in range(NT):
                ins = nc.vector.bn_aggr(mv[:, t, :], stats[:, t, :])
            link(ins)
            if rms:
                link(nc.vector.tensor_tensor(ms[:, :], mv[:, :, 0], mv[:, :, 0], ALU.mult))
                link(nc.vector.tensor_tensor(ve[:, :], ms[:, :], mv[:, :, 1], ALU.add))
                nc.vector.tensor_scalar(ms[:, :], ve[:, :], eps, None, ALU.add).then_inc(var_ready, 1)
            else:
                nc.vector.tensor_scalar(ms[:, :], mv[:, :, 1], eps, None, ALU.add).then_inc(var_ready, 1)
            dve.wait_ge(sd_ready, use + 1)
            link(nc.vector.reciprocal(rstd[:, :], sd[:, :]))
            for t in range(NT):
                if rms:
                    ins = nc.vector.tensor_scalar(xn[:, t, :], X[:, t, :], rstd[:, t:t + 1], None, ALU.mult)
                else:
                    ins = nc.vector.tensor_scalar(xn[:, t, :], X[:, t, :], mv[:, t, 0:1], rstd[:, t:t + 1],
                                                  ALU.subtract, ALU.mult)
                ins.then_inc(tile_normed, 1)

        @block.tensor
        def _(pe):
            for half in range(2):
                for c in range(KC):
                    for t in range(4):
                        if c == 0:
                            pe.wait_ge(tile_normed, NT * use + 4 * half + t + 1)
                        ins = nc.tensor.transpose(ps[:, 2 * half + c, t * P:(t + 1) * P],
                                                  xn[:, 4 * half + t, c * P:(c + 1) * P], ident)
                    ins.then_inc(transposed, 1)

        @block.scalar
        def _(act):
            act.wait_ge(var_ready, use + 1)
            nc.scalar.activation(sd[:, :], ms[:, :], ACT.Sqrt).then_inc(sd_ready, 1)
            for half in range(2):
                for c in range(KC):
                    act.wait_ge(transposed, 4 * use + 2 * half + c + 1)
                    ins = nc.scalar.activation(hT[:, c, half * BANK:(half + 1) * BANK], ps[:, 2 * half + c, :],
                                               ACT.Identity, bias=offset[:, c:c + 1] if offset is not None else 0.0,
                                               scale=scale[:, c:c + 1])
            ins.then_inc(hT_act, 1)
            act.wait_ge(hT_act, use + 1)
    k.pop()


def transpose_tokens(k, name, X, xT, ident):
    nc = k.nc
    k.push()
    ps = k.ps(f"{name}_ps", [P, 4, BANK])
    transposed = k.sem(f"{name}_transposed")
    copied = k.sem(f"{name}_copied")
    with nc.Block() as block:
        @block.tensor
        def _(pe):
            for n in range(4):
                half, c = n // KC, n % KC
                for t in range(4):
                    ins = nc.tensor.transpose(ps[:, n, t * P:(t + 1) * P],
                                              X[:, 4 * half + t, c * P:(c + 1) * P], ident)
                ins.then_inc(transposed, 1)

        @block.scalar
        def _(act):
            for n in range(0, 4, 2):
                act.wait_ge(transposed, n + 1)
                nc.scalar.copy(xT[:, n % KC, (n // KC) * BANK:(n // KC + 1) * BANK], ps[:, n, :]).then_inc(copied, 1)

        @block.vector
        def _(dve):
            for n in range(1, 4, 2):
                dve.wait_ge(transposed, n + 1)
                nc.vector.tensor_copy(xT[:, n % KC, (n // KC) * BANK:(n // KC + 1) * BANK],
                                      ps[:, n, :]).then_inc(copied, 1)
    k.pop()


def small_head_attention(k, name, J, queryT, keyTs, attnT, wq, wk, wv, bq, bk, bv_row, scale, mask_of,
                         sel_dram, expand, ident, loads, act_copies, mask_dram=None, mask=None, mask_in=None):
    nc = k.nc
    CH = 8
    W = 1024
    KEYS = W // J
    ST = KEYS // P
    RH = P // J
    FD = 32 // J
    VN = wv.shape[2]
    KPJ = BANK // KEYS
    NKS = 4 // KPJ
    SHARED = J == 4
    NV = ST // 2
    STEPS = B * 16
    OCTETS = STEPS // 8
    PV_TILES = [(0,), (1, 2), (3,), (4, 5), (6,), (7,)]
    TAIL = 6
    SM = 3
    RAW = [("kq", 0)] if SHARED else [("k", 0), ("q", 0)]
    STACKS = [("ks", i) for i in range(NKS)] + [("qs", i) for i in range(2)]
    if SHARED:
        PLAN = {-2: ("ks", 0, 0), 1: ("ks", 1, 0), 2: ("qs", 0, 0), 3: ("kq", 0, 1), 4: ("qs", 1, 0)}
    else:
        PLAN = {-2: ("ks", 0, 0), -1: ("ks", 1, 0), 0: ("ks", 2, 0), 1: ("ks", 3, 0),
                2: ("qs", 0, 0), 3: ("k", 0, 1), 4: ("qs", 1, 0), 5: ("q", 0, 1)}

    def planned(n):
        v, at = (n // 8 + 2, n % 8 - 8) if n % 8 >= 6 else (n // 8 + 1, n % 8)
        if at not in PLAN or v + PLAN[at][2] >= OCTETS:
            return None
        return (v + PLAN[at][2], *PLAN[at][:2])

    def v_job_at(n):
        b, v = n // 16 + 1, n % 16 // 8
        return (b, v) if n % 8 == 5 and b < B and v < NV else None

    first_jobs = [(0, *job) for job in RAW + STACKS]
    early_jobs = [(1, *job) for job in RAW] + [planned(n) for n in (-2, -1) if planned(n)]
    order = {job: i for i, job in enumerate(first_jobs + early_jobs + [planned(n) for n in range(STEPS)
                                                                       if planned(n)])}

    def raw_of(v, kind):
        return v + 1 if SHARED else 2 * v + (1 if kind in ("k", "ks") else 2)

    k.push()
    psS = k.ps(f"{name}_psS", [P, 2, W])
    psT = k.ps(f"{name}_psT", [P, W])
    psM = k.ps(f"{name}_psM", [P, BANK])
    psC = k.ps(f"{name}_psC", [P, BANK])
    sel = k.sb(f"{name}_sel", [P, 16, P], F32R)
    Qst = k.sb(f"{name}_Qst", [P, 2, 4, S], F32R)
    if SHARED:
        Kst = k.sb(f"{name}_Kst", [P, 2, BANK], F32R)
    Kbd = k.sb(f"{name}_Kbd", [P, 2, 4, J, KEYS], F32R)
    Vpad = k.sb(f"{name}_Vpad", [P, 2, ST, CH, J, 32])
    NK = len(keyTs) * S
    full = k.sb(f"{name}_full", [P, NK + S])
    hi = k.sb(f"{name}_hi", [P, 2, NK + S], F32R)
    lo = k.sb(f"{name}_lo", [P, 2, NK + S], F32R)
    Sm = k.sb(f"{name}_Sm", [P, SM, W])
    PT = k.sb(f"{name}_PT", [P, 8, 8, S])
    nmax = k.sb(f"{name}_nmax", [P, SM, J])
    sums = k.sb(f"{name}_sums", [P, 2, 2, 4 * J])
    rec = k.sb(f"{name}_rec", [P, 2, 4 * J])
    recT = k.sb(f"{name}_recT", [4 * J, S])
    R = k.sb(f"{name}_R", [P, S])

    sel_in = k.sem(f"{name}_sel_in")
    sel_ready = k.sem(f"{name}_sel_ready")
    zeroed = k.sem(f"{name}_zeroed")
    v_zeroed = k.sem(f"{name}_v_zeroed")
    m_done = k.sem(f"{name}_m_done")
    m_free = k.sem(f"{name}_m_free")
    hi_ready = k.sem(f"{name}_hi_ready")
    parts_ready = k.sem(f"{name}_parts_ready")
    if SHARED:
        first_placed = k.sem(f"{name}_first_placed")
        placed = k.sem(f"{name}_placed")
    v_done = k.sem(f"{name}_v_done")
    v_ready = k.sem(f"{name}_v_ready")
    scored = k.sem(f"{name}_scored")
    maxed = k.sem(f"{name}_maxed")
    exped = k.sem(f"{name}_exped")
    turned = k.sem(f"{name}_turned")
    pt_first = k.sem(f"{name}_pt_first")
    pt_second = k.sem(f"{name}_pt_second")
    rec_ready = k.sem(f"{name}_rec_ready")
    rec_turned = k.sem(f"{name}_rec_turned")
    recT_ready = k.sem(f"{name}_recT_ready")
    rec_spread = k.sem(f"{name}_rec_spread")
    R_ready = k.sem(f"{name}_R_ready")
    pv_done = k.sem(f"{name}_pv_done")
    out_ready = k.sem(f"{name}_out_ready")

    def where(n):
        b, r = divmod(n, 16)
        c4, r = divmod(r, 8)
        qt, gg = divmod(r, 4)
        return b, c4, qt, gg

    def bank_of(job):
        M = order[job]
        if job[0] == 0:
            return psS[:, M // 2 % 2, M % 2 * BANK:(M % 2 + 1) * BANK], M - 3
        return psM[:, :], M

    def wait_placed(eng, stack):
        if stack < NKS:
            eng.wait_ge(first_placed, (stack + 1) * J)
        else:
            eng.wait_ge(placed, (stack + 1 - NKS) * J)

    def pt_slot(n):
        return n // 8 % 2 * 4 + n % 4, n // 8 - 1

    def place(eng, v, i, signal):
        for j in range(J):
            r = slice(j * RH, (j + 1) * RH)
            src = Kst[r, i % 2, :].bitcast(F32).rearrange("p (c s) -> p c s", c=KPJ)
            eng.tensor_copy(Kbd[r, v % 2, i * KPJ:(i + 1) * KPJ, j, :], src).then_inc(signal, 1)

    def steps():
        for n in range(STEPS + TAIL):
            u = n // 8 - 1
            yield n, u, n % 8, n < STEPS, u >= 0

    with nc.Block() as block:
        @block.sync
        def _(sp):
            sp.dma_start(Sm[:, 0:2].rearrange("p a w -> p (a w)"), sel_dram).then_inc(sel_in, 16)
            for b in range(B if mask_dram is not None else 0):
                if b >= 2:
                    sp.wait_ge(maxed, 16 * (b - 1))
                sp.dma_start(mask[:, b % 2], mask_dram[b * S:(b + 1) * S].rearrange("(n p) d -> p n d", p=P)
                             ).then_inc(mask_in[b % 2], 16)

        @block.tensor
        def _(pe):
            def job(v, kind, i):
                bank, before = bank_of((v, kind, i))
                slot, b, c4 = v % 2, v // 2, v % 2
                if before > 0:
                    pe.wait_ge(m_free, before)
                if kind in ("ks", "qs"):
                    pe.wait_ge(parts_ready, raw_of(v, kind))
                if kind in ("k", "kq"):
                    which = 0 if SHARED else c4
                    for s, keyT in enumerate(keyTs):
                        for c in range(KC):
                            ins = nc.tensor.matmul(bank[:, s * S:(s + 1) * S], wk[:, c, which * P:(which + 1) * P],
                                                   keyT[:, c, b * S:(b + 1) * S], start=(c == 0), stop=(c == KC - 1))
                if kind in ("q", "kq"):
                    o = S if SHARED else 0
                    for c in range(KC):
                        ins = nc.tensor.matmul(bank[:, o:o + S], wq[:, c, c4 * P:(c4 + 1) * P],
                                               queryT[:, c, b * S:(b + 1) * S], start=(c == 0), stop=(c == KC - 1))
                if kind == "qs":
                    for x in range(2):
                        nc.tensor.matmul(bank[:, x * S:(x + 1) * S], sel[:, 2 * i + x, :], hi[:, slot, NK:NK + S],
                                         start=True, stop=False)
                        ins = nc.tensor.matmul(bank[:, x * S:(x + 1) * S], sel[:, 4 + 2 * i + x, :],
                                               lo[:, slot, NK:NK + S], start=False, stop=True)
                if kind == "ks" and SHARED:
                    for x in range(2):
                        ins = nc.tensor.matmul(bank[:, x * S:(x + 1) * S], sel[:, 8 + 4 * c4 + 2 * i + x, :],
                                               hi[:, slot, 0:S], start=True, stop=True)
                if kind == "ks" and not SHARED:
                    nc.tensor.matmul(bank[:, :], sel[:, 8 + i, :], hi[:, slot, 0:NK], start=True, stop=False)
                    ins = nc.tensor.matmul(bank[:, :], sel[:, 12 + i, :], lo[:, slot, 0:NK], start=False, stop=True)
                ins.then_inc(m_done, 1)

            def v_job(b, v, u):
                if u >= 0:
                    pe.wait_ge(out_ready, u + 1)
                if b * NV + v > 0:
                    pe.wait_ge(v_ready, b * NV + v)
                for i in range(2):
                    t = 2 * v + i
                    src, tt = keyTs[v], 2 * b + i
                    for c in range(KC):
                        ins = nc.tensor.matmul(psC[:, i * VN:(i + 1) * VN], src[:, c, tt * P:(tt + 1) * P],
                                               wv[:, c, :], start=(c == 0), stop=(c == KC - 1))
                ins.then_inc(v_done, 1)

            def score(n):
                b, c4, qt, gg = where(n)
                v = n // 8
                if n % 8 == 0:
                    pe.wait_ge(m_free, order[v, "qs", 1] + 1)
                    if SHARED:
                        wait_placed(pe, (v + 1) * NKS - 1)
                if n >= 2:
                    pe.wait_ge(maxed, n - 1)
                for x in range(2):
                    kk = Kbd[:, v % 2, gg, :, :].rearrange("p j s -> p (j s)")
                    ins = nc.tensor.matmul(psS[:, n % 2, x * BANK:(x + 1) * BANK],
                                           Qst[:, v % 2, gg, qt * P:(qt + 1) * P],
                                           kk[:, x * BANK:(x + 1) * BANK], start=True, stop=True)
                ins.then_inc(scored, 1)

            for load in loads:
                pe.wait_ge(*load)
            for j in first_jobs:
                if j[1:] == STACKS[0]:
                    pe.wait_ge(sel_ready, 1)
                job(*j)
            pe.wait_ge(zeroed, 2)
            score(0)
            score(1)
            for j in early_jobs:
                job(*j)
            for v in range(NV):
                v_job(0, v, -1)
            for n, u, s, in_range, lags in steps():
                if n + 2 < STEPS:
                    score(n + 2)
                for half in range(2):
                    if in_range:
                        if half == 0:
                            pe.wait_ge(exped, n + 1)
                        if n >= 1:
                            pe.wait_ge(pt_second if half else pt_first, n)
                        for t in range(4 * half, 4 * half + 4):
                            ins = nc.tensor.transpose(psT[:, t * P:(t + 1) * P], Sm[:, n % SM, t * P:(t + 1) * P],
                                                      ident)
                        ins.then_inc(turned, 1)
                    if lags and s < 3:
                        b, c4 = u // 2, u % 2
                        if s == 0 and half == 0:
                            pe.wait_ge(pt_first, 8 * u + 8)
                            pe.wait_ge(pt_second, 8 * u + 8)
                            pe.wait_ge(v_ready, (b + 1) * NV)
                            if u >= 1:
                                pe.wait_ge(out_ready, u)
                        for t in PV_TILES[2 * s + half]:
                            for gg in range(4):
                                ins = nc.tensor.matmul(psC[32 * gg:32 * gg + 32, 0:S],
                                                       Vpad[:, b % 2, t % ST, 4 * c4 + gg, t // ST, :],
                                                       PT[:, 4 * c4 + gg, t, :],
                                                       start=(t == 0), stop=(t == 7), tile_position=(0, 32 * gg))
                        if s == 2 and half == 1:
                            ins.then_inc(pv_done, 1)
                if lags and s == 2:
                    pe.wait_ge(rec_ready, u + 1)
                    for qt in range(2):
                        ins = nc.tensor.transpose(psC[0:4 * J, S + qt * P:S + (qt + 1) * P], rec[:, qt, :], ident)
                    ins.then_inc(rec_turned, 1)
                if lags and s == 3:
                    pe.wait_ge(recT_ready, u + 1)
                    nc.tensor.matmul(psC[:, S:2 * S], expand, recT[:, :], start=True, stop=True).then_inc(rec_spread, 1)
                if planned(n):
                    job(*planned(n))
                if v_job_at(n):
                    v_job(*v_job_at(n), u)

        @block.scalar
        def _(act):
            def evacuate(v, kind, i):
                M = order[v, kind, i]
                bank = bank_of((v, kind, i))[0]
                act.wait_ge(m_done, M + 1)
                if kind in ("k", "q", "kq") and v >= 1:
                    act.wait_ge(parts_ready, raw_of(v - 1, kind))
                if i == 0 and v >= 2 and kind in ("ks", "qs"):
                    act.wait_ge(scored, 8 * (v - 1))
                if kind in ("k", "kq"):
                    which = 0 if SHARED else v % 2
                    ins = nc.scalar.activation(full[:, 0:NK], bank[:, 0:NK], ACT.Identity,
                                               bias=bk[:, which:which + 1])
                if kind in ("q", "kq"):
                    o = S if SHARED else 0
                    ins = nc.scalar.activation(full[:, NK:NK + S], bank[:, o:o + S], ACT.Identity,
                                               bias=bq[:, v % 2:v % 2 + 1], scale=scale)
                if kind == "ks" and not SHARED:
                    if i == 0 and v < 2:
                        act.wait_ge(zeroed, v + 1)
                    for j in range(J):
                        ins = nc.scalar.copy(Kbd[j * RH:(j + 1) * RH, v % 2, i, j, :], bank[j * RH:(j + 1) * RH, :])
                if kind == "ks" and SHARED:
                    stack = v * NKS + i
                    if stack >= 2:
                        wait_placed(act, stack - 2)
                    ins = nc.scalar.copy(Kst[:, i % 2, :], bank[:, :])
                if kind == "qs":
                    ins = nc.scalar.copy(Qst[:, v % 2, 2 * i:2 * i + 2, :].rearrange("p c s -> p (c s)"), bank[:, :])
                ins.then_inc(m_free, 1)

            act.wait_ge(sel_in, 16)
            nc.scalar.copy(sel[:, :].rearrange("p a q -> p (a q)"), Sm[:, 0:2].rearrange("p a w -> p (a w)")
                           ).then_inc(sel_ready, 1)
            for j in first_jobs + early_jobs:
                evacuate(*j)
            for n, u, s, in_range, lags in steps():
                if in_range:
                    b, c4, qt, gg = where(n)
                    act.wait_ge(maxed, n + 1)
                    if n >= 16 and s == 0:
                        act.wait_ge(rec_ready, u)
                    for j in range(J):
                        ins = nc.scalar.activation(Sm[:, n % SM, j * KEYS:(j + 1) * KEYS],
                                                   Sm[:, n % SM, j * KEYS:(j + 1) * KEYS], ACT.Exp,
                                                   bias=nmax[:, n % SM, j:j + 1], scale=-1.0,
                                                   accum_out=sums[:, (n // 8) % 2, qt, gg * J + j:gg * J + j + 1])
                    ins.then_inc(exped, 1)
                if lags and s == 3:
                    act.wait_ge(rec_turned, u + 1)
                    nc.scalar.copy(recT[:, :], psC[0:4 * J, S:2 * S]).then_inc(recT_ready, 1)
                if lags and s == 4:
                    act.wait_ge(rec_spread, u + 1)
                    nc.scalar.copy(R[:, :], psC[:, S:2 * S]).then_inc(R_ready, 1)
                if 1 <= n <= STEPS and act_copies(n - 1):
                    t = n - 1
                    slot, octets = pt_slot(t)
                    act.wait_ge(turned, 2 * t + 1)
                    if octets > 0:
                        act.wait_ge(pv_done, octets)
                    qt = (t // 4) % 2
                    nc.scalar.copy(PT[:, slot, 0:4, qt * P:(qt + 1) * P],
                                   psT[:, 0:BANK].rearrange("p (t q) -> p t q", t=4)).then_inc(pt_first, 1)
                if n >= 1 and planned(n - 1):
                    evacuate(*planned(n - 1))

        @block.vector
        def _(dve):
            def parts(v, kind, i):
                a, z = {"k": (0, NK), "q": (NK, NK + S), "kq": (0, NK + S)}[kind]
                slot, raw = v % 2, raw_of(v, kind)
                dve.wait_ge(m_free, order[v, kind, i] + 1)
                if v >= 2:
                    dve.wait_ge(m_done, order[v - 2, "qs", 1] + 1)
                nc.vector.tensor_copy(hi[:, slot, a:z], full[:, a:z]).then_inc(hi_ready, 1)
                dve.wait_ge(hi_ready, raw)
                if SHARED:
                    nc.vector.tensor_tensor(hi[64:128, slot, 0:NK], full[64:128, 0:NK],
                                            hi[64:128, slot, 0:NK].bitcast(F32), ALU.subtract)
                    a = NK
                nc.vector.tensor_tensor(lo[:, slot, a:z], full[:, a:z], hi[:, slot, a:z].bitcast(F32),
                                        ALU.subtract).then_inc(parts_ready, 1)

            def v_out(b, v):
                dve.wait_ge(v_done, b * NV + v + 1)
                if b == 0 and v == 0:
                    dve.wait_ge(v_zeroed, 1)
                if b >= 2:
                    dve.wait_ge(pv_done, 2 * (b - 1))
                src = psC[:, 0:2 * VN].rearrange("p (t g d) -> p t g d", t=2, d=FD)
                row = bv_row.rearrange("p (g d) -> p g d", d=FD)
                for j in range(J):
                    for t in range(2):
                        a, r = (src[:, t], row) if SHARED else (src[:, t, j::J], row[:, j::J])
                        ins = nc.vector.tensor_tensor(Vpad[:, b % 2, 2 * v + t, :, j, FD * j:FD * (j + 1)], a, r, ALU.add)
                        if j == J - 1 and t == 1:
                            ins.then_inc(v_ready, 1)

            nc.vector.memset(Kbd[:, 0].rearrange("p c j s -> p (c j s)").bitcast(F32), 0.0).then_inc(zeroed, 1)
            for v, kind, i in first_jobs + early_jobs:
                if (kind, i) in RAW:
                    parts(v, kind, i)
                elif kind == "ks" and SHARED and v == 0:
                    dve.wait_ge(m_free, order[v, kind, i] + 1)
                    dve.wait_ge(zeroed, 1)
                    place(nc.vector, v, i, first_placed)
            for v in range(NV):
                v_out(0, v)
            dve.wait_ge(sel_ready, 1)
            for n, u, s, in_range, lags in steps():
                if in_range:
                    b, c4, qt, gg = where(n)
                    if mask_dram is not None and n % 16 == 0:
                        dve.wait_ge(mask_in[b % 2], 16 * (b // 2 + 1))
                    dve.wait_ge(scored, n + 1)
                    if n >= SM:
                        dve.wait_ge(turned, 2 * (n - SM + 1))
                    for j in range(J):
                        ins = nc.vector.tensor_tensor_reduce(Sm[:, n % SM, j * KEYS:(j + 1) * KEYS],
                                                             psS[:, n % 2, j * KEYS:(j + 1) * KEYS], mask_of(b, qt),
                                                             -1.0, 3.4e38, ALU.add, ALU.min,
                                                             nmax[:, n % SM, j:j + 1])
                    ins.then_inc(maxed, 1)
                if 2 <= n <= STEPS + 1:
                    t = n - 2
                    slot, octets = pt_slot(t)
                    if octets > 0:
                        dve.wait_ge(pv_done, octets)
                    qt = (t // 4) % 2
                    for half in range(act_copies(t), 2):
                        dve.wait_ge(turned, 2 * t + half + 1)
                        nc.vector.tensor_copy(PT[:, slot, 4 * half:4 * half + 4, qt * P:(qt + 1) * P],
                                              psT[:, half * BANK:(half + 1) * BANK].rearrange("p (t q) -> p t q", t=4)
                                              ).then_inc(pt_second if half else pt_first, 1)
                if n >= 3 and v_job_at(n - 3):
                    v_out(*v_job_at(n - 3))
                if n >= 3 and planned(n - 3) and planned(n - 3)[1:] in RAW:
                    parts(*planned(n - 3))
                if lags and s == 0:
                    dve.wait_ge(exped, 8 * u + 8)
                    if u >= 1:
                        dve.wait_ge(rec_turned, u)
                    nc.vector.reciprocal(rec[:, :, :], sums[:, u % 2, :, :]).then_inc(rec_ready, 1)
                if lags and s == 5:
                    b, c4 = u // 2, u % 2
                    dve.wait_ge(pv_done, u + 1)
                    dve.wait_ge(R_ready, u + 1)
                    nc.vector.tensor_tensor(attnT[:, c4, b * S:(b + 1) * S], psC[:, 0:S], R[:, :], ALU.mult
                                            ).then_inc(out_ready, 1)

        @block.gpsimd
        def _(pool):
            pool.wait_ge(zeroed, 1)
            nc.gpsimd.memset(Kbd[:, 1].rearrange("p c j s -> p (c j s)").bitcast(F32), 0.0
                             ).then_inc(zeroed, 1)
            nc.gpsimd.memset(Vpad[:, :].rearrange("p w a b c d -> p (w a b c d)"), 0.0).then_inc(v_zeroed, 1)
            for v in range(1, OCTETS if SHARED else 1):
                for i in range(NKS):
                    if v == 1 and i == 0:
                        pool.wait_ge(zeroed, 2)
                        pool.wait_ge(v_zeroed, 1)
                    pool.wait_ge(m_free, order[v, "ks", i] + 1)
                    if v >= 2 and i == 0:
                        pool.wait_ge(scored, 8 * (v - 1))
                    place(nc.gpsimd, v, i, placed)
    k.pop()


def out_projection(k, name, inT, nch, w, X, residual, row, load=None):
    nc = k.nc
    k.push()
    ps = k.ps(f"{name}_ps", [P, NT, BANK])
    addend = k.sb(f"{name}_addend", [P, NT, D])
    done = k.sem(f"{name}_done")
    added = k.sem(f"{name}_added")
    with nc.Block() as block:
        @block.tensor
        def _(pe):
            for t in range(NT):
                for c in range(nch):
                    ins = nc.tensor.matmul(ps[:, t, 0:D], inT[:, c, t * P:(t + 1) * P], w[:, c, :],
                                           start=(c == 0), stop=(c == nch - 1))
                ins.then_inc(done, 1)

        @block.vector
        def _(dve):
            if load is not None:
                dve.wait_ge(*load)
            nc.vector.tensor_tensor(addend[:, :, :], residual[:, :, :], row.unsqueeze(1).broadcast_to([P, NT, D]),
                                    ALU.add).then_inc(added, 1)
            dve.wait_ge(added, 1)
            for t in range(NT):
                dve.wait_ge(done, t + 1)
                ins = nc.vector.tensor_tensor(X[:, t, :], ps[:, t, 0:D], addend[:, t, :], ALU.add)
            ins.then_inc(added, 1)
    k.pop()


def hidden_layer(k, name, hT, w1, b1, gT, func, nf):
    nc = k.nc
    k.push()
    ps = k.ps(f"{name}_ps", [P, 8, BANK])
    done = k.sem(f"{name}_done")
    read = k.sem(f"{name}_read")
    with nc.Block() as block:
        @block.tensor
        def _(pe):
            for n in range(2 * nf):
                f, half = n // 2, n % 2
                if n >= 8:
                    pe.wait_ge(read, n - 7)
                for c in range(KC):
                    ins = nc.tensor.matmul(ps[:, n % 8, :], w1[:, c, f * P:(f + 1) * P],
                                           hT[:, c, half * BANK:(half + 1) * BANK],
                                           start=(c == 0), stop=(c == KC - 1))
                ins.then_inc(done, 1)

        @block.scalar
        def _(act):
            for n in range(2 * nf):
                f, half = n // 2, n % 2
                act.wait_ge(done, n + 1)
                nc.scalar.activation(gT[:, f, half * BANK:(half + 1) * BANK], ps[:, n % 8, :], func,
                                     bias=b1[:, f:f + 1]).then_inc(read, 1)
    k.pop()


def wide_head_attention(k, name, hT, cT, w_dram, wo_dram, X, ident, bq, bk, bias_k, bias_v, vrow, bo_row):
    nc = k.nc
    H = 16
    SCALE = 128 ** -0.5
    KS = S + 1
    NU = 4 * H
    k.push()
    psS = k.ps(f"{name}_psS", [P, 2, 2, BANK])
    psT = k.ps(f"{name}_psT", [P, 2, S])
    psC = k.ps(f"{name}_psC", [P, BANK])
    psP = k.ps(f"{name}_psP", [P, 2, BANK])
    wqkv = k.sb(f"{name}_w", [P, 2, KC, 3 * P])
    wo = k.sb(f"{name}_wo", [P, H, D])
    qT = k.sb(f"{name}_qT", [P, 2, TOK])
    kT = k.sb(f"{name}_kT", [P, 2, B, KS + 1])
    v = k.sb(f"{name}_v", [P, 2, NT, P])
    Pr = k.sb(f"{name}_Pr", [P, 2, 2, KS + 1])
    PT = k.sb(f"{name}_PT", [P, 2, 2, S])
    ctxT = k.sb(f"{name}_ctxT", [P, H, TOK])
    nmax = k.sb(f"{name}_nmax", [P, 2, 2])
    sums = k.sb(f"{name}_sums", [P, 2, 2])
    rec = k.sb(f"{name}_rec", [P, 2, 2])
    XB = k.sb(f"{name}_XB", [P, NT, D])

    w_in = [k.sem(f"{name}_w_in{i}") for i in range(2)]
    wo_in = k.sem(f"{name}_wo_in")
    proj_done = k.sem(f"{name}_proj_done")
    qk_ready = k.sem(f"{name}_qk_ready")
    v_ready = k.sem(f"{name}_v_ready")
    extra_key = k.sem(f"{name}_extra_key")
    xb_ready = k.sem(f"{name}_xb_ready")
    scored = k.sem(f"{name}_scored")
    maxed = k.sem(f"{name}_maxed")
    exped = k.sem(f"{name}_exped")
    rec_ready = k.sem(f"{name}_rec_ready")
    normed = k.sem(f"{name}_normed")
    turned = k.sem(f"{name}_turned")
    pt_ready = k.sem(f"{name}_pt_ready")
    pv_done = k.sem(f"{name}_pv_done")
    ctx_ready = k.sem(f"{name}_ctx_ready")
    o_done = k.sem(f"{name}_o_done")
    added = k.sem(f"{name}_added")

    JOBS = [("k", 0), ("q", 0), ("v", 0), ("k", 1), ("q", 1), ("v", 1)]
    AT = {0: (0, 1), 1: (2, 3), 2: (4, None), 3: (None, 5)}
    QK_COUNT = [1, 2, 2, 3, 4, 4]
    V_COUNT = [0, 0, 1, 1, 1, 2]

    with nc.Block() as block:
        @block.sync
        def _(sp):
            for h in range(H):
                if h >= 2:
                    sp.wait_ge(proj_done, 6 * (h - 1))
                sp.dma_start(wqkv[:, h % 2].rearrange("p c n -> p (c n)"), w_dram[h]).then_inc(w_in[h % 2], 16)
                if h == 1:
                    sp.dma_start(wo[:, :].rearrange("p h n -> p (h n)"), wo_dram).then_inc(wo_in, 16)

        @block.gpsimd
        def _(pool):
            for h in range(2):
                nc.gpsimd.tensor_copy(kT[:, h % 2, :, S:KS], bias_k[:, h:h + 1].unsqueeze(2).broadcast_to([P, B, 1])
                                      ).then_inc(extra_key, 1)
            nc.gpsimd.tensor_tensor(XB[:, :].rearrange("p t d -> p (t d)"), X[:, :].rearrange("p t d -> p (t d)"),
                                    bo_row.unsqueeze(1).broadcast_to([P, NT, D]), ALU.add).then_inc(xb_ready, 1)
            for h in range(2, H):
                pool.wait_ge(scored, 4 * (h - 1))
                nc.gpsimd.tensor_copy(kT[:, h % 2, :, S:KS], bias_k[:, h:h + 1].unsqueeze(2).broadcast_to([P, B, 1])
                                      ).then_inc(extra_key, 1)

        @block.tensor
        def _(pe):
            def project(h, m):
                n = 6 * h + m
                kind, half = JOBS[m]
                if m == 0:
                    pe.wait_ge(w_in[h % 2], 16 * (h // 2 + 1))
                if n >= 2:
                    hh, mm = divmod(n - 2, 6)
                    if JOBS[mm][0] == "v":
                        pe.wait_ge(v_ready, 2 * hh + V_COUNT[mm])
                    else:
                        pe.wait_ge(qk_ready, 4 * hh + QK_COUNT[mm])
                o = {"q": 0, "k": P, "v": 2 * P}[kind]
                if kind == "v":
                    for t in range(4):
                        for c in range(KC):
                            ins = nc.tensor.matmul(psP[:, n % 2, t * P:(t + 1) * P],
                                                   cT[:, c, (4 * half + t) * P:(4 * half + t + 1) * P],
                                                   wqkv[:, h % 2, c, o:o + P], start=(c == 0), stop=(c == KC - 1))
                else:
                    src = hT if kind == "q" else cT
                    for c in range(KC):
                        ins = nc.tensor.matmul(psP[:, n % 2, :], wqkv[:, h % 2, c, o:o + P],
                                               src[:, c, half * BANK:(half + 1) * BANK],
                                               start=(c == 0), stop=(c == KC - 1))
                ins.then_inc(proj_done, 1)

            def score(u):
                h, b = divmod(u, 4)
                pe.wait_ge(qk_ready, 4 * h + (2 if b < 2 else 4))
                if b == 0:
                    pe.wait_ge(extra_key, h + 1)
                if u >= 2:
                    pe.wait_ge(exped, u - 1)
                for qt in range(2):
                    o = b * S + qt * P
                    ins = nc.tensor.matmul(psS[:, u % 2, qt, 0:KS], qT[:, h % 2, o:o + P], kT[:, h % 2, b, 0:KS],
                                           start=True, stop=True)
                ins.then_inc(scored, 1)

            for m in range(6):
                project(0, m)
            score(0)
            for u in range(NU):
                h, b = divmod(u, 4)
                before, after = AT[b]
                if h + 1 < H and before is not None:
                    project(h + 1, before)
                if u + 1 < NU:
                    score(u + 1)
                pe.wait_ge(normed, u + 1)
                if u >= 1:
                    pe.wait_ge(pt_ready, u)
                for qt in range(2):
                    for st in range(2):
                        ins = nc.tensor.transpose(psT[:, st, qt * P:(qt + 1) * P],
                                                  Pr[:, u % 2, qt, st * P:(st + 1) * P], ident)
                ins.then_inc(turned, 1)
                if h + 1 < H and after is not None:
                    project(h + 1, after)
                pe.wait_ge(pt_ready, u + 1)
                pe.wait_ge(v_ready, 2 * h + (1 if b < 2 else 2))
                if b % 2 == 0 and u >= 2:
                    pe.wait_ge(ctx_ready, u // 2)
                for st in range(2):
                    ins = nc.tensor.matmul(psC[:, (b % 2) * S:(b % 2 + 1) * S], v[:, h % 2, 2 * b + st, :],
                                           PT[:, u % 2, st, :], start=(st == 0), stop=(st == 1))
                ins.then_inc(pv_done, 1)
            pe.wait_ge(wo_in, 16)
            pe.wait_ge(ctx_ready, NU // 2)
            for t in range(NT):
                if t >= 2:
                    pe.wait_ge(added, t - 1)
                for h in range(H):
                    ins = nc.tensor.matmul(psP[:, t % 2, 0:D], ctxT[:, h, t * P:(t + 1) * P], wo[:, h, :],
                                           start=(h == 0), stop=(h == H - 1))
                ins.then_inc(o_done, 1)

        def copy_ctx(act, pair):
            h, half = divmod(pair, 2)
            act.wait_ge(pv_done, 2 * pair + 2)
            nc.scalar.activation(ctxT[:, h, half * BANK:(half + 1) * BANK], psC[:, :], ACT.Identity,
                                 bias=bias_v[:, h:h + 1]).then_inc(ctx_ready, 1)

        @block.scalar
        def _(act):
            def evacuate(h, m):
                kind, half = JOBS[m]
                if kind == "v":
                    return
                act.wait_ge(proj_done, 6 * h + m + 1)
                if h >= 2:
                    act.wait_ge(scored, 4 * (h - 1))
                if kind == "q":
                    ins = nc.scalar.activation(qT[:, h % 2, half * BANK:(half + 1) * BANK],
                                               psP[:, (6 * h + m) % 2, :], ACT.Identity, bias=bq[:, h:h + 1],
                                               scale=SCALE)
                else:
                    ins = nc.scalar.activation(kT[:, h % 2, 2 * half:2 * half + 2, 0:S],
                                               psP[:, (6 * h + m) % 2, :].rearrange("p (b s) -> p b s", b=2),
                                               ACT.Identity, bias=bk[:, h:h + 1])
                ins.then_inc(qk_ready, 1)

            for m in range(6):
                evacuate(0, m)
            for u in range(NU):
                h, b = divmod(u, 4)
                before, after = AT[b]
                act.wait_ge(maxed, u + 1)
                if u >= 2:
                    act.wait_ge(turned, u - 1)
                for qt in range(2):
                    ins = nc.scalar.activation(Pr[:, u % 2, qt, 0:KS], psS[:, u % 2, qt, 0:KS], ACT.Exp,
                                               bias=nmax[:, u % 2, qt:qt + 1], accum_out=sums[:, u % 2, qt:qt + 1])
                ins.then_inc(exped, 1)
                if u >= 1 and (u - 1) % 2 == 1:
                    pair = (u - 1) // 2
                    copy_ctx(act, pair)
                if h + 1 < H and before is not None:
                    evacuate(h + 1, before)
                act.wait_ge(turned, u + 1)
                if u >= 2:
                    act.wait_ge(pv_done, u - 1)
                nc.scalar.copy(PT[:, u % 2], psT[:, :]).then_inc(pt_ready, 1)
                if h + 1 < H and after is not None:
                    evacuate(h + 1, after)
            copy_ctx(act, NU // 2 - 1)

        @block.vector
        def _(dve):
            def evacuate(h, m):
                kind, half = JOBS[m]
                if kind != "v":
                    return
                dve.wait_ge(proj_done, 6 * h + m + 1)
                if h >= 2:
                    dve.wait_ge(pv_done, 4 * (h - 1))
                row = vrow[:, h * P:(h + 1) * P].unsqueeze(1).broadcast_to([P, 4, P])
                nc.vector.tensor_tensor(v[:, h % 2, 4 * half:4 * half + 4, :],
                                        psP[:, (6 * h + m) % 2, :].rearrange("p (t n) -> p t n", t=4), row,
                                        ALU.add).then_inc(v_ready, 1)

            def top(u):
                dve.wait_ge(scored, u + 1)
                if u >= 2:
                    dve.wait_ge(exped, u - 1)
                nc.vector.tensor_reduce(nmax[:, u % 2], psS[:, u % 2, :, 0:KS], AXX, ALU.max,
                                        negate=True).then_inc(maxed, 1)

            for m in range(6):
                evacuate(0, m)
            top(0)
            for u in range(NU):
                h, b = divmod(u, 4)
                before, after = AT[b]
                dve.wait_ge(exped, u + 1)
                if u >= 1:
                    dve.wait_ge(normed, u)
                nc.vector.reciprocal(rec[:, u % 2], sums[:, u % 2]).then_inc(rec_ready, 1)
                dve.wait_ge(rec_ready, u + 1)
                for qt in range(2):
                    ins = nc.vector.tensor_scalar(Pr[:, u % 2, qt, 0:S], Pr[:, u % 2, qt, 0:S],
                                                  rec[:, u % 2, qt:qt + 1], None, ALU.mult)
                ins.then_inc(normed, 1)
                if h + 1 < H and before is not None:
                    evacuate(h + 1, before)
                if u + 1 < NU:
                    top(u + 1)
                if h + 1 < H and after is not None:
                    evacuate(h + 1, after)
            dve.wait_ge(xb_ready, 1)
            for t in range(NT):
                dve.wait_ge(o_done, t + 1)
                nc.vector.tensor_tensor(X[:, t, :], psP[:, t % 2, 0:D], XB[:, t, :], ALU.add).then_inc(added, 1)
    k.pop()


def norm_rows(k, name, X, eps, gamma, beta):
    nc = k.nc
    k.push()
    stats = k.sb(f"{name}_stats", [P, NT, 6])
    mv = k.sb(f"{name}_mv", [P, NT, 2])
    ve = k.sb(f"{name}_ve", [P, NT])
    sd = k.sb(f"{name}_sd", [P, NT])
    rstd = k.sb(f"{name}_rstd", [P, NT])
    small = k.sem(f"{name}_small")
    var_ready = k.sem(f"{name}_var_ready")
    sd_ready = k.sem(f"{name}_sd_ready")
    with nc.Block() as block:
        @block.vector
        def _(dve):
            done = [0]

            def link(ins):
                done[0] += 1
                ins.then_inc(small, 1)
                dve.wait_ge(small, done[0])

            for t in range(NT):
                ins = nc.vector.bn_stats(stats[:, t, :], X[:, t, :])
            link(ins)
            for t in range(NT):
                ins = nc.vector.bn_aggr(mv[:, t, :], stats[:, t, :])
            link(ins)
            nc.vector.tensor_scalar(ve[:, :], mv[:, :, 1], eps, None, ALU.add).then_inc(var_ready, 1)
            dve.wait_ge(sd_ready, 1)
            link(nc.vector.reciprocal(rstd[:, :], sd[:, :]))
            for t in range(NT):
                ins = nc.vector.tensor_scalar(X[:, t, :], X[:, t, :], mv[:, t, 0:1], rstd[:, t:t + 1],
                                              ALU.subtract, ALU.mult)
            link(ins)
            link(nc.vector.tensor_tensor(X[:, :, :], X[:, :, :], gamma.unsqueeze(1).broadcast_to([P, NT, D]), ALU.mult))
            link(nc.vector.tensor_tensor(X[:, :, :], X[:, :, :], beta.unsqueeze(1).broadcast_to([P, NT, D]), ALU.add))

        @block.scalar
        def _(act):
            act.wait_ge(var_ready, 1)
            nc.scalar.activation(sd[:, :], ve[:, :], ACT.Sqrt).then_inc(sd_ready, 1)
    k.pop()


def single_head_attention(k, name, xT, cT, X, w, w_in, alpha, ident):
    nc = k.nc
    SCALE = D ** -0.5
    k.push()
    qT = k.sb(f"{name}_qT", [P, KC, TOK])
    kT = k.sb(f"{name}_kT", [P, KC, TOK])
    v = k.sb(f"{name}_v", [P, NT, D])
    k.push()
    ps = k.ps(f"{name}_ps", [P, 8, BANK])
    proj_done = k.sem(f"{name}_proj_done")
    by_act = k.sem(f"{name}_by_act")
    by_dve = k.sem(f"{name}_by_dve")
    NJ = 12
    with nc.Block() as block:
        @block.tensor
        def _(pe):
            pe.wait_ge(w_in, 16)
            for n in range(NJ):
                if n >= 8:
                    pe.wait_ge(by_dve if n % 2 else by_act, (n - 8) // 2 + 1)
                if n < 8:
                    a, oc, half = n // 4, n // 2 % 2, n % 2
                    for c in range(KC):
                        ins = nc.tensor.matmul(ps[:, n % 8, :], w[:, c, a, oc * P:(oc + 1) * P],
                                               (xT, cT)[a][:, c, half * BANK:(half + 1) * BANK],
                                               start=(c == 0), stop=(c == KC - 1))
                else:
                    for i in range(2):
                        t = 2 * (n - 8) + i
                        for c in range(KC):
                            ins = nc.tensor.matmul(ps[:, n % 8, i * D:(i + 1) * D], cT[:, c, t * P:(t + 1) * P],
                                                   w[:, c, 2, :], start=(c == 0), stop=(c == KC - 1))
                ins.then_inc(proj_done, 1)

        def target(n):
            if n < 8:
                a, oc, half = n // 4, n // 2 % 2, n % 2
                return (qT, kT)[a][:, oc, half * BANK:(half + 1) * BANK]
            return v[:, 2 * (n - 8):2 * (n - 8) + 2, :].rearrange("p t d -> p (t d)")

        @block.scalar
        def _(act):
            for n in range(0, NJ, 2):
                act.wait_ge(proj_done, n + 1)
                nc.scalar.activation(target(n), ps[:, n % 8, :], ACT.Copy, scale=SCALE if n < 4 else 1.0
                                     ).then_inc(by_act, 1)

        @block.vector
        def _(dve):
            for n in range(1, NJ, 2):
                dve.wait_ge(proj_done, n + 1)
                nc.vector.tensor_scalar(target(n), ps[:, n % 8, :], SCALE if n < 4 else 1.0, None, ALU.mult
                                        ).then_inc(by_dve, 1)
    k.pop()

    psS = k.ps(f"{name}_psS", [P, 2, BANK])
    psT = k.ps(f"{name}_psT", [P, 2, S])
    psX = k.ps(f"{name}_psX", [P, KC, S])
    psD = k.ps(f"{name}_psD", [P, 2, BANK])
    Pr = k.sb(f"{name}_Pr", [P, 2, S])
    PT = k.sb(f"{name}_PT", [P, 2, 2, S])
    cxT = k.sb(f"{name}_cxT", [P, KC, S])
    nmax = k.sb(f"{name}_nmax", [P, 2])
    sums = k.sb(f"{name}_sums", [P, 2])
    rec = k.sb(f"{name}_rec", [P, 2])
    scored = k.sem(f"{name}_scored")
    maxed = k.sem(f"{name}_maxed")
    exped = k.sem(f"{name}_exped")
    rec_ready = k.sem(f"{name}_rec_ready")
    normed = k.sem(f"{name}_normed")
    turned = k.sem(f"{name}_turned")
    pt_ready = k.sem(f"{name}_pt_ready")
    x_done = k.sem(f"{name}_x_done")
    cx_ready = k.sem(f"{name}_cx_ready")
    d_done = k.sem(f"{name}_d_done")
    added = k.sem(f"{name}_added")
    with nc.Block() as block:
        @block.tensor
        def _(pe):
            def score(n):
                if n >= 2:
                    pe.wait_ge(exped, n - 1)
                for c in range(KC):
                    ins = nc.tensor.matmul(psS[:, n % 2, 0:S], qT[:, c, n * P:(n + 1) * P],
                                           kT[:, c, (n // 2) * S:(n // 2 + 1) * S],
                                           start=(c == 0), stop=(c == KC - 1))
                ins.then_inc(scored, 1)

            score(0)
            for n in range(NT):
                if n + 1 < NT:
                    score(n + 1)
                pe.wait_ge(normed, n + 1)
                if n >= 1:
                    pe.wait_ge(pt_ready, n)
                qt, b = n % 2, n // 2
                for st in range(2):
                    ins = nc.tensor.transpose(psT[:, st, qt * P:(qt + 1) * P], Pr[:, n % 2, st * P:(st + 1) * P],
                                              ident)
                ins.then_inc(turned, 1)
                if qt == 0:
                    continue
                pe.wait_ge(pt_ready, n + 1)
                if b >= 1:
                    pe.wait_ge(cx_ready, b)
                for fc in range(KC):
                    for st in range(2):
                        ins = nc.tensor.matmul(psX[:, fc, :], v[:, 2 * b + st, fc * P:(fc + 1) * P],
                                               PT[:, b % 2, st, :], start=(st == 0), stop=(st == 1))
                ins.then_inc(x_done, 1)
                pe.wait_ge(cx_ready, b + 1)
                for i in range(2):
                    t = 2 * b + i
                    if t >= 2:
                        pe.wait_ge(added, t - 1)
                    for c in range(KC):
                        ins = nc.tensor.matmul(psD[:, t % 2, 0:D], cxT[:, c, i * P:(i + 1) * P], w[:, c, 3, :],
                                               start=(c == 0), stop=(c == KC - 1))
                    ins.then_inc(d_done, 1)

        @block.scalar
        def _(act):
            for n in range(NT):
                act.wait_ge(maxed, n + 1)
                if n >= 2:
                    act.wait_ge(turned, n - 1)
                nc.scalar.activation(Pr[:, n % 2, :], psS[:, n % 2, 0:S], ACT.Exp, bias=nmax[:, n % 2:n % 2 + 1],
                                     accum_out=sums[:, n % 2:n % 2 + 1]).then_inc(exped, 1)
                qt, b = n % 2, n // 2
                act.wait_ge(turned, n + 1)
                if b >= 2 and qt == 0:
                    act.wait_ge(x_done, b - 1)
                nc.scalar.copy(PT[:, b % 2, :, qt * P:(qt + 1) * P], psT[:, :, qt * P:(qt + 1) * P]
                               ).then_inc(pt_ready, 1)
                if qt == 1:
                    act.wait_ge(x_done, b + 1)
                    if b >= 1:
                        act.wait_ge(d_done, 2 * b)
                    nc.scalar.copy(cxT[:, :, :], psX[:, :, :]).then_inc(cx_ready, 1)

        def add(dve, t):
            dve.wait_ge(d_done, t + 1)
            nc.vector.scalar_tensor_tensor(out=X[:, t, :], in0=psD[:, t % 2, 0:D], scalar=alpha, in1=X[:, t, :],
                                           op0=ALU.mult, op1=ALU.add).then_inc(added, 1)

        @block.vector
        def _(dve):
            for n in range(NT):
                dve.wait_ge(scored, n + 1)
                if n >= 2:
                    dve.wait_ge(exped, n - 1)
                nc.vector.tensor_reduce(nmax[:, n % 2:n % 2 + 1], psS[:, n % 2, 0:S], AXX, ALU.max,
                                        negate=True).then_inc(maxed, 1)
                dve.wait_ge(exped, n + 1)
                if n >= 1:
                    dve.wait_ge(normed, n)
                nc.vector.reciprocal(rec[:, n % 2:n % 2 + 1], sums[:, n % 2:n % 2 + 1]).then_inc(rec_ready, 1)
                dve.wait_ge(rec_ready, n + 1)
                nc.vector.tensor_scalar(Pr[:, n % 2, :], Pr[:, n % 2, :], rec[:, n % 2:n % 2 + 1], None,
                                        ALU.mult).then_inc(normed, 1)
                if n >= 2 and n % 2 == 0:
                    add(dve, n - 2)
                    add(dve, n - 1)
            add(dve, NT - 2)
            add(dve, NT - 1)

    k.pop()


COLS = ["g_bq", "g_bk", "l_bq", "l_bk",
        "ln1_scale", "ln1_offset", "bq1", "bk1", "bias_k1", "bias_v1",
        "ln2_scale", "ln2_offset", "bq2", "bk2", "bias_k2", "bias_v2",
        "ln_mlp_scale", "ln_mlp_offset", "b_fc1", "alpha", "postnorm_w", "mlp_b1"]
ROWS = ["g_bv", "g_bo", "gamma", "beta", "bo1", "bo2", "b_fc2", "l_bv", "l_bo", "mlp_b2"]


def cross_attention_stack(nc, a, at_col, at_row, out):
    with ExitStack() as outer:
        k = Core(nc, outer)
        X = k.sb("X", [P, NT, D])
        xT = k.sb("xT", [P, KC, TOK])
        cT = k.sb("cT", [P, KC, TOK])
        NCOL, NROW = a["cols"].shape[1], a["rows"].shape[1]
        cols = k.sb("cols", [P, NCOL])
        rows = k.sb("rows", [P, NROW])
        consts = k.sb("consts", [P, 3 * P])
        ident = consts[:, 0:P]
        expand_g = consts[0:16, P:2 * P]
        expand_l = consts[0:8, 2 * P:3 * P]

        def col(name, dt=None):
            o, w = at_col[name]
            return cols[:, o:o + w]

        def row(name):
            o, w = at_row[name]
            return rows[:, o:o + w]

        act_in = k.sem("activations_in")
        vec_in = k.sem("vectors_in")
        x_in = k.sem("x_in")
        g_in = k.sem("g_weights_in")
        mask_in = [k.sem(f"mask_in{i}") for i in range(2)]
        prep = k.sem("vectors_prepared")

        k.push()
        g_wo = k.sb("g_wo", [P, KC, D])
        k.push()
        g_w = k.sb("g_w", [P, KC, D + P + 64])
        mask = k.sb("mask", [P, 2, 2, S])
        with nc.Block() as block:
            @block.sync
            def _(sp):
                sp.dma_start(xT[:, :].rearrange("p c t -> p (c t)"), a["xT"]).then_inc(act_in, 16)
                sp.dma_start(cT[:, :].rearrange("p c t -> p (c t)"), a["cT"]).then_inc(act_in, 16)
                sp.dma_start(X[:, :], a["x"].rearrange("(n p) d -> p n d", p=P)).then_inc(x_in, 16)

            @block.scalar
            def _(act):
                act.dma_start(cols[:, :], a["cols"]).then_inc(vec_in, 16)
                act.dma_start(rows[:, :], a["rows"].broadcast_to([P, NROW])).then_inc(vec_in, 16)
                act.dma_start(consts[:, :], a["consts"]).then_inc(vec_in, 16)
                act.dma_start(g_w[:, :].rearrange("p c n -> p (c n)"), a["g_w"]).then_inc(g_in, 16)
                act.dma_start(g_wo[:, :].rearrange("p c n -> p (c n)"), a["g_wo"]).then_inc(g_in, 16)

            @block.vector
            def _(dve):
                dve.wait_ge(vec_in, 48)
                for name, scale in (("g_bq", 8 ** -0.5), ("bq1", 128 ** -0.5), ("bq2", 128 ** -0.5),
                                    ("l_bq", 1 / 16)):
                    ins = nc.vector.tensor_scalar(col(name), col(name), scale, None, ALU.mult)
                ins.then_inc(prep, 1)
                dve.wait_ge(prep, 1)
        small_head_attention(
            k, "gqa", 4, xT, [cT], xT, g_w[:, :, 0:D], g_w[:, :, D:D + P], g_w[:, :, D + P:],
            col("g_bq"), col("g_bk"), row("g_bv"), 8 ** -0.5, lambda b, qt: mask[:, b % 2, qt, :],
            a["g_sel"], expand_g, ident, [(act_in, 32), (vec_in, 48), (g_in, 32)], lambda n: n % 4 == 0,
            a["mask"], mask, mask_in)
        k.pop()
        out_projection(k, "gqa_out", xT, KC, g_wo, X, X, row("g_bo"), (x_in, 16))
        k.pop()
        norm_rows(k, "gqa_norm", X, 1e-6, row("gamma"), row("beta"))

        hT = xT
        for i in (1, 2):
            k.push()
            xn = k.sb(f"ln{i}_xn", [P, NT, D])
            norm_transpose(k, f"ln{i}", X, hT, xn, ident, 1e-5, col(f"ln{i}_scale"), col(f"ln{i}_offset"))
            k.pop()
            k.push()
            vrow = k.sb(f"vrow{i}", [P, 16 * P])
            k.push()
            bvr = k.sb(f"bias_v_row{i}", [P, 16 * P])
            rows_in = k.sem(f"v_rows_in{i}")
            with nc.Block() as block:
                @block.sync
                def _(sp):
                    sp.dma_start(vrow[:, :], a[f"bv{i}"].broadcast_to([P, 16 * P])).then_inc(rows_in, 16)
                    sp.dma_start(bvr[:, :], a[f"bias_v{i}"].broadcast_to([P, 16 * P])).then_inc(rows_in, 16)

                @block.vector
                def _(dve):
                    dve.wait_ge(rows_in, 32)
                    nc.vector.tensor_tensor(vrow[:, :], vrow[:, :], bvr[:, :], ALU.subtract).then_inc(rows_in, 1)
                    dve.wait_ge(rows_in, 33)
            k.pop()
            wide_head_attention(k, f"wide{i}", hT, cT, a[f"w{i}"], a[f"wo{i}"], X, ident, col(f"bq{i}"), col(f"bk{i}"),
                                col(f"bias_k{i}"), col(f"bias_v{i}"), vrow, row(f"bo{i}"))
            k.pop()

        def mlp(name, w1_dram, w2_dram, b1, func, residual, b2, norm):
            k.push()
            w1 = k.sb(f"{name}_w1", [P, KC, 1024])
            w2 = k.sb(f"{name}_w2", [P, 8, D])
            gT = k.sb(f"{name}_gT", [P, 8, TOK])
            xn = k.sb(f"{name}_xn", [P, NT, D])
            w_in = k.sem(f"{name}_w_in")
            with nc.Block() as block:
                @block.sync
                def _(sp):
                    sp.dma_start(w1[:, :].rearrange("p c n -> p (c n)"), w1_dram).then_inc(w_in, 16)
                    sp.dma_start(w2[:, :].rearrange("p c n -> p (c n)"), w2_dram).then_inc(w_in, 16)
                    sp.wait_ge(w_in, 32)
            norm(xn)
            hidden_layer(k, f"{name}_1", hT, w1, b1, gT, func, 8)
            out_projection(k, f"{name}_2", gT, 8, w2, X, residual, b2)
            k.pop()

        mlp("mlp1", a["w_fc1"], a["w_fc2"], col("b_fc1"), ACT.Gelu, X, row("b_fc2"),
            lambda xn: norm_transpose(k, "ln_mlp", X, hT, xn, ident, 1e-5, col("ln_mlp_scale"), col("ln_mlp_offset")))

        k.push()
        s_w = k.sb("s_w", [P, KC, 4, D])
        s_in = k.sem("s_weights_in")
        with nc.Block() as block:
            @block.sync
            def _(sp):
                sp.dma_start(s_w[:, :].rearrange("p c a n -> p (c a n)"), a["s_w"]).then_inc(s_in, 16)
        transpose_tokens(k, "x2", X, xT, ident)
        single_head_attention(k, "one", xT, cT, X, s_w, s_in, col("alpha"), ident)
        k.pop()

        transpose_tokens(k, "x3", X, xT, ident)
        l_wo = k.sb("l_wo", [P, KC, D])
        k.push()
        l_w = k.sb("l_w", [P, KC, 3 * D])
        far = k.sb("far", [P, B, 2 * S], BF16)
        k.push()
        mask_int = k.sb("mask_int", [P, B * S], I32)
        l_in = k.sem("l_weights_in")
        lm_in = k.sem("l_mask_in")
        far_ready = k.sem("far_ready")
        with nc.Block() as block:
            @block.sync
            def _(sp):
                sp.dma_start(mask_int[:, :], a["key_mask"].broadcast_to([P, B * S])).then_inc(lm_in, 16)
                sp.dma_start(l_w[:, :].rearrange("p c n -> p (c n)"), a["l_w"]).then_inc(l_in, 16)
                sp.dma_start(l_wo[:, :].rearrange("p c n -> p (c n)"), a["l_wo"]).then_inc(l_in, 16)

            @block.vector
            def _(dve):
                nc.vector.memset(far[:, :, S:2 * S], 0.0)
                dve.wait_ge(lm_in, 16)
                nc.vector.tensor_scalar(far[:, :, 0:S], mask_int[:, :].rearrange("p (b s) -> p b s", b=B), 0.0, FAR,
                                        ALU.is_equal, ALU.mult).then_inc(far_ready, 1)
                dve.wait_ge(far_ready, 1)
        k.pop()
        small_head_attention(
            k, "latent", 2, xT, [cT, xT], xT, l_w[:, :, 0:D], l_w[:, :, D:2 * D], l_w[:, :, 2 * D:],
            col("l_bq"), col("l_bk"), row("l_bv"), 1 / 16, lambda b, qt: far[:, b, :],
            a["l_sel"], expand_l, ident, [(l_in, 32)], lambda n: n % 8 in (1, 2, 3, 4, 5))
        k.pop()
        LX = k.sb("LX", [P, NT, D])
        out_projection(k, "latent_out", xT, KC, l_wo, LX, X, row("l_bo"))
        saved = X
        X = LX
        mlp("mlp3", a["mlp_w1"], a["mlp_w2"], col("mlp_b1"), ACT.Gelu_apprx_tanh, saved, row("mlp_b2"),
            lambda xn: norm_transpose(k, "rms", X, hT, xn, ident, 1e-6, col("postnorm_w"), None, rms=True))
        stored = k.sem("stored")
        with nc.Block() as block:
            @block.sync
            def _(sp):
                sp.dma_start(out.rearrange("(n p) d -> p n d", p=P), X[:, :]).then_inc(stored, 16)
                sp.wait_ge(stored, 16)


def kernel(**inputs):
    import numpy as np
    import concourse.bacc as bacc
    from concourse.bass_utils import run_bass_kernel_spmd

    v = {n: np.asarray(x) for n, x in inputs.items()}

    def w(m):
        m = np.asarray(m)
        return np.ascontiguousarray(m.reshape(-1, 128, m.shape[1]).transpose(1, 0, 2).reshape(128, -1))

    def by_feature(vec):
        return np.asarray(vec).reshape(-1, 128).T

    L0, L1, L2, L3 = "L0_xattn_", "L1_xattn_", "L2_xattn_", "L3_xattn_"
    p = np.arange(128)
    kv_b = v[L3 + "kv_b"].reshape(256, 2)
    kv_w = v[L3 + "kv_w"].reshape(256, 256, 2)
    col = {
        "g_bq": by_feature(v[L0 + "bq"]), "g_bk": by_feature(np.tile(v[L0 + "bk"], 2)),
        "l_bq": by_feature(v[L3 + "q_b"]), "l_bk": by_feature(kv_b[:, 0]),
        "alpha": np.broadcast_to(v[L2 + "alpha"].reshape(1, 1), (128, 1)),
        "postnorm_w": by_feature(v[L3 + "postnorm_w"]), "mlp_b1": by_feature(v[L3 + "mlp_b1"]),
    }
    for n in COLS:
        if n not in col:
            col[n] = by_feature(v[L1 + n])
    row = {"g_bv": v[L0 + "bv"], "g_bo": v[L0 + "bo"], "gamma": v[L0 + "gamma"], "beta": v[L0 + "beta"],
           "bo1": v[L1 + "bo1"], "bo2": v[L1 + "bo2"], "b_fc2": v[L1 + "b_fc2"],
           "l_bv": kv_b[:, 1], "l_bo": v[L3 + "out_b"], "mlp_b2": v[L3 + "mlp_b2"]}

    def offsets(names, widths):
        at, o = {}, 0
        for n in names:
            at[n] = (o, widths[n])
            o += widths[n]
        return at

    at_col = offsets(COLS, {n: col[n].shape[1] for n in COLS})
    at_row = offsets(ROWS, {n: row[n].size for n in ROWS})
    consts = np.zeros((128, 384), np.float32)
    consts[:, 0:128] = np.eye(128)
    consts[p // 8, 128 + p] = 1.0
    consts[p // 16, 256 + p] = 1.0

    sels = {}
    for name, fd in (("g_sel", 8), ("l_sel", 16)):
        head, copy, feature = p // (4 * fd), p // fd % 4, p % fd
        m = np.zeros((128, 16, 128), np.float32)
        for quarter in range(4):
            source = 32 * quarter + head * fd + feature
            m[source, quarter, p] = copy < 2
            m[source, 4 + quarter, p] = copy >= 2
            if fd == 16:
                m[source, 8 + quarter, p] = copy % 2 == 0
                m[source, 12 + quarter, p] = copy % 2 == 1
        if fd == 8:
            for chunk in range(8):
                m[64 * (copy % 2) + 8 * chunk + feature, 8 + chunk, p] = 1.0
        sels[name] = m.reshape(128, 2048)

    arrays = {
        **sels,
        "x": v["x"].reshape(1024, 256), "xT": w(v["x"].reshape(1024, 256).T), "cT": w(v["ctx_2048"].reshape(1024, 256).T),
        "mask": v["mask_Bx1xSxS2_ff0"].reshape(1024, 256), "key_mask": v["mask_BxS2_ik0"].reshape(1, 1024),
        "cols": np.concatenate([col[n] for n in COLS], axis=1),
        "rows": np.concatenate([row[n].reshape(1, -1) for n in ROWS], axis=1),
        "consts": consts,
        "g_w": w(np.concatenate([v[L0 + "Wq"], v[L0 + "Wk"], v[L0 + "Wk"], v[L0 + "Wv"]], axis=1)),
        "g_wo": w(v[L0 + "Wo"]), "l_wo": w(v[L3 + "out_w"]),
        "s_w": w(np.concatenate([v[L2 + n].T for n in ("w_q", "w_k", "w_v", "w_o")], axis=1)),
        "l_w": w(np.concatenate([v[L3 + "q_w"], kv_w[:, :, 0], kv_w[:, :, 1]], axis=1)),
        "w_fc1": w(v[L1 + "w_fc1"]), "w_fc2": w(v[L1 + "w_fc2"]),
        "mlp_w1": w(v[L3 + "mlp_w1"]), "mlp_w2": w(v[L3 + "mlp_w2"]),
    }
    for i in ("1", "2"):
        qkv = np.stack([v[L1 + n + i].reshape(2, 128, 16, 128) for n in ("wq", "wk", "wv")])
        arrays["w" + i] = qkv.transpose(3, 2, 1, 0, 4).reshape(16, 128, 768)
        arrays["wo" + i] = w(v[L1 + "wo" + i])
        arrays["bv" + i] = v[L1 + "bv" + i].reshape(1, 2048)
        arrays["bias_v" + i] = v[L1 + "bias_v" + i].reshape(1, 2048)

    nc = bacc.Bacc("TRN2", target_bir_lowering=False, num_devices=1)
    feed, aps = {}, {}
    for n, x in arrays.items():
        x = np.ascontiguousarray(x)
        feed[f"in_{n}"] = x
        aps[n] = nc.dram_tensor(f"in_{n}", x.shape, mybir.dt.from_np(x.dtype), kind="ExternalInput").ap()
    out = nc.dram_tensor("out", (1024, 256), F32, kind="ExternalOutput").ap()
    cross_attention_stack(nc, aps, at_col, at_row, out)
    r = run_bass_kernel_spmd(nc, [feed], core_ids=[0])
    return r.results[0]["out"].reshape(4, 256, 256)
```

```python
from contextlib import ExitStack

import concourse.bass as bass
from concourse import mybir

F32 = mybir.dt.float32
F32R = mybir.dt.float32r
BF16 = mybir.dt.bfloat16
I32 = mybir.dt.int32
ACT = mybir.ActivationFunctionType
ALU = mybir.AluOpType
AXX = mybir.AxisListType.X

P = 128
B = 4
S = 256
TOK = B * S
NT = TOK // P
D = 256
KC = D // P
BANK = 512
FAR = -1e30
TERMS = {1: [(0, 0)], 2: [(0, 0), (0, 1), (1, 0)]}


class Core:

    def __init__(self, nc, outer):
        self.nc, self.outer, self.stack, self.stage_sems = nc, outer, [outer], None
        self.norm_sems = [self.sem(f"norm_{n}") for n in ("small", "var_ready", "sd_ready", "tile_normed",
                                                          "transposed", "hT_ready", "table")]
        self.norm_uses, self.norm_links = 0, [0]
        self.out_sems = [self.sem(f"out_{n}") for n in ("done", "added")]
        self.out_uses = 0
        self.hidden_sems = [self.sem(f"hidden_{n}") for n in ("done", "read", "high", "low")]
        self.hidden_uses = 0

    def sb(self, name, shape, dt=F32):
        return self.stack[-1].enter_context(self.nc.sbuf_tensor(name, shape, dt))

    def ps(self, name, shape, dt=F32):
        return self.stack[-1].enter_context(self.nc.psum_tensor(name, shape, dt))

    def sem(self, name):
        if self.stage_sems is None:
            return self.outer.enter_context(self.nc.semaphore(name))
        self.stage_sems.append(self.nc.alloc_semaphore(name=name))
        return self.stage_sems[-1]

    def begin_stage(self):
        self.stage_sems = []

    def end_stage(self):
        self.nc.clear_and_free_semaphores(self.stage_sems)
        self.nc.all_engine_barrier()
        self.stage_sems = None

    def push(self):
        self.stack.append(ExitStack())

    def pop(self):
        self.stack.pop().close()


def norm_transpose(k, name, X, hT, xn, ident, eps, scale, offset=None, rms=False, parts=None,
                   beside=None):
    nc = k.nc
    beside = beside or {}
    k.push()
    ps = k.ps(f"{name}_ps", [P, 4, BANK])
    stats = k.sb(f"{name}_stats", [P, NT, 6])
    mv = k.sb(f"{name}_mv", [P, NT, 2])
    ms = k.sb(f"{name}_ms", [P, NT])
    ve = k.sb(f"{name}_ve", [P, NT])
    sd = k.sb(f"{name}_sd", [P, NT])
    rstd = k.sb(f"{name}_rstd", [P, NT])
    small, var_ready, sd_ready, tile_normed, transposed, hT_act, table = k.norm_sems
    use, done = k.norm_uses, k.norm_links
    k.norm_uses += 1
    with nc.Block() as block:
        @block.vector
        def _(dve):
            def link(ins):
                done[0] += 1
                ins.then_inc(small, 1)
                dve.wait_ge(small, done[0])

            for t in range(NT):
                ins = nc.vector.bn_stats(stats[:, t, :], X[:, t, :])
            link(ins)
            for t in range(NT):
                ins = nc.vector.bn_aggr(mv[:, t, :], stats[:, t, :])
            link(ins)
            if rms:
                link(nc.vector.tensor_tensor(ms[:, :], mv[:, :, 0], mv[:, :, 0], ALU.mult))
                link(nc.vector.tensor_tensor(ve[:, :], ms[:, :], mv[:, :, 1], ALU.add))
                nc.vector.tensor_scalar(ms[:, :], ve[:, :], eps, None, ALU.add).then_inc(var_ready, 1)
            else:
                nc.vector.tensor_scalar(ms[:, :], mv[:, :, 1], eps, None, ALU.add).then_inc(var_ready, 1)
            dve.wait_ge(sd_ready, use + 1)
            link(nc.vector.reciprocal(rstd[:, :], sd[:, :]))
            for t in range(NT):
                if rms:
                    ins = nc.vector.tensor_scalar(xn[:, t, :], X[:, t, :], rstd[:, t:t + 1], None, ALU.mult)
                else:
                    ins = nc.vector.tensor_scalar(xn[:, t, :], X[:, t, :], mv[:, t, 0:1], rstd[:, t:t + 1],
                                                  ALU.subtract, ALU.mult)
                ins.then_inc(tile_normed, 1)
            if parts is not None:
                for half in range(2):
                    for c in range(KC):
                        dve.wait_ge(hT_act, 4 * use + 2 * half + c + 1)
                        piece = slice(half * BANK, (half + 1) * BANK)
                        link(nc.vector.tensor_copy(parts[0][:, c, piece], hT[:, c, piece]))
                        nc.vector.tensor_tensor(parts[1][:, c, piece], hT[:, c, piece],
                                                parts[0][:, c, piece].bitcast(F32), ALU.subtract)
            if "dve" in beside:
                beside["dve"](dve)

        @block.tensor
        def _(pe):
            for half in range(2):
                for c in range(KC):
                    for t in range(4):
                        if c == 0:
                            pe.wait_ge(tile_normed, NT * use + 4 * half + t + 1)
                        ins = nc.tensor.transpose(ps[:, 2 * half + c, t * P:(t + 1) * P],
                                                  xn[:, 4 * half + t, c * P:(c + 1) * P], ident)
                    ins.then_inc(transposed, 1)

        if "sp" in beside:
            block.sync(beside["sp"])
        if "pool" in beside:
            block.gpsimd(beside["pool"])

        @block.scalar
        def _(act):
            nc.scalar.activation(sd[:, 0:1], ident[:, 0:1], ACT.Sqrt).then_inc(table, 1)
            act.wait_ge(table, use + 1)
            act.wait_ge(var_ready, use + 1)
            nc.scalar.activation(sd[:, :], ms[:, :], ACT.Sqrt).then_inc(sd_ready, 1)
            for half in range(2):
                for c in range(KC):
                    act.wait_ge(transposed, 4 * use + 2 * half + c + 1)
                    ins = nc.scalar.activation(hT[:, c, half * BANK:(half + 1) * BANK], ps[:, 2 * half + c, :],
                                               ACT.Identity, bias=offset[:, c:c + 1] if offset is not None else 0.0,
                                               scale=scale[:, c:c + 1])
                    ins.then_inc(hT_act, 1)
            if "act" in beside:
                beside["act"](act)
    k.pop()


def transpose_tokens(k, name, X, xT, ident):
    nc = k.nc
    k.push()
    ps = k.ps(f"{name}_ps", [P, 4, BANK])
    transposed = k.sem(f"{name}_transposed")
    copied = k.sem(f"{name}_copied")
    with nc.Block() as block:
        @block.tensor
        def _(pe):
            for n in range(4):
                half, c = n // KC, n % KC
                for t in range(4):
                    ins = nc.tensor.transpose(ps[:, n, t * P:(t + 1) * P],
                                              X[:, 4 * half + t, c * P:(c + 1) * P], ident)
                ins.then_inc(transposed, 1)

        @block.scalar
        def _(act):
            for n in range(0, 4, 2):
                act.wait_ge(transposed, n + 1)
                nc.scalar.copy(xT[:, n % KC, (n // KC) * BANK:(n // KC + 1) * BANK], ps[:, n, :]).then_inc(copied, 1)

        @block.vector
        def _(dve):
            for n in range(1, 4, 2):
                dve.wait_ge(transposed, n + 1)
                nc.vector.tensor_copy(xT[:, n % KC, (n // KC) * BANK:(n // KC + 1) * BANK],
                                      ps[:, n, :]).then_inc(copied, 1)
    k.pop()


def small_head_attention(k, name, J, queryT, keyTs, attnT, wq, wk, wv, bq, bk, bv_row, scale, mask_of,
                         sel_dram, expand, ident, loads, late_loads, row_in, act_copies, mask_dram=None, mask=None, mask_in=None,
                         load_more=None):
    nc = k.nc
    CH = 8
    W = 1024
    KEYS = W // J
    ST = KEYS // P
    RH = P // J
    FD = 32 // J
    VN = wv.shape[2]
    KPJ = BANK // KEYS
    NKS = 4 // KPJ
    SHARED = J == 4
    NV = ST // 2
    STEPS = B * 16
    OCTETS = STEPS // 8
    PV_TILES = [(t,) for t in range(8)]
    TAIL = 7
    SM = 3
    RAW = [("kq", 0)] if SHARED else [("k", 0), ("q", 0)]
    STACKS = [("ks", i) for i in range(NKS)] + [("qs", i) for i in range(2)]
    if SHARED:
        PLAN = {-2: ("ks", 0, 0), 1: ("ks", 1, 0), 2: ("qs", 0, 0), 3: ("kq", 0, 1), 4: ("qs", 1, 0)}
    else:
        PLAN = {-2: ("ks", 0, 0), -1: ("ks", 1, 0), 0: ("ks", 2, 0), 1: ("ks", 3, 0),
                2: ("qs", 0, 0), 3: ("k", 0, 1), 4: ("qs", 1, 0), 5: ("q", 0, 1)}

    def planned(n):
        v, at = (n // 8 + 2, n % 8 - 8) if n % 8 >= 6 else (n // 8 + 1, n % 8)
        if at not in PLAN or v + PLAN[at][2] >= OCTETS:
            return None
        return (v + PLAN[at][2], *PLAN[at][:2])

    def v_job_at(n):
        if n < NV:
            return (0, n)
        b, v = n // 16 + 1, n % 16 // 8
        return (b, v) if n % 8 == 6 and b < B and v < NV else None

    first_jobs = [(0, *job) for job in RAW + STACKS]
    early_raws = [(1, *job) for job in RAW]
    early_stacks = [planned(n) for n in (-2, -1) if planned(n)]
    order = {job: i for i, job in enumerate(first_jobs + early_raws + early_stacks + [planned(n) for n in range(STEPS)
                                                                       if planned(n)])}

    def raw_of(v, kind):
        return v + 1 if SHARED else 2 * v + (1 if kind in ("k", "ks") else 2)

    k.push()
    psS = k.ps(f"{name}_psS", [P, 2, W])
    psT = k.ps(f"{name}_psT", [P, W])
    psM = k.ps(f"{name}_psM", [P, BANK])
    psC = k.ps(f"{name}_psC", [P, BANK])
    sel = k.sb(f"{name}_sel", [P, 16, P], F32R)
    Qst = k.sb(f"{name}_Qst", [P, 2, 4, S], F32R)
    if SHARED:
        Kst = k.sb(f"{name}_Kst", [P, 2, BANK], F32R)
    Kbd = k.sb(f"{name}_Kbd", [P, 2, 4, J, KEYS], F32R)
    Vpad = k.sb(f"{name}_Vpad", [P, 2, ST, CH, J, 32])
    NK = len(keyTs) * S
    full = k.sb(f"{name}_full", [P, NK + S])
    hi = k.sb(f"{name}_hi", [P, 2, NK + S], F32R)
    lo = k.sb(f"{name}_lo", [P, 2, NK + S], F32R)
    Sm = k.sb(f"{name}_Sm", [P, SM, W])
    PT = k.sb(f"{name}_PT", [P, 8, 8, S])
    nmax = k.sb(f"{name}_nmax", [P, SM, J])
    sums = k.sb(f"{name}_sums", [P, 2, 2, 4 * J])
    rec = k.sb(f"{name}_rec", [P, 2, 4 * J])
    recT = k.sb(f"{name}_recT", [4 * J, S])
    R = k.sb(f"{name}_R", [P, S])

    sel_in = k.sem(f"{name}_sel_in")
    sel_ready = k.sem(f"{name}_sel_ready")
    zeroed = k.sem(f"{name}_zeroed")
    v_zeroed = k.sem(f"{name}_v_zeroed")
    m_done = k.sem(f"{name}_m_done")
    m_free = k.sem(f"{name}_m_free")
    hi_ready = k.sem(f"{name}_hi_ready")
    parts_ready = k.sem(f"{name}_parts_ready")
    if SHARED:
        first_placed = k.sem(f"{name}_first_placed")
        placed = k.sem(f"{name}_placed")
    v_done = k.sem(f"{name}_v_done")
    v_ready = k.sem(f"{name}_v_ready")
    scored = k.sem(f"{name}_scored")
    maxed = k.sem(f"{name}_maxed")
    exped = k.sem(f"{name}_exped")
    turned = k.sem(f"{name}_turned")
    pt_first = k.sem(f"{name}_pt_first")
    pt_second = k.sem(f"{name}_pt_second")
    rec_ready = k.sem(f"{name}_rec_ready")
    rec_turned = k.sem(f"{name}_rec_turned")
    recT_ready = k.sem(f"{name}_recT_ready")
    rec_spread = k.sem(f"{name}_rec_spread")
    R_ready = k.sem(f"{name}_R_ready")
    pv_done = k.sem(f"{name}_pv_done")
    out_ready = k.sem(f"{name}_out_ready")

    def where(n):
        b, r = divmod(n, 16)
        c4, r = divmod(r, 8)
        qt, gg = divmod(r, 4)
        return b, c4, qt, gg

    def bank_of(job):
        M = order[job]
        if job[0] == 0:
            return psS[:, M // 2 % 2, M % 2 * BANK:(M % 2 + 1) * BANK], M - 3
        return psM[:, :], M

    def wait_placed(eng, stack):
        if stack < NKS:
            eng.wait_ge(first_placed, (stack + 1) * J)
        else:
            eng.wait_ge(placed, (stack + 1 - NKS) * J)

    def pt_slot(n):
        return n // 8 % 2 * 4 + n % 4, n // 8 - 1

    def place(eng, v, i, signal):
        for j in range(J):
            r = slice(j * RH, (j + 1) * RH)
            src = Kst[r, i % 2, :].bitcast(F32).rearrange("p (c s) -> p c s", c=KPJ)
            eng.tensor_copy(Kbd[r, v % 2, i * KPJ:(i + 1) * KPJ, j, :], src).then_inc(signal, 1)

    def steps():
        for n in range(STEPS + TAIL):
            u = n // 8 - 1
            yield n, u, n % 8, n < STEPS, u >= 0

    with nc.Block() as block:
        @block.sync
        def _(sp):
            sp.dma_start(Sm[:, 0:2].rearrange("p a w -> p (a w)"), sel_dram).then_inc(sel_in, 16)
            for b in range(B if mask_dram is not None else 0):
                if b >= 2:
                    sp.wait_ge(maxed, 16 * (b - 1))
                sp.dma_start(mask[:, b % 2], mask_dram[b * S:(b + 1) * S].rearrange("(n p) d -> p n d", p=P)
                             ).then_inc(mask_in[b % 2], 16)
                if b == 0 and load_more is not None:
                    load_more(sp)

        @block.tensor
        def _(pe):
            def job(v, kind, i):
                bank, before = bank_of((v, kind, i))
                slot, b, c4 = v % 2, v // 2, v % 2
                if before > 0:
                    pe.wait_ge(m_free, before)
                if kind in ("ks", "qs"):
                    pe.wait_ge(parts_ready, raw_of(v, kind))
                if kind in ("k", "kq"):
                    which = 0 if SHARED else c4
                    for s, keyT in enumerate(keyTs):
                        for c in range(KC):
                            ins = nc.tensor.matmul(bank[:, s * S:(s + 1) * S], wk[:, c, which * P:(which + 1) * P],
                                                   keyT[:, c, b * S:(b + 1) * S], start=(c == 0), stop=(c == KC - 1))
                if kind in ("q", "kq"):
                    o = S if SHARED else 0
                    for c in range(KC):
                        ins = nc.tensor.matmul(bank[:, o:o + S], wq[:, c, c4 * P:(c4 + 1) * P],
                                               queryT[:, c, b * S:(b + 1) * S], start=(c == 0), stop=(c == KC - 1))
                if kind == "qs":
                    for x in range(2):
                        nc.tensor.matmul(bank[:, x * S:(x + 1) * S], sel[:, 2 * i + x, :], hi[:, slot, NK:NK + S],
                                         start=True, stop=False)
                        ins = nc.tensor.matmul(bank[:, x * S:(x + 1) * S], sel[:, 4 + 2 * i + x, :],
                                               lo[:, slot, NK:NK + S], start=False, stop=True)
                if kind == "ks" and SHARED:
                    for x in range(2):
                        ins = nc.tensor.matmul(bank[:, x * S:(x + 1) * S], sel[:, 8 + 4 * c4 + 2 * i + x, :],
                                               hi[:, slot, 0:S], start=True, stop=True)
                if kind == "ks" and not SHARED:
                    nc.tensor.matmul(bank[:, :], sel[:, 8 + i, :], hi[:, slot, 0:NK], start=True, stop=False)
                    ins = nc.tensor.matmul(bank[:, :], sel[:, 12 + i, :], lo[:, slot, 0:NK], start=False, stop=True)
                ins.then_inc(m_done, 1)

            def v_job(b, v, u):
                if u >= 0:
                    pe.wait_ge(out_ready, u + 1)
                if b * NV + v > 0:
                    pe.wait_ge(v_ready, b * NV + v)
                for i in range(2):
                    t = 2 * v + i
                    src, tt = keyTs[v], 2 * b + i
                    for c in range(KC):
                        ins = nc.tensor.matmul(psC[:, i * VN:(i + 1) * VN], src[:, c, tt * P:(tt + 1) * P],
                                               wv[:, c, :], start=(c == 0), stop=(c == KC - 1))
                ins.then_inc(v_done, 1)

            def score(n):
                b, c4, qt, gg = where(n)
                v = n // 8
                if n % 8 == 0:
                    pe.wait_ge(m_free, order[v, "qs", 1] + 1)
                    if SHARED:
                        wait_placed(pe, (v + 1) * NKS - 1)
                if n >= 2:
                    pe.wait_ge(maxed, n - 1)
                for x in range(2):
                    kk = Kbd[:, v % 2, gg, :, :].rearrange("p j s -> p (j s)")
                    ins = nc.tensor.matmul(psS[:, n % 2, x * BANK:(x + 1) * BANK],
                                           Qst[:, v % 2, gg, qt * P:(qt + 1) * P],
                                           kk[:, x * BANK:(x + 1) * BANK], start=True, stop=True)
                ins.then_inc(scored, 1)

            for load in loads:
                pe.wait_ge(*load)
            for j in first_jobs:
                if j[1:] == STACKS[0]:
                    pe.wait_ge(sel_ready, 1)
                job(*j)
            pe.wait_ge(zeroed, 2)
            score(0)
            score(1)
            for j in early_raws:
                job(*j)
            for n, u, s, in_range, lags in steps():
                if n + 2 < STEPS:
                    score(n + 2)
                for half in range(2):
                    if in_range:
                        if half == 0:
                            pe.wait_ge(exped, n + 1)
                        if n >= 1:
                            pe.wait_ge(pt_second if half else pt_first, n)
                        for t in range(4 * half, 4 * half + 4):
                            ins = nc.tensor.transpose(psT[:, t * P:(t + 1) * P], Sm[:, n % SM, t * P:(t + 1) * P],
                                                      ident)
                        ins.then_inc(turned, 1)
                    if lags and s < 4:
                        b, c4 = u // 2, u % 2
                        if s == 0 and half == 0:
                            pe.wait_ge(pt_first, 8 * u + 8)
                            pe.wait_ge(pt_second, 8 * u + 8)
                            pe.wait_ge(v_ready, (b + 1) * NV)
                            if u >= 1:
                                pe.wait_ge(out_ready, u)
                        for t in PV_TILES[2 * s + half]:
                            for gg in range(4):
                                ins = nc.tensor.matmul(psC[32 * gg:32 * gg + 32, 0:S],
                                                       Vpad[:, b % 2, t % ST, 4 * c4 + gg, t // ST, :],
                                                       PT[:, 4 * c4 + gg, t, :],
                                                       start=(t == 0), stop=(t == 7), tile_position=(0, 32 * gg))
                        if s == 3 and half == 1:
                            ins.then_inc(pv_done, 1)
                if lags and s == 3:
                    pe.wait_ge(rec_ready, u + 1)
                    for qt in range(2):
                        ins = nc.tensor.transpose(psC[0:4 * J, S + qt * P:S + (qt + 1) * P], rec[:, qt, :], ident)
                    ins.then_inc(rec_turned, 1)
                if lags and s == 4:
                    pe.wait_ge(recT_ready, u + 1)
                    nc.tensor.matmul(psC[:, S:2 * S], expand, recT[:, :], start=True, stop=True).then_inc(rec_spread, 1)
                if n == 0:
                    for j in early_stacks:
                        job(*j)
                if n == 8:
                    for load in late_loads:
                        pe.wait_ge(*load)
                if v_job_at(n):
                    v_job(*v_job_at(n), u)
                if planned(n):
                    job(*planned(n))

        @block.scalar
        def _(act):
            def evacuate(v, kind, i):
                M = order[v, kind, i]
                bank = bank_of((v, kind, i))[0]
                act.wait_ge(m_done, M + 1)
                if kind in ("k", "q", "kq") and v >= 1:
                    act.wait_ge(parts_ready, raw_of(v - 1, kind))
                if i == 0 and v >= 2 and kind in ("ks", "qs"):
                    act.wait_ge(scored, 8 * (v - 1))
                if kind in ("k", "kq"):
                    which = 0 if SHARED else v % 2
                    ins = nc.scalar.activation(full[:, 0:NK], bank[:, 0:NK], ACT.Identity,
                                               bias=bk[:, which:which + 1])
                if kind in ("q", "kq"):
                    o = S if SHARED else 0
                    ins = nc.scalar.activation(full[:, NK:NK + S], bank[:, o:o + S], ACT.Identity,
                                               bias=bq[:, v % 2:v % 2 + 1], scale=scale)
                if kind == "ks" and not SHARED:
                    if i == 0 and v < 2:
                        act.wait_ge(zeroed, v + 1)
                    for j in range(J):
                        ins = nc.scalar.copy(Kbd[j * RH:(j + 1) * RH, v % 2, i, j, :], bank[j * RH:(j + 1) * RH, :])
                if kind == "ks" and SHARED:
                    stack = v * NKS + i
                    if stack >= 2:
                        wait_placed(act, stack - 2)
                    ins = nc.scalar.copy(Kst[:, i % 2, :], bank[:, :])
                if kind == "qs":
                    ins = nc.scalar.copy(Qst[:, v % 2, 2 * i:2 * i + 2, :].rearrange("p c s -> p (c s)"), bank[:, :])
                ins.then_inc(m_free, 1)

            act.wait_ge(sel_in, 16)
            nc.scalar.copy(sel[:, :].rearrange("p a q -> p (a q)"), Sm[:, 0:2].rearrange("p a w -> p (a w)")
                           ).then_inc(sel_ready, 1)
            for j in first_jobs + early_raws:
                evacuate(*j)
            for n, u, s, in_range, lags in steps():
                if in_range:
                    b, c4, qt, gg = where(n)
                    act.wait_ge(maxed, n + 1)
                    if n >= 16 and s == 0:
                        act.wait_ge(rec_ready, u)
                    for j in range(J):
                        ins = nc.scalar.activation(Sm[:, n % SM, j * KEYS:(j + 1) * KEYS],
                                                   Sm[:, n % SM, j * KEYS:(j + 1) * KEYS], ACT.Exp,
                                                   bias=nmax[:, n % SM, j:j + 1], scale=-1.0,
                                                   accum_out=sums[:, (n // 8) % 2, qt, gg * J + j:gg * J + j + 1])
                    ins.then_inc(exped, 1)
                if lags and s == 4:
                    act.wait_ge(rec_turned, u + 1)
                    nc.scalar.copy(recT[:, :], psC[0:4 * J, S:2 * S]).then_inc(recT_ready, 1)
                if lags and s == 5:
                    act.wait_ge(rec_spread, u + 1)
                    nc.scalar.copy(R[:, :], psC[:, S:2 * S]).then_inc(R_ready, 1)
                if 1 <= n <= STEPS and act_copies(n - 1):
                    t = n - 1
                    slot, octets = pt_slot(t)
                    act.wait_ge(turned, 2 * t + 1)
                    if octets > 0:
                        act.wait_ge(pv_done, octets)
                    qt = (t // 4) % 2
                    nc.scalar.copy(PT[:, slot, 0:4, qt * P:(qt + 1) * P],
                                   psT[:, 0:BANK].rearrange("p (t q) -> p t q", t=4)).then_inc(pt_first, 1)
                if n == 1:
                    for j in early_stacks:
                        evacuate(*j)
                if n >= 1 and planned(n - 1):
                    evacuate(*planned(n - 1))

        @block.vector
        def _(dve):
            def parts(v, kind, i):
                a, z = {"k": (0, NK), "q": (NK, NK + S), "kq": (0, NK + S)}[kind]
                slot, raw = v % 2, raw_of(v, kind)
                dve.wait_ge(m_free, order[v, kind, i] + 1)
                if v >= 2:
                    dve.wait_ge(m_done, order[v - 2, "qs", 1] + 1)
                nc.vector.tensor_copy(hi[:, slot, a:z], full[:, a:z]).then_inc(hi_ready, 1)
                dve.wait_ge(hi_ready, raw)
                if SHARED:
                    nc.vector.tensor_tensor(hi[64:128, slot, 0:NK], full[64:128, 0:NK],
                                            hi[64:128, slot, 0:NK].bitcast(F32), ALU.subtract)
                    a = NK
                nc.vector.tensor_tensor(lo[:, slot, a:z], full[:, a:z], hi[:, slot, a:z].bitcast(F32),
                                        ALU.subtract).then_inc(parts_ready, 1)

            def v_out(b, v):
                dve.wait_ge(v_done, b * NV + v + 1)
                if b == 0 and v == 0:
                    dve.wait_ge(v_zeroed, 1)
                    if row_in is not None:
                        dve.wait_ge(*row_in)
                if b >= 2:
                    dve.wait_ge(pv_done, 2 * (b - 1))
                src = psC[:, 0:2 * VN].rearrange("p (t g d) -> p t g d", t=2, d=FD)
                row = bv_row.rearrange("p (g d) -> p g d", d=FD)
                for j in range(J):
                    for t in range(2):
                        a, r = (src[:, t], row) if SHARED else (src[:, t, j::J], row[:, j::J])
                        ins = nc.vector.tensor_tensor(Vpad[:, b % 2, 2 * v + t, :, j, FD * j:FD * (j + 1)], a, r, ALU.add)
                        if j == J - 1 and t == 1:
                            ins.then_inc(v_ready, 1)

            nc.vector.memset(Kbd[:, 0].rearrange("p c j s -> p (c j s)").bitcast(F32), 0.0).then_inc(zeroed, 1)
            for v, kind, i in first_jobs:
                if (kind, i) in RAW:
                    parts(v, kind, i)
                elif kind == "ks" and SHARED and v == 0:
                    dve.wait_ge(m_free, order[v, kind, i] + 1)
                    dve.wait_ge(zeroed, 1)
                    place(nc.vector, v, i, first_placed)
            dve.wait_ge(sel_ready, 1)
            for n, u, s, in_range, lags in steps():
                if in_range:
                    b, c4, qt, gg = where(n)
                    if mask_dram is not None and n % 16 == 0:
                        dve.wait_ge(mask_in[b % 2], 16 * (b // 2 + 1))
                    dve.wait_ge(scored, n + 1)
                    if n >= SM:
                        dve.wait_ge(turned, 2 * (n - SM + 1))
                    for j in range(J):
                        ins = nc.vector.tensor_tensor_reduce(Sm[:, n % SM, j * KEYS:(j + 1) * KEYS],
                                                             psS[:, n % 2, j * KEYS:(j + 1) * KEYS], mask_of(b, qt),
                                                             -1.0, 3.4e38, ALU.add, ALU.min,
                                                             nmax[:, n % SM, j:j + 1])
                    ins.then_inc(maxed, 1)
                if n == 0:
                    for j in early_raws:
                        parts(*j)
                if 2 <= n <= STEPS + 1:
                    t = n - 2
                    slot, octets = pt_slot(t)
                    if octets > 0:
                        dve.wait_ge(pv_done, octets)
                    qt = (t // 4) % 2
                    for half in range(act_copies(t), 2):
                        dve.wait_ge(turned, 2 * t + half + 1)
                        nc.vector.tensor_copy(PT[:, slot, 4 * half:4 * half + 4, qt * P:(qt + 1) * P],
                                              psT[:, half * BANK:(half + 1) * BANK].rearrange("p (t q) -> p t q", t=4)
                                              ).then_inc(pt_second if half else pt_first, 1)
                if n >= 2 and v_job_at(n - 2):
                    v_out(*v_job_at(n - 2))
                if n >= 3 and planned(n - 3) and planned(n - 3)[1:] in RAW:
                    parts(*planned(n - 3))
                if lags and s == 0:
                    dve.wait_ge(exped, 8 * u + 8)
                    if u >= 1:
                        dve.wait_ge(rec_turned, u)
                    nc.vector.reciprocal(rec[:, :, :], sums[:, u % 2, :, :]).then_inc(rec_ready, 1)
                if lags and s == 6:
                    b, c4 = u // 2, u % 2
                    dve.wait_ge(pv_done, u + 1)
                    dve.wait_ge(R_ready, u + 1)
                    nc.vector.tensor_tensor(attnT[:, c4, b * S:(b + 1) * S], psC[:, 0:S], R[:, :], ALU.mult
                                            ).then_inc(out_ready, 1)

        @block.gpsimd
        def _(pool):
            pool.wait_ge(zeroed, 1)
            nc.gpsimd.memset(Kbd[:, 1].rearrange("p c j s -> p (c j s)").bitcast(F32), 0.0
                             ).then_inc(zeroed, 1)
            nc.gpsimd.memset(Vpad[:, :].rearrange("p w a b c d -> p (w a b c d)"), 0.0).then_inc(v_zeroed, 1)
            for v in range(1, OCTETS if SHARED else 1):
                for i in range(NKS):
                    if v == 1 and i == 0:
                        pool.wait_ge(zeroed, 2)
                        pool.wait_ge(v_zeroed, 1)
                    pool.wait_ge(m_free, order[v, "ks", i] + 1)
                    if v >= 2 and i == 0:
                        pool.wait_ge(scored, 8 * (v - 1))
                    place(nc.gpsimd, v, i, placed)
    k.pop()


def out_projection(k, name, inT, nch, w, X, residual, row, load=None):
    nc = k.nc
    k.push()
    ps = k.ps(f"{name}_ps", [P, NT, BANK])
    addend = k.sb(f"{name}_addend", [P, NT, D])
    (done, added), use = k.out_sems, k.out_uses
    k.out_uses += 1
    with nc.Block() as block:
        @block.tensor
        def _(pe):
            if load is not None:
                pe.wait_ge(*load)
            for t in range(NT):
                terms = [(x, y, c) for x, y in TERMS[len(w)] for c in range(nch)]
                for x, y, c in terms:
                    ins = nc.tensor.matmul(ps[:, t, 0:D], inT[x][:, c, t * P:(t + 1) * P], w[y][:, c, :],
                                           start=(x, y, c) == terms[0], stop=(x, y, c) == terms[-1])
                ins.then_inc(done, 1)

        @block.vector
        def _(dve):
            if load is not None:
                dve.wait_ge(*load)
            nc.vector.tensor_tensor(addend[:, :, :], residual[:, :, :], row.unsqueeze(1).broadcast_to([P, NT, D]),
                                    ALU.add).then_inc(added, 1)
            dve.wait_ge(added, 2 * use + 1)
            for t in range(NT):
                dve.wait_ge(done, NT * use + t + 1)
                ins = nc.vector.tensor_tensor(X[:, t, :], ps[:, t, 0:D], addend[:, t, :], ALU.add)
            ins.then_inc(added, 1)
    k.pop()


def hidden_layer(k, name, hT, w1, b1, gT, func, nf, pool_program):
    nc = k.nc
    k.push()
    ps = k.ps(f"{name}_ps", [P, 8, BANK])
    full = k.sb(f"{name}_full", [P, 4, BANK])
    (done, read, high, low), before = k.hidden_sems, k.hidden_uses * 2 * nf
    k.hidden_uses += 1
    terms = [(x, y, c) for x, y in TERMS[2] for c in range(KC)]
    with nc.Block() as block:
        block.gpsimd(pool_program)

        @block.tensor
        def _(pe):
            for n in range(2 * nf):
                f, half = n // 2, n % 2
                if n >= 8:
                    pe.wait_ge(read, before + n - 7)
                for x, y, c in terms:
                    ins = nc.tensor.matmul(ps[:, n % 8, :], w1[x][:, c, f * P:(f + 1) * P],
                                           hT[y][:, c, half * BANK:(half + 1) * BANK],
                                           start=(x, y, c) == terms[0], stop=(x, y, c) == terms[-1])
                ins.then_inc(done, 1)

        @block.scalar
        def _(act):
            for n in range(2 * nf):
                f, half = n // 2, n % 2
                act.wait_ge(done, before + n + 1)
                if n >= 4:
                    act.wait_ge(low, before + n - 3)
                nc.scalar.activation(full[:, n % 4, :], ps[:, n % 8, :], func, bias=b1[:, f:f + 1]).then_inc(read, 1)

        @block.vector
        def _(dve):
            for n in range(2 * nf):
                f, piece = n // 2, slice(n % 2 * BANK, (n % 2 + 1) * BANK)
                dve.wait_ge(read, before + n + 1)
                nc.vector.tensor_copy(gT[0][:, f, piece], full[:, n % 4, :]).then_inc(high, 1)
                dve.wait_ge(high, before + n + 1)
                nc.vector.tensor_tensor(gT[1][:, f, piece], full[:, n % 4, :], gT[0][:, f, piece].bitcast(F32),
                                        ALU.subtract).then_inc(low, 1)
    k.pop()


class HeadWeights:

    def __init__(self, k, name, wqk_dram, wv_dram):
        self.nc, self.wqk_dram, self.wv_dram = k.nc, wqk_dram, wv_dram
        self.wqk_full = k.sb(f"{name}_wqk_full", [P, 2, KC, 2 * P])
        self.wv_full = k.sb(f"{name}_wv_full", [P, KC, 2 * P])
        self.wqk = k.sb(f"{name}_wqk", [P, 2, 2, KC, 2 * P], F32R)
        self.wv = k.sb(f"{name}_wv", [P, 2, KC, 2 * P], F32R)
        self.wqk_in = [k.sem(f"{name}_wqk_in{i}") for i in range(2)]
        self.wv_in = k.sem(f"{name}_wv_in")
        self.wqk_split = k.sem(f"{name}_wqk_split")
        self.wv_split = k.sem(f"{name}_wv_split")
        self.pool_step = k.sem(f"{name}_pool_step")
        self.steps = 0

    def load_qk(self, sp, h):
        sp.dma_start(self.wqk_full[:, h % 2].rearrange("p c n -> p (c n)"), self.wqk_dram[h]
                     ).then_inc(self.wqk_in[h % 2], 16)

    def load_v(self, sp, p):
        sp.dma_start(self.wv_full[:, :].rearrange("p c n -> p (c n)"), self.wv_dram[p]).then_inc(self.wv_in, 16)

    def link(self, pool, ins):
        self.steps += 1
        ins.then_inc(self.pool_step, 1)
        pool.wait_ge(self.pool_step, self.steps)

    def split(self, pool, full, hi, lo, done):
        self.link(pool, self.nc.gpsimd.tensor_copy(hi, full))
        self.nc.gpsimd.tensor_tensor(lo, full, hi.bitcast(F32), ALU.subtract).then_inc(done, 1)

    def split_qk(self, pool, h, scale):
        pool.wait_ge(self.wqk_in[h % 2], 16 * (h // 2 + 1))
        q = self.wqk_full[:, h % 2, :, 0:P]
        self.link(pool, self.nc.gpsimd.tensor_scalar(q, q, scale, None, ALU.mult))
        self.split(pool, self.wqk_full[:, h % 2].rearrange("p c n -> p (c n)"),
                   self.wqk[:, h % 2, 0].rearrange("p c n -> p (c n)"),
                   self.wqk[:, h % 2, 1].rearrange("p c n -> p (c n)"), self.wqk_split)

    def split_v(self, pool, p):
        pool.wait_ge(self.wv_in, 16 * (p + 1))
        self.split(pool, self.wv_full[:, :].rearrange("p c n -> p (c n)"),
                   self.wv[:, 0].rearrange("p c n -> p (c n)"),
                   self.wv[:, 1].rearrange("p c n -> p (c n)"), self.wv_split)


def wide_head_attention(k, name, h_parts, c_parts, weights, wo_dram, X, ident, bq, bk, bias_k, bias_v,
                        vrow, bo_row):
    nc = k.nc
    H = 16
    SCALE = 128 ** -0.5
    KS = S + 1
    KW = S + 2
    NU = 4 * H
    PAIRS = H // 2
    CTX = 3
    k.push()
    psS = k.ps(f"{name}_psS", [P, 2, 2, BANK])
    psT = k.ps(f"{name}_psT", [P, BANK])
    psC = k.ps(f"{name}_psC", [P, BANK])
    psP = k.ps(f"{name}_psP", [P, 2, BANK])
    wqk, wv, wqk_split, wv_split = weights.wqk, weights.wv, weights.wqk_split, weights.wv_split
    wo_full = k.sb(f"{name}_wo_full", [P, 2, D])
    wo = k.sb(f"{name}_wo", [P, 2, 2, D], F32R)
    qT = k.sb(f"{name}_qT", [P, 2, 2, TOK], F32R)
    kT = k.sb(f"{name}_kT", [P, 2, 2, B, KW], F32R)
    v_full = k.sb(f"{name}_v_full", [P, 2, BANK])
    v = k.sb(f"{name}_v", [P, 2, 2, NT, 2 * P], F32R)
    Pr = k.sb(f"{name}_Pr", [P, 2, 2, KS + 1])
    PT = k.sb(f"{name}_PT", [P, 2, 2, 2, S], F32R)
    ctxT = k.sb(f"{name}_ctxT", [P, 2, CTX, TOK], F32R)
    key = k.sb(f"{name}_key", [P, 2, H], F32R)
    nmax = k.sb(f"{name}_nmax", [P, 2, 2])
    sums = k.sb(f"{name}_sums", [P, 2, 2])
    rec = k.sb(f"{name}_rec", [P, 2, 2])

    wo_in = k.sem(f"{name}_wo_in")
    wo_split = k.sem(f"{name}_wo_split")
    extra_key = k.sem(f"{name}_extra_key")
    x_ready = k.sem(f"{name}_x_ready")
    qk_done = k.sem(f"{name}_qk_done")
    vo_done = k.sem(f"{name}_vo_done")
    qk_hi = k.sem(f"{name}_qk_hi")
    qk_lo = k.sem(f"{name}_qk_lo")
    vo_read = k.sem(f"{name}_vo_read")
    v_hi = k.sem(f"{name}_v_hi")
    v_lo = k.sem(f"{name}_v_lo")
    scored = k.sem(f"{name}_scored")
    maxed = k.sem(f"{name}_maxed")
    exped = k.sem(f"{name}_exped")
    rec_ready = k.sem(f"{name}_rec_ready")
    normed = k.sem(f"{name}_normed")
    turned = k.sem(f"{name}_turned")
    pt_hi = k.sem(f"{name}_pt_hi")
    pt_lo = k.sem(f"{name}_pt_lo")
    pv_done = k.sem(f"{name}_pv_done")
    ctx_hi = k.sem(f"{name}_ctx_hi")
    ctx_lo = k.sem(f"{name}_ctx_lo")

    QK = [("k", 0), ("q", 0), ("k", 1), ("q", 1)]
    vo_jobs = [("v", 0, 0), ("v", 0, 1), ("v", 0, 2)]
    vo_at = {}
    for u in range(NU + 5):
        p, r = divmod(u, 8)
        if r == 0 and p < PAIRS:
            job = ("v", p, 3)
        elif 1 <= r <= 4 and p >= 1:
            job = ("o", p - 1, r - 1)
        elif r >= 5 and p + 1 < PAIRS:
            job = ("v", p + 1, r - 5)
        else:
            continue
        vo_at[u] = job
        vo_jobs.append(job)
    vo_number = {job: i + 1 for i, job in enumerate(vo_jobs)}

    def vo_slot(kind, p, i):
        return 0 if (kind, p, i % 2) == ("o", PAIRS - 1, 1) else 1

    def v_jobs_to(p, i):
        return 4 * p + i + 1

    with nc.Block() as block:
        @block.sync
        def _(sp):
            def load_output_weights(p):
                if p >= 1:
                    sp.wait_ge(wo_split, p)
                sp.dma_start(wo_full[:, :].rearrange("p h n -> p (h n)"), wo_dram[p]).then_inc(wo_in, 16)

            for h in range(2, H):
                sp.wait_ge(wqk_split, h - 1)
                weights.load_qk(sp, h)
                if h % 2 == 0:
                    sp.wait_ge(wv_split, h // 2)
                    weights.load_v(sp, h // 2)
                    load_output_weights(h // 2 - 1)
            load_output_weights(PAIRS - 1)

        @block.gpsimd
        def _(pool):
            def link(ins):
                weights.link(pool, ins)

            def split_qk(h):
                if h >= 2:
                    pool.wait_ge(qk_done, 4 * (h - 1))
                weights.split_qk(pool, h, SCALE)

            def split_v_weights(p):
                pool.wait_ge(vo_done, vo_number["v", p - 1, 3])
                weights.split_v(pool, p)

            def split_o_weights(p):
                pool.wait_ge(wo_in, 16 * (p + 1))
                if p >= 1:
                    pool.wait_ge(vo_done, vo_number["o", p - 1, 3])
                weights.split(pool, wo_full[:, :].rearrange("p h n -> p (h n)"),
                              wo[:, 0].rearrange("p h n -> p (h n)"), wo[:, 1].rearrange("p h n -> p (h n)"),
                              wo_split)

            def add_key(h):
                if h >= 2:
                    pool.wait_ge(scored, 4 * (h - 1))
                for part in range(2):
                    ins = nc.gpsimd.tensor_copy(kT[:, h % 2, part, :, S:KS],
                                                key[:, part, h:h + 1].bitcast(F32).unsqueeze(2).broadcast_to([P, B, 1]))
                ins.then_inc(extra_key, 1)

            def low_v(p, i):
                n = v_jobs_to(p, i)
                pool.wait_ge(v_hi, n)
                o = v[:, p % 2, :, 2 * i:2 * i + 2, :]
                nc.gpsimd.tensor_tensor(o[:, 1].rearrange("p t n -> p (t n)"), v_full[:, (n - 1) % 2, :],
                                        o[:, 0].rearrange("p t n -> p (t n)").bitcast(F32), ALU.subtract
                                        ).then_inc(v_lo, 1)

            for slot in range(2):
                for part in range(2):
                    nc.gpsimd.memset(kT[:, slot, part, :, KS:KW].bitcast(F32), 0.0)
            link(nc.gpsimd.tensor_copy(key[:, 0], bias_k))
            link(nc.gpsimd.tensor_tensor(key[:, 1], bias_k, key[:, 0].bitcast(F32), ALU.subtract))
            add_key(0)
            split_qk(1)
            add_key(1)
            for i in range(3):
                low_v(0, i)
            nc.gpsimd.tensor_tensor(X[:, :].rearrange("p t d -> p (t d)"), X[:, :].rearrange("p t d -> p (t d)"),
                                    bo_row.unsqueeze(1).broadcast_to([P, NT, D]), ALU.add).then_inc(x_ready, 1)
            for p in range(PAIRS):
                low_v(p, 3)
                if p + 1 < PAIRS:
                    split_qk(2 * p + 2)
                    split_v_weights(p + 1)
                    add_key(2 * p + 2)
                if p == 0:
                    split_o_weights(0)
                if p + 1 < PAIRS:
                    split_qk(2 * p + 3)
                    if p >= 1:
                        split_o_weights(p)
                    for i in range(3):
                        low_v(p + 1, i)
                    add_key(2 * p + 3)
                elif p >= 1:
                    split_o_weights(p)

        @block.tensor
        def _(pe):
            def project(h, m):
                kind, half = QK[m]
                n = 4 * h + m
                if m == 0:
                    pe.wait_ge(wqk_split, h + 1)
                if n >= 1:
                    pe.wait_ge(qk_lo, n)
                o = 0 if kind == "q" else P
                src = h_parts if kind == "q" else c_parts
                for x, y in TERMS[2]:
                    for c in range(KC):
                        ins = nc.tensor.matmul(psP[:, 0, :], wqk[:, h % 2, x, c, o:o + P],
                                               src[y][:, c, half * BANK:(half + 1) * BANK],
                                               start=(x, y, c) == (0, 0, 0), stop=(x, y, c) == (1, 0, KC - 1))
                ins.then_inc(qk_done, 1)

            def value_or_output(kind, p, i):
                n = vo_number[kind, p, i]
                slot = vo_slot(kind, p, i)
                if (kind, p, i) == ("o", PAIRS - 1, 1):
                    pe.wait_ge(qk_lo, 4 * H)
                elif kind == "o" and p == PAIRS - 1 and i >= 2:
                    pe.wait_ge(vo_read, n - 2)
                elif n >= 2:
                    pe.wait_ge(vo_read, n - 1)
                if kind == "v":
                    if i == 0:
                        pe.wait_ge(wv_split, p + 1)
                elif i == 0:
                    pe.wait_ge(wo_split, p + 1)
                    pe.wait_ge(ctx_lo, 4 * p + 3)
                elif i == 2:
                    pe.wait_ge(ctx_lo, 4 * p + 4)
                for j in range(2):
                    t = 2 * i + j
                    for x, y in TERMS[2]:
                        for c in range(2):
                            if kind == "v":
                                first, second = c_parts[x][:, c, t * P:(t + 1) * P], wv[:, y, c, :]
                            else:
                                first, second = ctxT[:, x, (2 * p + c) % CTX, t * P:(t + 1) * P], wo[:, y, c, :]
                            ins = nc.tensor.matmul(psP[:, slot, j * D:(j + 1) * D], first, second,
                                                   start=(x, y, c) == (0, 0, 0), stop=(x, y, c) == (1, 0, 1))
                ins.then_inc(vo_done, 1)

            def score(u):
                h, b = divmod(u, 4)
                pe.wait_ge(qk_lo, 4 * h + (2 if b < 2 else 4))
                if b == 0:
                    pe.wait_ge(extra_key, h + 1)
                if u >= 2:
                    pe.wait_ge(exped, u - 1)
                for qt in range(2):
                    o = b * S + qt * P
                    for x, y in TERMS[2]:
                        ins = nc.tensor.matmul(psS[:, u % 2, qt, 0:KW], qT[:, h % 2, x, o:o + P],
                                               kT[:, h % 2, y, b, :], start=(x, y) == (0, 0), stop=(x, y) == (1, 0))
                ins.then_inc(scored, 1)

            def values(u):
                h, b = divmod(u, 4)
                pe.wait_ge(pt_lo, u + 1)
                pe.wait_ge(v_lo, v_jobs_to(h // 2, b))
                if b % 2 == 0 and u >= 2:
                    pe.wait_ge(ctx_lo, u // 2)
                o = (h % 2) * P
                for x, y in TERMS[2]:
                    for st in range(2):
                        ins = nc.tensor.matmul(psC[:, (b % 2) * S:(b % 2 + 1) * S],
                                               v[:, h // 2 % 2, x, 2 * b + st, o:o + P], PT[:, u % 2, y, st, :],
                                               start=(x, y, st) == (0, 0, 0), stop=(x, y, st) == (1, 0, 1))
                ins.then_inc(pv_done, 1)

            for m in range(4):
                project(0, m)
                if m < 3:
                    value_or_output("v", 0, m)
            score(0)
            for u in range(NU + 5):
                h, b = divmod(u, 4)
                if h + 1 < H:
                    project(h + 1, b)
                if u + 1 < NU:
                    score(u + 1)
                if u < NU:
                    pe.wait_ge(normed, u + 1)
                    if u >= 1:
                        pe.wait_ge(pt_lo, u)
                    for qt in range(2):
                        for st in range(2):
                            ins = nc.tensor.transpose(psT[:, st * S + qt * P:st * S + (qt + 1) * P],
                                                      Pr[:, u % 2, qt, st * P:(st + 1) * P], ident)
                    ins.then_inc(turned, 1)
                if 1 <= u <= NU:
                    values(u - 1)
                if u in vo_at:
                    value_or_output(*vo_at[u])

        @block.scalar
        def _(act):
            def high_qk(h, m):
                kind, half = QK[m]
                act.wait_ge(qk_done, 4 * h + m + 1)
                if h >= 2:
                    act.wait_ge(scored, 4 * (h - 1))
                if kind == "q":
                    ins = nc.scalar.activation(qT[:, h % 2, 0, half * BANK:(half + 1) * BANK], psP[:, 0, :],
                                               ACT.Identity, bias=bq[:, h:h + 1])
                else:
                    ins = nc.scalar.activation(kT[:, h % 2, 0, 2 * half:2 * half + 2, 0:S],
                                               psP[:, 0, :].rearrange("p (b s) -> p b s", b=2),
                                               ACT.Identity, bias=bk[:, h:h + 1])
                ins.then_inc(qk_hi, 1)

            def high_v(p, i):
                n = v_jobs_to(p, i)
                act.wait_ge(vo_read, vo_number["v", p, i])
                if p >= 2:
                    act.wait_ge(pv_done, 8 * (p - 1))
                nc.scalar.copy(v[:, p % 2, 0, 2 * i:2 * i + 2, :].rearrange("p t n -> p (t n)"),
                               v_full[:, (n - 1) % 2, :]).then_inc(v_hi, 1)

            def high_ctx(pair):
                h, half = divmod(pair, 2)
                act.wait_ge(pv_done, 2 * pair + 2)
                if h >= CTX and half == 0:
                    act.wait_ge(vo_done, vo_number["o", (h - CTX) // 2, 3])
                nc.scalar.activation(ctxT[:, 0, h % CTX, half * BANK:(half + 1) * BANK], psC[:, :], ACT.Identity,
                                     bias=bias_v[:, h:h + 1]).then_inc(ctx_hi, 1)

            for m in range(4):
                high_qk(0, m)
                if m < 3:
                    high_v(0, m)
            for u in range(NU + 1):
                h, b = divmod(u, 4)
                if u < NU:
                    act.wait_ge(maxed, u + 1)
                    if u >= 2:
                        act.wait_ge(turned, u - 1)
                    for qt in range(2):
                        ins = nc.scalar.activation(Pr[:, u % 2, qt, 0:KS], psS[:, u % 2, qt, 0:KS], ACT.Exp,
                                                   bias=nmax[:, u % 2, qt:qt + 1],
                                                   accum_out=sums[:, u % 2, qt:qt + 1])
                    ins.then_inc(exped, 1)
                if h + 1 < H:
                    high_qk(h + 1, b)
                if u >= 1 and vo_at.get(u - 1, ("o",))[0] == "v":
                    high_v(*vo_at[u - 1][1:])
                if u < NU:
                    act.wait_ge(turned, u + 1)
                    if u >= 2:
                        act.wait_ge(pv_done, u - 1)
                    nc.scalar.copy(PT[:, u % 2, 0].rearrange("p a s -> p (a s)"), psT[:, :]).then_inc(pt_hi, 1)
                if u >= 2 and u % 2 == 0:
                    high_ctx(u // 2 - 1)

        @block.vector
        def _(dve):
            def low_qk(h, m):
                kind, half = QK[m]
                dve.wait_ge(qk_hi, 4 * h + m + 1)
                if kind == "q":
                    o = qT[:, h % 2, :, half * BANK:(half + 1) * BANK]
                    ins = nc.vector.scalar_tensor_tensor(out=o[:, 1], in0=psP[:, 0, :], scalar=bq[:, h:h + 1],
                                                         in1=o[:, 0].bitcast(F32), op0=ALU.add, op1=ALU.subtract)
                else:
                    o = kT[:, h % 2, :, 2 * half:2 * half + 2, 0:S]
                    ins = nc.vector.scalar_tensor_tensor(out=o[:, 1], in0=psP[:, 0, :].rearrange("p (b s) -> p b s", b=2),
                                                         scalar=bk[:, h:h + 1], in1=o[:, 0].bitcast(F32),
                                                         op0=ALU.add, op1=ALU.subtract)
                ins.then_inc(qk_lo, 1)

            def take(kind, p, i):
                dve.wait_ge(vo_done, vo_number[kind, p, i])
                slot = vo_slot(kind, p, i)
                if kind == "v":
                    n = v_jobs_to(p, i)
                    if n > 2:
                        dve.wait_ge(v_lo, n - 2)
                    row = vrow[:, 2 * p * P:2 * (p + 1) * P].unsqueeze(1).broadcast_to([P, 2, 2 * P])
                    ins = nc.vector.tensor_tensor(v_full[:, (n - 1) % 2, :].rearrange("p (t n) -> p t n", t=2),
                                                  psP[:, slot, :].rearrange("p (t n) -> p t n", t=2), row, ALU.add)
                else:
                    if p == 0 and i == 0:
                        dve.wait_ge(x_ready, 1)
                    if p > 0:
                        dve.wait_ge(vo_read, vo_number["o", p - 1, i])
                    x = X[:, 2 * i:2 * i + 2, :].rearrange("p t d -> p (t d)")
                    ins = nc.vector.tensor_tensor(x, psP[:, slot, :], x, ALU.add)
                ins.then_inc(vo_read, 1)

            def top(u):
                dve.wait_ge(scored, u + 1)
                if u >= 2:
                    dve.wait_ge(exped, u - 1)
                nc.vector.tensor_reduce(nmax[:, u % 2], psS[:, u % 2, :, 0:KS], AXX, ALU.max,
                                        negate=True).then_inc(maxed, 1)

            def low_ctx(pair):
                h, half = divmod(pair, 2)
                dve.wait_ge(ctx_hi, pair + 1)
                o = ctxT[:, :, h % CTX, half * BANK:(half + 1) * BANK]
                nc.vector.scalar_tensor_tensor(out=o[:, 1], in0=psC[:, :], scalar=bias_v[:, h:h + 1],
                                               in1=o[:, 0].bitcast(F32), op0=ALU.add, op1=ALU.subtract
                                               ).then_inc(ctx_lo, 1)

            for m in range(4):
                low_qk(0, m)
                if m < 3:
                    take("v", 0, m)
            top(0)
            for u in range(NU + 6):
                h, b = divmod(u, 4)
                if u < NU:
                    dve.wait_ge(exped, u + 1)
                    if u >= 1:
                        dve.wait_ge(normed, u)
                    nc.vector.reciprocal(rec[:, u % 2], sums[:, u % 2]).then_inc(rec_ready, 1)
                    dve.wait_ge(rec_ready, u + 1)
                    for qt in range(2):
                        ins = nc.vector.tensor_scalar(Pr[:, u % 2, qt, 0:S], Pr[:, u % 2, qt, 0:S],
                                                      rec[:, u % 2, qt:qt + 1], None, ALU.mult)
                    ins.then_inc(normed, 1)
                if u - 1 in vo_at:
                    take(*vo_at[u - 1])
                if h + 1 < H:
                    low_qk(h + 1, b)
                if u + 1 < NU:
                    top(u + 1)
                if u < NU:
                    dve.wait_ge(pt_hi, u + 1)
                    nc.vector.tensor_tensor(PT[:, u % 2, 1].rearrange("p a s -> p (a s)"), psT[:, :],
                                            PT[:, u % 2, 0].rearrange("p a s -> p (a s)").bitcast(F32),
                                            ALU.subtract).then_inc(pt_lo, 1)
                if 2 <= u <= NU and u % 2 == 0:
                    low_ctx(u // 2 - 1)
            dve.wait_ge(vo_read, len(vo_jobs))
    k.pop()


def norm_rows(k, name, X, eps, gamma, beta, ident, full, parts):
    nc = k.nc
    k.push()
    stats = k.sb(f"{name}_stats", [P, NT, 6])
    mv = k.sb(f"{name}_mv", [P, NT, 2])
    ve = k.sb(f"{name}_ve", [P, NT])
    sd = k.sb(f"{name}_sd", [P, NT])
    rstd = k.sb(f"{name}_rstd", [P, NT])
    small = k.sem(f"{name}_small")
    var_ready = k.sem(f"{name}_var_ready")
    sd_ready = k.sem(f"{name}_sd_ready")
    table = k.sem(f"{name}_table")
    hi_ready = k.sem(f"{name}_hi_ready")
    with nc.Block() as block:
        @block.vector
        def _(dve):
            done = [0]

            def link(ins):
                done[0] += 1
                ins.then_inc(small, 1)
                dve.wait_ge(small, done[0])

            for t in range(NT):
                ins = nc.vector.bn_stats(stats[:, t, :], X[:, t, :])
            link(ins)
            for t in range(NT):
                ins = nc.vector.bn_aggr(mv[:, t, :], stats[:, t, :])
            link(ins)
            nc.vector.tensor_scalar(ve[:, :], mv[:, :, 1], eps, None, ALU.add).then_inc(var_ready, 1)
            dve.wait_ge(sd_ready, 1)
            link(nc.vector.reciprocal(rstd[:, :], sd[:, :]))
            for t in range(NT):
                ins = nc.vector.tensor_scalar(X[:, t, :], X[:, t, :], mv[:, t, 0:1], rstd[:, t:t + 1],
                                              ALU.subtract, ALU.mult)
            link(ins)
            link(nc.vector.tensor_tensor(X[:, :, :], X[:, :, :], gamma.unsqueeze(1).broadcast_to([P, NT, D]), ALU.mult))
            link(nc.vector.tensor_tensor(X[:, :, :], X[:, :, :], beta.unsqueeze(1).broadcast_to([P, NT, D]), ALU.add))

        @block.scalar
        def _(act):
            nc.scalar.activation(sd[:, 0:1], ident[:, 0:1], ACT.Sqrt).then_inc(table, 1)
            act.wait_ge(table, 1)
            act.wait_ge(var_ready, 1)
            nc.scalar.activation(sd[:, :], ve[:, :], ACT.Sqrt).then_inc(sd_ready, 1)
            for c in range(KC):
                nc.scalar.copy(parts[0][:, c, :], full[:, c, :]).then_inc(hi_ready, 1)

        @block.gpsimd
        def _(pool):
            for c in range(KC):
                pool.wait_ge(hi_ready, c + 1)
                nc.gpsimd.tensor_tensor(parts[1][:, c, :], full[:, c, :], parts[0][:, c, :].bitcast(F32),
                                        ALU.subtract)
    k.pop()


def single_head_attention(k, name, xT, cT, X, w, w_in, alpha, ident):
    nc = k.nc
    SCALE = D ** -0.5
    k.push()
    qT = k.sb(f"{name}_qT", [P, KC, TOK])
    kT = k.sb(f"{name}_kT", [P, KC, TOK])
    v = k.sb(f"{name}_v", [P, NT, D])
    k.push()
    ps = k.ps(f"{name}_ps", [P, 8, BANK])
    proj_done = k.sem(f"{name}_proj_done")
    by_act = k.sem(f"{name}_by_act")
    by_dve = k.sem(f"{name}_by_dve")
    NJ = 12
    with nc.Block() as block:
        @block.tensor
        def _(pe):
            pe.wait_ge(w_in, 16)
            for n in range(NJ):
                if n >= 8:
                    pe.wait_ge(by_dve if n % 2 else by_act, (n - 8) // 2 + 1)
                if n < 8:
                    a, oc, half = n // 4, n // 2 % 2, n % 2
                    for c in range(KC):
                        ins = nc.tensor.matmul(ps[:, n % 8, :], w[:, c, a, oc * P:(oc + 1) * P],
                                               (xT, cT)[a][:, c, half * BANK:(half + 1) * BANK],
                                               start=(c == 0), stop=(c == KC - 1))
                else:
                    for i in range(2):
                        t = 2 * (n - 8) + i
                        for c in range(KC):
                            ins = nc.tensor.matmul(ps[:, n % 8, i * D:(i + 1) * D], cT[:, c, t * P:(t + 1) * P],
                                                   w[:, c, 2, :], start=(c == 0), stop=(c == KC - 1))
                ins.then_inc(proj_done, 1)

        def target(n):
            if n < 8:
                a, oc, half = n // 4, n // 2 % 2, n % 2
                return (qT, kT)[a][:, oc, half * BANK:(half + 1) * BANK]
            return v[:, 2 * (n - 8):2 * (n - 8) + 2, :].rearrange("p t d -> p (t d)")

        @block.scalar
        def _(act):
            for n in range(0, NJ, 2):
                act.wait_ge(proj_done, n + 1)
                nc.scalar.activation(target(n), ps[:, n % 8, :], ACT.Copy, scale=SCALE if n < 4 else 1.0
                                     ).then_inc(by_act, 1)

        @block.vector
        def _(dve):
            for n in range(1, NJ, 2):
                dve.wait_ge(proj_done, n + 1)
                nc.vector.tensor_scalar(target(n), ps[:, n % 8, :], SCALE if n < 4 else 1.0, None, ALU.mult
                                        ).then_inc(by_dve, 1)
    k.pop()

    psS = k.ps(f"{name}_psS", [P, 4, BANK])
    psT = k.ps(f"{name}_psT", [P, 2, S])
    psX = k.ps(f"{name}_psX", [P, KC, S])
    psD = k.ps(f"{name}_psD", [P, 2, BANK])
    Pr = k.sb(f"{name}_Pr", [P, 2, S])
    PT = k.sb(f"{name}_PT", [P, 2, 2, S])
    cxT = k.sb(f"{name}_cxT", [P, KC, S])
    nmax = k.sb(f"{name}_nmax", [P, 4])
    sums = k.sb(f"{name}_sums", [P, 2])
    rec = k.sb(f"{name}_rec", [P, 2])
    scored = k.sem(f"{name}_scored")
    maxed = k.sem(f"{name}_maxed")
    exped = k.sem(f"{name}_exped")
    rec_ready = k.sem(f"{name}_rec_ready")
    normed = k.sem(f"{name}_normed")
    turned = k.sem(f"{name}_turned")
    pt_ready = k.sem(f"{name}_pt_ready")
    x_done = k.sem(f"{name}_x_done")
    cx_ready = k.sem(f"{name}_cx_ready")
    d_done = k.sem(f"{name}_d_done")
    added = k.sem(f"{name}_added")
    with nc.Block() as block:
        @block.tensor
        def _(pe):
            def score(n):
                if n >= 4:
                    pe.wait_ge(exped, n - 3)
                for c in range(KC):
                    ins = nc.tensor.matmul(psS[:, n % 4, 0:S], qT[:, c, n * P:(n + 1) * P],
                                           kT[:, c, (n // 2) * S:(n // 2 + 1) * S],
                                           start=(c == 0), stop=(c == KC - 1))
                ins.then_inc(scored, 1)

            def turn(n):
                pe.wait_ge(normed, n + 1)
                if n >= 1:
                    pe.wait_ge(pt_ready, n)
                qt = n % 2
                for st in range(2):
                    ins = nc.tensor.transpose(psT[:, st, qt * P:(qt + 1) * P], Pr[:, n % 2, st * P:(st + 1) * P],
                                              ident)
                ins.then_inc(turned, 1)

            def context(b):
                pe.wait_ge(pt_ready, 2 * b + 2)
                if b >= 1:
                    pe.wait_ge(cx_ready, b)
                for fc in range(KC):
                    for st in range(2):
                        ins = nc.tensor.matmul(psX[:, fc, :], v[:, 2 * b + st, fc * P:(fc + 1) * P],
                                               PT[:, b % 2, st, :], start=(st == 0), stop=(st == 1))
                ins.then_inc(x_done, 1)

            def output(b):
                pe.wait_ge(cx_ready, b + 1)
                for i in range(2):
                    t = 2 * b + i
                    if t >= 2:
                        pe.wait_ge(added, t - 1)
                    for c in range(KC):
                        ins = nc.tensor.matmul(psD[:, t % 2, 0:D], cxT[:, c, i * P:(i + 1) * P], w[:, c, 3, :],
                                               start=(c == 0), stop=(c == KC - 1))
                    ins.then_inc(d_done, 1)

            for n in range(3):
                score(n)
            for n in range(NT + 3):
                if n + 3 < NT:
                    score(n + 3)
                if n < NT:
                    turn(n)
                if 2 <= n <= NT and n % 2 == 0:
                    context(n // 2 - 1)
                if n >= 4 and n % 2 == 0:
                    output(n // 2 - 2)

        @block.scalar
        def _(act):
            for n in range(NT + 2):
                if n < NT:
                    act.wait_ge(maxed, n + 1)
                    if n >= 2:
                        act.wait_ge(turned, n - 1)
                    nc.scalar.activation(Pr[:, n % 2, :], psS[:, n % 4, 0:S], ACT.Exp, bias=nmax[:, n % 4:n % 4 + 1],
                                         accum_out=sums[:, n % 2:n % 2 + 1]).then_inc(exped, 1)
                if 1 <= n <= NT:
                    t = n - 1
                    qt, b = t % 2, t // 2
                    act.wait_ge(turned, t + 1)
                    if b >= 2 and qt == 0:
                        act.wait_ge(x_done, b - 1)
                    nc.scalar.copy(PT[:, b % 2, :, qt * P:(qt + 1) * P], psT[:, :, qt * P:(qt + 1) * P]
                                   ).then_inc(pt_ready, 1)
                if n >= 3 and n % 2 == 1:
                    b = (n - 3) // 2
                    act.wait_ge(x_done, b + 1)
                    if b >= 1:
                        act.wait_ge(d_done, 2 * b)
                    nc.scalar.copy(cxT[:, :, :], psX[:, :, :]).then_inc(cx_ready, 1)

        def add(dve, t):
            dve.wait_ge(d_done, t + 1)
            nc.vector.scalar_tensor_tensor(out=X[:, t, :], in0=psD[:, t % 2, 0:D], scalar=alpha, in1=X[:, t, :],
                                           op0=ALU.mult, op1=ALU.add).then_inc(added, 1)

        @block.vector
        def _(dve):
            def top(n):
                dve.wait_ge(scored, n + 1)
                if n >= 4:
                    dve.wait_ge(exped, n - 3)
                nc.vector.tensor_reduce(nmax[:, n % 4:n % 4 + 1], psS[:, n % 4, 0:S], AXX, ALU.max,
                                        negate=True).then_inc(maxed, 1)

            top(0)
            top(1)
            for n in range(NT + 4):
                if n + 2 < NT:
                    top(n + 2)
                if n < NT:
                    dve.wait_ge(exped, n + 1)
                    if n >= 1:
                        dve.wait_ge(normed, n)
                    nc.vector.reciprocal(rec[:, n % 2:n % 2 + 1], sums[:, n % 2:n % 2 + 1]).then_inc(rec_ready, 1)
                    dve.wait_ge(rec_ready, n + 1)
                    nc.vector.tensor_scalar(Pr[:, n % 2, :], Pr[:, n % 2, :], rec[:, n % 2:n % 2 + 1], None,
                                            ALU.mult).then_inc(normed, 1)
                if n >= 5 and n % 2 == 1:
                    add(dve, n - 5)
                    add(dve, n - 4)

    k.pop()


COLS = ["g_bq", "g_bk", "l_bq", "l_bk",
        "ln1_scale", "ln1_offset", "bq1", "bk1", "bias_k1", "bias_v1",
        "ln2_scale", "ln2_offset", "bq2", "bk2", "bias_k2", "bias_v2",
        "ln_mlp_scale", "ln_mlp_offset", "b_fc1", "alpha", "postnorm_w", "mlp_b1"]
ROWS = ["g_bv", "g_bo", "gamma", "beta", "bo1", "bo2", "b_fc2", "l_bv", "l_bo", "mlp_b2"]


def cross_attention_stack(nc, a, at_col, at_row, out):
    with ExitStack() as outer:
        k = Core(nc, outer)
        X = k.sb("X", [P, NT, D])
        cT = k.sb("cT", [P, KC, TOK])
        NCOL, NROW = a["cols"].shape[1], a["rows"].shape[1]
        cols = k.sb("cols", [P, NCOL])
        rows = k.sb("rows", [P, NROW])
        consts = k.sb("consts", [P, 3 * P])
        ident = consts[:, 0:P]
        expand_g = consts[0:16, P:2 * P]
        expand_l = consts[0:8, 2 * P:3 * P]

        def col(name, dt=None):
            o, w = at_col[name]
            return cols[:, o:o + w]

        def row(name):
            o, w = at_row[name]
            return rows[:, o:o + w]

        act_in = [k.sem(f"activations_in{i}") for i in range(2)]
        cols_in = k.sem("cols_in")
        vec_in = k.sem("vectors_in")
        x_in = k.sem("x_in")
        g_in = k.sem("g_weights_in")
        mask_in = [k.sem(f"mask_in{i}") for i in range(2)]
        prep = k.sem("vectors_prepared")

        k.push()
        xT = k.sb("xT", [P, KC, TOK])
        g_wo = k.sb("g_wo", [P, KC, D])
        k.push()
        g_w = k.sb("g_w", [P, KC, D + P + 64])
        mask = k.sb("mask", [P, 2, 2, S])

        def load_tokens(sp, i, part):
            for tile, dram in ((cT, a["cT"]), (xT, a["xT"])):
                sp.dma_start(tile[:, :, part], dram.rearrange("p (c t) -> p c t", c=KC)[:, :, part]
                             ).then_inc(act_in[i], 16)

        with nc.Block() as block:
            @block.sync
            def _(sp):
                sp.dma_start(g_w[:, :].rearrange("p c n -> p (c n)"), a["g_w"]).then_inc(g_in, 16)
                load_tokens(sp, 0, slice(0, S))

            @block.scalar
            def _(act):
                act.dma_start(cols[:, :], a["cols"]).then_inc(cols_in, 16)
                act.dma_start(consts[:, :], a["consts"]).then_inc(cols_in, 16)

            @block.vector
            def _(dve):
                dve.wait_ge(cols_in, 32)
                for name, scale in (("g_bq", 8 ** -0.5), ("bq1", 128 ** -0.5), ("bq2", 128 ** -0.5),
                                    ("l_bq", 1 / 16)):
                    ins = nc.vector.tensor_scalar(col(name), col(name), scale, None, ALU.mult)
                ins.then_inc(prep, 1)
                dve.wait_ge(prep, 1)

        def load_the_rest(sp):
            load_tokens(sp, 1, slice(S, TOK))
            sp.dma_start(rows[:, :], a["rows"].broadcast_to([P, NROW])).then_inc(vec_in, 16)
            sp.dma_start(g_wo[:, :].rearrange("p c n -> p (c n)"), a["g_wo"]).then_inc(x_in, 16)
            sp.dma_start(X[:, :], a["x"].rearrange("(n p) d -> p n d", p=P)).then_inc(x_in, 16)

        k.begin_stage()
        small_head_attention(
            k, "gqa", 4, xT, [cT], xT, g_w[:, :, 0:D], g_w[:, :, D:D + P], g_w[:, :, D + P:],
            col("g_bq"), col("g_bk"), row("g_bv"), 8 ** -0.5, lambda b, qt: mask[:, b % 2, qt, :],
            a["g_sel"], expand_g, ident, [(g_in, 16), (act_in[0], 32), (cols_in, 32)], [(act_in[1], 32)], (vec_in, 16),
            lambda n: n % 8 in (3, 6, 7), a["mask"], mask, mask_in, load_the_rest)
        k.end_stage()
        k.pop()
        out_projection(k, "gqa_out", [xT], KC, [g_wo], X, X, row("g_bo"), (x_in, 32))
        k.pop()
        k.push()
        c_parts = [k.sb(f"cT_{part}", [P, KC, TOK], F32R) for part in ("high", "low")]
        norm_rows(k, "gqa_norm", X, 1e-6, row("gamma"), row("beta"), ident, cT, c_parts)

        for i in (1, 2):
            k.push()
            h_parts = [k.sb(f"hT{i}_{part}", [P, KC, TOK], F32R) for part in ("high", "low")]
            vrow = k.sb(f"vrow{i}", [P, 16 * P])
            weights = HeadWeights(k, f"wide{i}", a[f"wqk{i}"], a[f"wv{i}"])
            k.push()
            hT = k.sb(f"hT{i}", [P, KC, TOK])
            xn = k.sb(f"ln{i}_xn", [P, NT, D])
            bvr = k.sb(f"bias_v_row{i}", [P, 16 * P])
            rows_in = k.sem(f"v_rows_in{i}")

            def load_first(sp):
                weights.load_qk(sp, 0)
                weights.load_v(sp, 0)
                sp.dma_start(vrow[:, :], a[f"bv{i}"].broadcast_to([P, 16 * P])).then_inc(rows_in, 16)
                sp.dma_start(bvr[:, :], a[f"bias_v{i}"].broadcast_to([P, 16 * P])).then_inc(rows_in, 16)
                weights.load_qk(sp, 1)

            def split_first(pool):
                weights.split_qk(pool, 0, 128 ** -0.5)
                weights.split_v(pool, 0)

            def value_row(dve):
                dve.wait_ge(rows_in, 32)
                nc.vector.tensor_tensor(vrow[:, :], vrow[:, :], bvr[:, :], ALU.subtract)

            norm_transpose(k, f"ln{i}", X, hT, xn, ident, 1e-5, col(f"ln{i}_scale"), col(f"ln{i}_offset"),
                           parts=h_parts, beside={"sp": load_first, "pool": split_first, "dve": value_row})
            k.pop()
            wide_head_attention(k, f"wide{i}", h_parts, c_parts, weights, a[f"wo{i}"],
                                X, ident, col(f"bq{i}"), col(f"bk{i}"), col(f"bias_k{i}"), col(f"bias_v{i}"), vrow,
                                row(f"bo{i}"))
            k.pop()
        k.pop()
        def mlp(name, w1_dram, w2_dram, b1, func, residual, b2, **norm):
            k.push()
            w1 = [k.sb(f"{name}_w1_{part}", [P, KC, 1024], F32R) for part in ("high", "low")]
            w2 = [k.sb(f"{name}_w2_{part}", [P, 8, D], F32R) for part in ("high", "low")]
            w2_full = k.sb(f"{name}_w2", [P, 8, D])
            h_parts = [k.sb(f"{name}_hT_{part}", [P, KC, TOK], F32R) for part in ("high", "low")]
            w1_in, w2_in = k.sem(f"{name}_w1_in"), k.sem(f"{name}_w2_in")
            w1_high = k.sem(f"{name}_w1_high")
            w2_high = k.sem(f"{name}_w2_high")
            k.push()
            w1_full = k.sb(f"{name}_w1", [P, KC, 1024])
            xn = k.sb(f"{name}_xn", [P, NT, D])
            hT = k.sb(f"{name}_hT", [P, KC, TOK])

            def load(sp):
                sp.dma_start(w1_full[:, :].rearrange("p c n -> p (c n)"), w1_dram).then_inc(w1_in, 16)
                sp.dma_start(w2_full[:, :].rearrange("p c n -> p (c n)"), w2_dram).then_inc(w2_in, 16)

            def high_w1(act):
                act.wait_ge(w1_in, 16)
                for c in range(KC):
                    nc.scalar.copy(w1[0][:, c, :], w1_full[:, c, :]).then_inc(w1_high, 1)

            def low_w1(engine, c):
                engine.wait_ge(w1_high, c + 1)
                engine.tensor_tensor(w1[1][:, c, :], w1_full[:, c, :], w1[0][:, c, :].bitcast(F32), ALU.subtract)

            norm_transpose(k, f"{name}_norm", X, hT, xn, ident, parts=h_parts,
                           beside={"sp": load, "act": high_w1, "pool": lambda pool: low_w1(pool, 0),
                                   "dve": lambda dve: low_w1(dve, 1)}, **norm)
            k.pop()
            gT = [k.sb(f"{name}_gT_{part}", [P, 8, TOK], F32R) for part in ("high", "low")]

            def split_w2(pool):
                pool.wait_ge(w2_in, 16)
                nc.gpsimd.tensor_copy(w2[0][:, :, :], w2_full[:, :, :]).then_inc(w2_high, 1)
                pool.wait_ge(w2_high, 1)
                nc.gpsimd.tensor_tensor(w2[1][:, :, :], w2_full[:, :, :], w2[0][:, :, :].bitcast(F32), ALU.subtract)

            hidden_layer(k, f"{name}_1", h_parts, w1, b1, gT, func, 8, split_w2)
            out_projection(k, f"{name}_2", gT, 8, w2, X, residual, b2)
            k.pop()

        mlp("mlp1", a["w_fc1"], a["w_fc2"], col("b_fc1"), ACT.Gelu, X, row("b_fc2"), eps=1e-5,
            scale=col("ln_mlp_scale"), offset=col("ln_mlp_offset"))

        xT = k.sb("xT_later", [P, KC, TOK])
        l_wo = k.sb("l_wo", [P, KC, D])
        k.push()
        l_w = k.sb("l_w", [P, KC, 3 * D])
        far = k.sb("far", [P, B, 2 * S], BF16)
        l_in = k.sem("l_weights_in")
        lm_in = k.sem("l_mask_in")
        k.push()
        mask_int = k.sb("mask_int", [P, B * S], I32)
        s_w = k.sb("s_w", [P, KC, 4, D])
        s_in = k.sem("s_weights_in")
        with nc.Block() as block:
            @block.sync
            def _(sp):
                sp.dma_start(s_w[:, :].rearrange("p c a n -> p (c a n)"), a["s_w"]).then_inc(s_in, 16)
                sp.dma_start(mask_int[:, :], a["key_mask"].broadcast_to([P, B * S])).then_inc(lm_in, 16)
                sp.dma_start(l_w[:, :].rearrange("p c n -> p (c n)"), a["l_w"]).then_inc(l_in, 16)
                sp.dma_start(l_wo[:, :].rearrange("p c n -> p (c n)"), a["l_wo"]).then_inc(l_in, 16)
        transpose_tokens(k, "x2", X, xT, ident)
        single_head_attention(k, "one", xT, cT, X, s_w, s_in, col("alpha"), ident)

        transpose_tokens(k, "x3", X, xT, ident)
        with nc.Block() as block:
            @block.vector
            def _(dve):
                nc.vector.memset(far[:, :, S:2 * S], 0.0)
                dve.wait_ge(lm_in, 16)
                nc.vector.tensor_scalar(far[:, :, 0:S], mask_int[:, :].rearrange("p (b s) -> p b s", b=B), 0.0, FAR,
                                        ALU.is_equal, ALU.mult)
        k.pop()
        small_head_attention(
            k, "latent", 2, xT, [cT, xT], xT, l_w[:, :, 0:D], l_w[:, :, D:2 * D], l_w[:, :, 2 * D:],
            col("l_bq"), col("l_bk"), row("l_bv"), 1 / 16, lambda b, qt: far[:, b, :],
            a["l_sel"], expand_l, ident, [(l_in, 32)], [], None, lambda n: n % 8 != 0)
        k.pop()
        LX = k.sb("LX", [P, NT, D])
        out_projection(k, "latent_out", [xT], KC, [l_wo], LX, X, row("l_bo"))
        saved = X
        X = LX
        mlp("mlp3", a["mlp_w1"], a["mlp_w2"], col("mlp_b1"), ACT.Gelu_apprx_tanh, saved, row("mlp_b2"), eps=1e-6,
            scale=col("postnorm_w"), rms=True)
        stored = k.sem("stored")
        with nc.Block() as block:
            @block.sync
            def _(sp):
                sp.dma_start(out.rearrange("(n p) d -> p n d", p=P), X[:, :]).then_inc(stored, 16)
                sp.wait_ge(stored, 16)


def kernel(**inputs):
    import numpy as np
    import concourse.bacc as bacc
    from concourse.bass_utils import run_bass_kernel_spmd

    v = {n: np.asarray(x) for n, x in inputs.items()}

    def w(m):
        m = np.asarray(m)
        return np.ascontiguousarray(m.reshape(-1, 128, m.shape[1]).transpose(1, 0, 2).reshape(128, -1))

    def by_feature(vec):
        return np.asarray(vec).reshape(-1, 128).T

    L0, L1, L2, L3 = "L0_xattn_", "L1_xattn_", "L2_xattn_", "L3_xattn_"
    p = np.arange(128)
    kv_b = v[L3 + "kv_b"].reshape(256, 2)
    kv_w = v[L3 + "kv_w"].reshape(256, 256, 2)
    col = {
        "g_bq": by_feature(v[L0 + "bq"]), "g_bk": by_feature(np.tile(v[L0 + "bk"], 2)),
        "l_bq": by_feature(v[L3 + "q_b"]), "l_bk": by_feature(kv_b[:, 0]),
        "alpha": np.broadcast_to(v[L2 + "alpha"].reshape(1, 1), (128, 1)),
        "postnorm_w": by_feature(v[L3 + "postnorm_w"]), "mlp_b1": by_feature(v[L3 + "mlp_b1"]),
    }
    for n in COLS:
        if n not in col:
            col[n] = by_feature(v[L1 + n])
    row = {"g_bv": v[L0 + "bv"], "g_bo": v[L0 + "bo"], "gamma": v[L0 + "gamma"], "beta": v[L0 + "beta"],
           "bo1": v[L1 + "bo1"], "bo2": v[L1 + "bo2"], "b_fc2": v[L1 + "b_fc2"],
           "l_bv": kv_b[:, 1], "l_bo": v[L3 + "out_b"], "mlp_b2": v[L3 + "mlp_b2"]}

    def offsets(names, widths):
        at, o = {}, 0
        for n in names:
            at[n] = (o, widths[n])
            o += widths[n]
        return at

    at_col = offsets(COLS, {n: col[n].shape[1] for n in COLS})
    at_row = offsets(ROWS, {n: row[n].size for n in ROWS})
    consts = np.zeros((128, 384), np.float32)
    consts[:, 0:128] = np.eye(128)
    consts[p // 8, 128 + p] = 1.0
    consts[p // 16, 256 + p] = 1.0

    sels = {}
    for name, fd in (("g_sel", 8), ("l_sel", 16)):
        head, copy, feature = p // (4 * fd), p // fd % 4, p % fd
        m = np.zeros((128, 16, 128), np.float32)
        for quarter in range(4):
            source = 32 * quarter + head * fd + feature
            m[source, quarter, p] = copy < 2
            m[source, 4 + quarter, p] = copy >= 2
            if fd == 16:
                m[source, 8 + quarter, p] = copy % 2 == 0
                m[source, 12 + quarter, p] = copy % 2 == 1
        if fd == 8:
            for chunk in range(8):
                m[64 * (copy % 2) + 8 * chunk + feature, 8 + chunk, p] = 1.0
        sels[name] = m.reshape(128, 2048)

    arrays = {
        **sels,
        "x": v["x"].reshape(1024, 256), "xT": w(v["x"].reshape(1024, 256).T), "cT": w(v["ctx_2048"].reshape(1024, 256).T),
        "mask": v["mask_Bx1xSxS2_ff0"].reshape(1024, 256), "key_mask": v["mask_BxS2_ik0"].reshape(1, 1024),
        "cols": np.concatenate([col[n] for n in COLS], axis=1),
        "rows": np.concatenate([row[n].reshape(1, -1) for n in ROWS], axis=1),
        "consts": consts,
        "g_w": w(np.concatenate([v[L0 + "Wq"], v[L0 + "Wk"], v[L0 + "Wk"], v[L0 + "Wv"]], axis=1)),
        "g_wo": w(v[L0 + "Wo"]), "l_wo": w(v[L3 + "out_w"]),
        "s_w": w(np.concatenate([v[L2 + n].T for n in ("w_q", "w_k", "w_v", "w_o")], axis=1)),
        "l_w": w(np.concatenate([v[L3 + "q_w"], kv_w[:, :, 0], kv_w[:, :, 1]], axis=1)),
        "w_fc1": w(v[L1 + "w_fc1"]), "w_fc2": w(v[L1 + "w_fc2"]),
        "mlp_w1": w(v[L3 + "mlp_w1"]), "mlp_w2": w(v[L3 + "mlp_w2"]),
    }
    for i in ("1", "2"):
        qk = np.stack([v[L1 + n + i].reshape(2, 128, 16, 128) for n in ("wq", "wk")])
        arrays["wqk" + i] = qk.transpose(3, 2, 1, 0, 4).reshape(16, 128, 512)
        arrays["wv" + i] = v[L1 + "wv" + i].reshape(2, 128, 8, 256).transpose(2, 1, 0, 3).reshape(8, 128, 512)
        arrays["wo" + i] = v[L1 + "wo" + i].reshape(8, 2, 128, 256).transpose(0, 2, 1, 3).reshape(8, 128, 512)
        arrays["bv" + i] = v[L1 + "bv" + i].reshape(1, 2048)
        arrays["bias_v" + i] = v[L1 + "bias_v" + i].reshape(1, 2048)

    nc = bacc.Bacc("TRN2", target_bir_lowering=False, num_devices=1)
    feed, aps = {}, {}
    for n, x in arrays.items():
        x = np.ascontiguousarray(x)
        feed[f"in_{n}"] = x
        aps[n] = nc.dram_tensor(f"in_{n}", x.shape, mybir.dt.from_np(x.dtype), kind="ExternalInput").ap()
    out = nc.dram_tensor("out", (1024, 256), F32, kind="ExternalOutput").ap()
    cross_attention_stack(nc, aps, at_col, at_row, out)
    r = run_bass_kernel_spmd(nc, [feed], core_ids=[0])
    return r.results[0]["out"].reshape(4, 256, 256)
```
